# Optimizing a Trainium2 kernel written in Bass

```python
import numpy as np
import jax
import jax.numpy as jnp

def _softmax(x, axis=-1):
    return jax.nn.softmax(x, axis=axis)

def _gelu(x):
    return jax.nn.gelu(x, approximate=True)

def _silu(x):
    return jax.nn.silu(x)

def _sigmoid(x):
    return jax.nn.sigmoid(x)

def _layernorm(x, axis=-1, eps=1e-05):
    m = jnp.mean(x, axis=axis, keepdims=True)
    v = jnp.var(x, axis=axis, keepdims=True)
    return (x - m) / jnp.sqrt(v + eps)

def _scatter_add(tgt, idx, src, axis=0):
    return tgt.at[idx].add(src)

def _segment_sum(src, seg, n):
    return jax.ops.segment_sum(src, seg, n)
kernel_name = 'mk_vit_tower_cls_d2_tok_img768_r4_31c7b2'

def setup_inputs(seed: int=0):
    np.random.seed(seed)
    _w = jnp.asarray

    def _rec_inputs():
        import jax
        import jax.numpy as jnp
        _rk = jax.random.key(seed)
        x = 7.57192e-06 + 1.00007 * jax.random.normal(jax.random.fold_in(_rk, 1), (32, 3, 128, 128), jnp.float32)
        cls_tok = 0.02 * jax.random.normal(jax.random.fold_in(_rk, 5), (1, 1, 192), jnp.float32)
        return (x, cls_tok)
    x, cls_tok = _rec_inputs()

    def _L0_tok_setup():
        import jax, jax.numpy as jnp
        import numpy as np
        import math
        EMB = 64
        M = 32

        def _unfold(x, k, s, p):
            patches = jax.lax.conv_general_dilated_patches(x, filter_shape=(k, k), window_strides=(s, s), padding=((p, p), (p, p)), dimension_numbers=('NCHW', 'OIHW', 'NCHW'))
            B, D, Ho, Wo = patches.shape
            return patches.reshape(B, D, Ho * Wo).transpose(0, 2, 1)

        def _ln(x, g, b):
            mu = jnp.mean(x, -1, keepdims=True)
            var = jnp.var(x, -1, keepdims=True)
            return (x - mu) * jax.lax.rsqrt(var + 1e-05) * g + b

        def _prm_exp(x, w):
            xd = jnp.sum(x * x, -1, keepdims=True) * 0.5
            wtx = jnp.einsum('btd,md->btm', x, w)
            return jnp.exp(wtx - xd) / jnp.sqrt(jnp.float32(w.shape[0]))

        def _performer(x, n1g, n1b, kqvw, kqvb, projw, projb, n2g, n2b, w1, b1, w2, b2, wrand):
            h = _ln(x, n1g, n1b)
            kqv = h @ kqvw + kqvb
            k, q, v = (kqv[..., :EMB], kqv[..., EMB:2 * EMB], kqv[..., 2 * EMB:])
            kp, qp = (_prm_exp(k, wrand), _prm_exp(q, wrand))
            D = jnp.einsum('btm,bm->bt', qp, jnp.sum(kp, 1))[..., None]
            kptv = jnp.einsum('btd,btm->bdm', v, kp)
            y = jnp.einsum('btm,bdm->btd', qp, kptv) / (D + 1e-08)
            y = v + (y @ projw + projb)
            h2 = _ln(y, n2g, n2b)
            return y + (jax.nn.gelu(h2 @ w1 + b1, approximate=False) @ w2 + b2)

        def _forward(x, a1, a2, proj_w, proj_b):
            t = _unfold(x, 7, 4, 2)
            t = _performer(t, *a1)
            B, L, C = t.shape
            s = round(math.sqrt(L))
            t = t.transpose(0, 2, 1).reshape(B, C, s, s)
            t = _unfold(t, 3, 2, 1)
            t = _performer(t, *a2)
            B, L, C = t.shape
            s = round(math.sqrt(L))
            t = t.transpose(0, 2, 1).reshape(B, C, s, s)
            t = _unfold(t, 3, 2, 1)
            return t @ proj_w + proj_b
        key = jax.random.key(seed)
        ks = iter(jax.random.split(key, 40))

        def nrm(shape, s=0.02):
            return jax.random.normal(next(ks), shape, jnp.float32) * s

        def ortho():
            a = jax.random.normal(next(ks), (EMB, M), jnp.float32)
            q, _ = jnp.linalg.qr(a)
            return q.T * jnp.sqrt(jnp.float32(M))

        def attn_params(dim):
            return dict(n1g=jnp.ones((dim,), jnp.float32), n1b=jnp.zeros((dim,), jnp.float32), kqvw=nrm((dim, 3 * EMB)), kqvb=jnp.zeros((3 * EMB,), jnp.float32), projw=nrm((EMB, EMB)), projb=jnp.zeros((EMB,), jnp.float32), n2g=jnp.ones((EMB,), jnp.float32), n2b=jnp.zeros((EMB,), jnp.float32), w1=nrm((EMB, EMB)), b1=jnp.zeros((EMB,), jnp.float32), w2=nrm((EMB, EMB)), b2=jnp.zeros((EMB,), jnp.float32), w=ortho())
        inp = {'x': jax.random.normal(next(ks), (64, 3, 224, 224), jnp.float32)}
        for pre, dim in (('a1_', 3 * 7 * 7), ('a2_', EMB * 3 * 3)):
            for k2, v in attn_params(dim).items():
                inp[pre + k2] = v
        inp['proj_w'] = nrm((EMB * 9, 192))
        inp['proj_b'] = jnp.zeros((192,), jnp.float32)
        return inp
    _L0_tok_all = _L0_tok_setup()
    _L0_tok_in = {k: v for k, v in _L0_tok_all.items() if k in ('a1_n1g', 'a1_n1b', 'a1_kqvw', 'a1_kqvb', 'a1_projw', 'a1_projb', 'a1_n2g', 'a1_n2b', 'a1_w1', 'a1_b1', 'a1_w2', 'a1_b2', 'a1_w', 'a2_n1g', 'a2_n1b', 'a2_kqvw', 'a2_kqvb', 'a2_projw', 'a2_projb', 'a2_n2g', 'a2_n2b', 'a2_w1', 'a2_b1', 'a2_w2', 'a2_b2', 'a2_w', 'proj_w', 'proj_b')}
    del _L0_tok_all

    def _L0_attn_setup():
        import jax, jax.numpy as jnp
        import numpy as np
        NUM_HEADS = 12
        D = 192
        HD = D // NUM_HEADS
        key = jax.random.key(seed)
        ks = jax.random.split(key, 9)
        s = 0.02
        return {'x': jax.random.normal(ks[0], (4, 512, D), dtype=jnp.float32), 'QW_w': jax.random.normal(ks[1], (D, D), dtype=jnp.float32) * s, 'QW_b': jax.random.normal(ks[2], (D,), dtype=jnp.float32) * s, 'KW_w': jax.random.normal(ks[3], (D, D), dtype=jnp.float32) * s, 'KW_b': jax.random.normal(ks[4], (D,), dtype=jnp.float32) * s, 'VW_w': jax.random.normal(ks[5], (D, D), dtype=jnp.float32) * s, 'VW_b': jax.random.normal(ks[6], (D,), dtype=jnp.float32) * s, 'OW_w': jax.random.normal(ks[7], (D, D), dtype=jnp.float32) * s, 'OW_b': jax.random.normal(ks[8], (D,), dtype=jnp.float32) * s}
    _L0_attn_all = _L0_attn_setup()
    _L0_attn_in = {k: v for k, v in _L0_attn_all.items() if k in ('QW_w', 'QW_b', 'KW_w', 'KW_b', 'VW_w', 'VW_b', 'OW_w', 'OW_b')}
    del _L0_attn_all

    def _L0_ffn_setup():
        import jax, jax.numpy as jnp
        import numpy as np
        B, N, DIM, HEADS = (4, 256, 192, 12)
        HIDDEN, E, TOPK = (768, 8, 2)
        EPS = 1e-05

        def _layernorm(x, g, b):
            mu = jnp.mean(x, axis=-1, keepdims=True)
            var = jnp.var(x, axis=-1, keepdims=True)
            return (x - mu) * jax.lax.rsqrt(var + EPS) * g + b
        key = jax.random.key(seed)
        ks = jax.random.split(key, 10)
        s = 0.02
        return {'x': jax.random.normal(ks[0], (B, N, DIM), dtype=jnp.float32), 'ln1_g': jnp.ones((DIM,), jnp.float32), 'ln1_b': jnp.zeros((DIM,), jnp.float32), 'qkv_w': jax.random.normal(ks[1], (3 * DIM, DIM), jnp.float32) * s, 'proj_w': jax.random.normal(ks[2], (DIM, DIM), jnp.float32) * s, 'proj_b': jnp.zeros((DIM,), jnp.float32), 'ln2_g': jnp.ones((DIM,), jnp.float32), 'ln2_b': jnp.zeros((DIM,), jnp.float32), 'gate_w': jax.random.normal(ks[3], (E, DIM), jnp.float32) * s, 'gate_b': jnp.zeros((E,), jnp.float32), 'w1': jax.random.normal(ks[4], (E, HIDDEN, DIM), jnp.float32) * s, 'b1': jnp.zeros((E, HIDDEN), jnp.float32), 'w2': jax.random.normal(ks[5], (E, DIM, HIDDEN), jnp.float32) * s, 'b2': jnp.zeros((E, DIM), jnp.float32)}
    _L0_ffn_all = _L0_ffn_setup()
    _L0_ffn_in = {k: v for k, v in _L0_ffn_all.items() if k in ('ln1_g', 'ln1_b', 'qkv_w', 'proj_w', 'proj_b', 'ln2_g', 'ln2_b', 'gate_w', 'gate_b', 'w1', 'b1', 'w2', 'b2')}
    del _L0_ffn_all

    def _L1_attn_setup():
        import jax, jax.numpy as jnp
        import numpy as np
        D_MODEL = 192
        D_STATE = 16
        DT_MIN, DT_MAX = (0.001, 0.1)

        def _mlp(x, w1, b1, w2, b2):
            return jax.nn.silu(x @ w1 + b1) @ w2 + b2

        def _ssm_forward(x, A_w1, A_b1, A_w2, A_b2, B_w1, B_b1, B_w2, B_b2, C_w1, C_b1, C_w2, C_b2, d_w1, d_b1, d_w2, d_b2, D_param, log_dt):
            Bsz, L, Dm = x.shape
            N = A_w2.shape[1]
            A_log = -jnp.abs(_mlp(x, A_w1, A_b1, A_w2, A_b2))
            Bv = _mlp(x, B_w1, B_b1, B_w2, B_b2)
            Cv = _mlp(x, C_w1, C_b1, C_w2, C_b2)
            delta = jax.nn.sigmoid(_mlp(x, d_w1, d_b1, d_w2, d_b2))
            dt = jnp.exp(log_dt)

            def step(state, inp):
                a, b, c, dlt, u_t = inp
                dA = jnp.exp(a[:, None, :] * dt[None, :, None])
                dB = b[:, None, :] * dt[None, :, None]
                cur = u_t[:, :, None] * dB
                state = (dlt[:, :, None] * state + (1.0 - dlt[:, :, None]) * cur) * dA
                y = jnp.sum(state * c[:, None, :], axis=2) + u_t * D_param
                return (state, y)
            init = jnp.zeros((Bsz, Dm, N), x.dtype)
            xs = (jnp.swapaxes(A_log, 0, 1), jnp.swapaxes(Bv, 0, 1), jnp.swapaxes(Cv, 0, 1), jnp.swapaxes(delta, 0, 1), jnp.swapaxes(x, 0, 1))
            _, ys = jax.lax.scan(step, init, xs)
            return jnp.swapaxes(ys, 0, 1)
        key = jax.random.key(seed)
        ks = jax.random.split(key, 16)
        d, n = (D_MODEL, D_STATE)

        def lin(k, fan_in, fan_out):
            kw, kb = jax.random.split(k)
            s = 1.0 / np.sqrt(fan_in)
            return (jax.random.uniform(kw, (fan_in, fan_out), jnp.float32, -s, s), jax.random.uniform(kb, (fan_out,), jnp.float32, -s, s))
        A_w1, A_b1 = lin(ks[0], d, 2 * d)
        A_w2, A_b2 = lin(ks[1], 2 * d, n)
        B_w1, B_b1 = lin(ks[2], d, 2 * d)
        B_w2, B_b2 = lin(ks[3], 2 * d, n)
        C_w1, C_b1 = lin(ks[4], d, 2 * d)
        C_w2, C_b2 = lin(ks[5], 2 * d, n)
        d_w1, d_b1 = lin(ks[6], d, d)
        d_w2, d_b2 = lin(ks[7], d, d)
        D_param = jax.random.normal(ks[8], (d,), jnp.float32)
        log_dt = jnp.linspace(np.log(DT_MIN), np.log(DT_MAX), d).astype(jnp.float32)
        x = jax.random.normal(ks[9], (4, 512, d), jnp.float32)
        return {'x': x, 'A_w1': A_w1, 'A_b1': A_b1, 'A_w2': A_w2, 'A_b2': A_b2, 'B_w1': B_w1, 'B_b1': B_b1, 'B_w2': B_w2, 'B_b2': B_b2, 'C_w1': C_w1, 'C_b1': C_b1, 'C_w2': C_w2, 'C_b2': C_b2, 'd_w1': d_w1, 'd_b1': d_b1, 'd_w2': d_w2, 'd_b2': d_b2, 'D_param': D_param, 'log_dt': log_dt}
    _L1_attn_all = _L1_attn_setup()
    _L1_attn_in = {k: v for k, v in _L1_attn_all.items() if k in ('A_w1', 'A_b1', 'A_w2', 'A_b2', 'B_w1', 'B_b1', 'B_w2', 'B_b2', 'C_w1', 'C_b1', 'C_w2', 'C_b2', 'd_w1', 'd_b1', 'd_w2', 'd_b2', 'D_param', 'log_dt')}
    del _L1_attn_all

    def _L1_ffn_setup():
        import jax, jax.numpy as jnp
        import numpy as np
        NUM_EXPERT = 8
        TOP_K = 1
        key = jax.random.key(seed)
        ks = jax.random.split(key, 6)
        B, S, D, E, F = (8, 512, 192, 8, 469)
        scale = 0.02
        return {'x': jax.random.normal(ks[0], (B, S, D), dtype=jnp.float32), 'Wg': jax.random.normal(ks[1], (E, D), dtype=jnp.float32) * scale, 'bg': jnp.zeros((E,), dtype=jnp.float32), 'W1': jax.random.normal(ks[2], (E, F, D), dtype=jnp.float32) * scale, 'W2': jax.random.normal(ks[3], (E, F, D), dtype=jnp.float32) * scale, 'W3': jax.random.normal(ks[4], (E, D, F), dtype=jnp.float32) * scale}
    _L1_ffn_all = _L1_ffn_setup()
    _L1_ffn_in = {k: v for k, v in _L1_ffn_all.items() if k in ('Wg', 'bg', 'W1', 'W2', 'W3')}
    del _L1_ffn_all
    return {'x': x, 'cls_tok': cls_tok, 'L0_tok_a1_n1g': _L0_tok_in['a1_n1g'], 'L0_tok_a1_n1b': _L0_tok_in['a1_n1b'], 'L0_tok_a1_kqvw': _L0_tok_in['a1_kqvw'], 'L0_tok_a1_kqvb': _L0_tok_in['a1_kqvb'], 'L0_tok_a1_projw': _L0_tok_in['a1_projw'], 'L0_tok_a1_projb': _L0_tok_in['a1_projb'], 'L0_tok_a1_n2g': _L0_tok_in['a1_n2g'], 'L0_tok_a1_n2b': _L0_tok_in['a1_n2b'], 'L0_tok_a1_w1': _L0_tok_in['a1_w1'], 'L0_tok_a1_b1': _L0_tok_in['a1_b1'], 'L0_tok_a1_w2': _L0_tok_in['a1_w2'], 'L0_tok_a1_b2': _L0_tok_in['a1_b2'], 'L0_tok_a1_w': _L0_tok_in['a1_w'], 'L0_tok_a2_n1g': _L0_tok_in['a2_n1g'], 'L0_tok_a2_n1b': _L0_tok_in['a2_n1b'], 'L0_tok_a2_kqvw': _L0_tok_in['a2_kqvw'], 'L0_tok_a2_kqvb': _L0_tok_in['a2_kqvb'], 'L0_tok_a2_projw': _L0_tok_in['a2_projw'], 'L0_tok_a2_projb': _L0_tok_in['a2_projb'], 'L0_tok_a2_n2g': _L0_tok_in['a2_n2g'], 'L0_tok_a2_n2b': _L0_tok_in['a2_n2b'], 'L0_tok_a2_w1': _L0_tok_in['a2_w1'], 'L0_tok_a2_b1': _L0_tok_in['a2_b1'], 'L0_tok_a2_w2': _L0_tok_in['a2_w2'], 'L0_tok_a2_b2': _L0_tok_in['a2_b2'], 'L0_tok_a2_w': _L0_tok_in['a2_w'], 'L0_tok_proj_w': _L0_tok_in['proj_w'], 'L0_tok_proj_b': _L0_tok_in['proj_b'], 'L0_attn_QW_w': _L0_attn_in['QW_w'], 'L0_attn_QW_b': _L0_attn_in['QW_b'], 'L0_attn_KW_w': _L0_attn_in['KW_w'], 'L0_attn_KW_b': _L0_attn_in['KW_b'], 'L0_attn_VW_w': _L0_attn_in['VW_w'], 'L0_attn_VW_b': _L0_attn_in['VW_b'], 'L0_attn_OW_w': _L0_attn_in['OW_w'], 'L0_attn_OW_b': _L0_attn_in['OW_b'], 'L0_ffn_ln1_g': _L0_ffn_in['ln1_g'], 'L0_ffn_ln1_b': _L0_ffn_in['ln1_b'], 'L0_ffn_qkv_w': _L0_ffn_in['qkv_w'], 'L0_ffn_proj_w': _L0_ffn_in['proj_w'], 'L0_ffn_proj_b': _L0_ffn_in['proj_b'], 'L0_ffn_ln2_g': _L0_ffn_in['ln2_g'], 'L0_ffn_ln2_b': _L0_ffn_in['ln2_b'], 'L0_ffn_gate_w': _L0_ffn_in['gate_w'], 'L0_ffn_gate_b': _L0_ffn_in['gate_b'], 'L0_ffn_w1': _L0_ffn_in['w1'], 'L0_ffn_b1': _L0_ffn_in['b1'], 'L0_ffn_w2': _L0_ffn_in['w2'], 'L0_ffn_b2': _L0_ffn_in['b2'], 'L1_attn_A_w1': _L1_attn_in['A_w1'], 'L1_attn_A_b1': _L1_attn_in['A_b1'], 'L1_attn_A_w2': _L1_attn_in['A_w2'], 'L1_attn_A_b2': _L1_attn_in['A_b2'], 'L1_attn_B_w1': _L1_attn_in['B_w1'], 'L1_attn_B_b1': _L1_attn_in['B_b1'], 'L1_attn_B_w2': _L1_attn_in['B_w2'], 'L1_attn_B_b2': _L1_attn_in['B_b2'], 'L1_attn_C_w1': _L1_attn_in['C_w1'], 'L1_attn_C_b1': _L1_attn_in['C_b1'], 'L1_attn_C_w2': _L1_attn_in['C_w2'], 'L1_attn_C_b2': _L1_attn_in['C_b2'], 'L1_attn_d_w1': _L1_attn_in['d_w1'], 'L1_attn_d_b1': _L1_attn_in['d_b1'], 'L1_attn_d_w2': _L1_attn_in['d_w2'], 'L1_attn_d_b2': _L1_attn_in['d_b2'], 'L1_attn_D_param': _L1_attn_in['D_param'], 'L1_attn_log_dt': _L1_attn_in['log_dt'], 'L1_ffn_Wg': _L1_ffn_in['Wg'], 'L1_ffn_bg': _L1_ffn_in['bg'], 'L1_ffn_W1': _L1_ffn_in['W1'], 'L1_ffn_W2': _L1_ffn_in['W2'], 'L1_ffn_W3': _L1_ffn_in['W3']}

def reference(x, cls_tok, L0_tok_a1_n1g, L0_tok_a1_n1b, L0_tok_a1_kqvw, L0_tok_a1_kqvb, L0_tok_a1_projw, L0_tok_a1_projb, L0_tok_a1_n2g, L0_tok_a1_n2b, L0_tok_a1_w1, L0_tok_a1_b1, L0_tok_a1_w2, L0_tok_a1_b2, L0_tok_a1_w, L0_tok_a2_n1g, L0_tok_a2_n1b, L0_tok_a2_kqvw, L0_tok_a2_kqvb, L0_tok_a2_projw, L0_tok_a2_projb, L0_tok_a2_n2g, L0_tok_a2_n2b, L0_tok_a2_w1, L0_tok_a2_b1, L0_tok_a2_w2, L0_tok_a2_b2, L0_tok_a2_w, L0_tok_proj_w, L0_tok_proj_b, L0_attn_QW_w, L0_attn_QW_b, L0_attn_KW_w, L0_attn_KW_b, L0_attn_VW_w, L0_attn_VW_b, L0_attn_OW_w, L0_attn_OW_b, L0_ffn_ln1_g, L0_ffn_ln1_b, L0_ffn_qkv_w, L0_ffn_proj_w, L0_ffn_proj_b, L0_ffn_ln2_g, L0_ffn_ln2_b, L0_ffn_gate_w, L0_ffn_gate_b, L0_ffn_w1, L0_ffn_b1, L0_ffn_w2, L0_ffn_b2, L1_attn_A_w1, L1_attn_A_b1, L1_attn_A_w2, L1_attn_A_b2, L1_attn_B_w1, L1_attn_B_b1, L1_attn_B_w2, L1_attn_B_b2, L1_attn_C_w1, L1_attn_C_b1, L1_attn_C_w2, L1_attn_C_b2, L1_attn_d_w1, L1_attn_d_b1, L1_attn_d_w2, L1_attn_d_b2, L1_attn_D_param, L1_attn_log_dt, L1_ffn_Wg, L1_ffn_bg, L1_ffn_W1, L1_ffn_W2, L1_ffn_W3):
    import jax
    import jax.numpy as jnp

    def _L0_tok_ref(x, a1_n1g, a1_n1b, a1_kqvw, a1_kqvb, a1_projw, a1_projb, a1_n2g, a1_n2b, a1_w1, a1_b1, a1_w2, a1_b2, a1_w, a2_n1g, a2_n1b, a2_kqvw, a2_kqvb, a2_projw, a2_projb, a2_n2g, a2_n2b, a2_w1, a2_b1, a2_w2, a2_b2, a2_w, proj_w, proj_b):
        import jax, jax.numpy as jnp
        import numpy as np
        import math
        EMB = 64
        M = 32

        def _unfold(x, k, s, p):
            patches = jax.lax.conv_general_dilated_patches(x, filter_shape=(k, k), window_strides=(s, s), padding=((p, p), (p, p)), dimension_numbers=('NCHW', 'OIHW', 'NCHW'))
            B, D, Ho, Wo = patches.shape
            return patches.reshape(B, D, Ho * Wo).transpose(0, 2, 1)

        def _ln(x, g, b):
            mu = jnp.mean(x, -1, keepdims=True)
            var = jnp.var(x, -1, keepdims=True)
            return (x - mu) * jax.lax.rsqrt(var + 1e-05) * g + b

        def _prm_exp(x, w):
            xd = jnp.sum(x * x, -1, keepdims=True) * 0.5
            wtx = jnp.einsum('btd,md->btm', x, w)
            return jnp.exp(wtx - xd) / jnp.sqrt(jnp.float32(w.shape[0]))

        def _performer(x, n1g, n1b, kqvw, kqvb, projw, projb, n2g, n2b, w1, b1, w2, b2, wrand):
            h = _ln(x, n1g, n1b)
            kqv = h @ kqvw + kqvb
            k, q, v = (kqv[..., :EMB], kqv[..., EMB:2 * EMB], kqv[..., 2 * EMB:])
            kp, qp = (_prm_exp(k, wrand), _prm_exp(q, wrand))
            D = jnp.einsum('btm,bm->bt', qp, jnp.sum(kp, 1))[..., None]
            kptv = jnp.einsum('btd,btm->bdm', v, kp)
            y = jnp.einsum('btm,bdm->btd', qp, kptv) / (D + 1e-08)
            y = v + (y @ projw + projb)
            h2 = _ln(y, n2g, n2b)
            return y + (jax.nn.gelu(h2 @ w1 + b1, approximate=False) @ w2 + b2)

        def _forward(x, a1, a2, proj_w, proj_b):
            t = _unfold(x, 7, 4, 2)
            t = _performer(t, *a1)
            B, L, C = t.shape
            s = round(math.sqrt(L))
            t = t.transpose(0, 2, 1).reshape(B, C, s, s)
            t = _unfold(t, 3, 2, 1)
            t = _performer(t, *a2)
            B, L, C = t.shape
            s = round(math.sqrt(L))
            t = t.transpose(0, 2, 1).reshape(B, C, s, s)
            t = _unfold(t, 3, 2, 1)
            return t @ proj_w + proj_b
        a1 = (a1_n1g, a1_n1b, a1_kqvw, a1_kqvb, a1_projw, a1_projb, a1_n2g, a1_n2b, a1_w1, a1_b1, a1_w2, a1_b2, a1_w)
        a2 = (a2_n1g, a2_n1b, a2_kqvw, a2_kqvb, a2_projw, a2_projb, a2_n2g, a2_n2b, a2_w1, a2_b1, a2_w2, a2_b2, a2_w)
        return _forward(x, a1, a2, proj_w, proj_b)

    def _L0_attn_ref(x, QW_w, QW_b, KW_w, KW_b, VW_w, VW_b, OW_w, OW_b):
        import jax, jax.numpy as jnp
        import numpy as np
        NUM_HEADS = 12
        D = 192
        HD = D // NUM_HEADS
        b, s, _ = x.shape

        def proj(w, bias):
            y = jnp.einsum('bsd,ed->bse', x, w) + bias
            return y.reshape(b, s, NUM_HEADS, HD).transpose(0, 2, 1, 3)
        q = proj(QW_w, QW_b)
        k = proj(KW_w, KW_b)
        v = proj(VW_w, VW_b)
        scores = jnp.einsum('bhqd,bhkd->bhqk', q, k) / jnp.sqrt(jnp.float32(HD))
        attn = jax.nn.softmax(scores, axis=-1)
        out = jnp.einsum('bhqk,bhkd->bhqd', attn, v)
        out = out.transpose(0, 2, 1, 3).reshape(b, s, NUM_HEADS * HD)
        return jnp.einsum('bsd,ed->bse', out, OW_w) + OW_b

    def _L0_ffn_ref(x, ln1_g, ln1_b, qkv_w, proj_w, proj_b, ln2_g, ln2_b, gate_w, gate_b, w1, b1, w2, b2):
        import jax, jax.numpy as jnp
        import numpy as np
        B, N, DIM, HEADS = (4, 256, 192, 12)
        HIDDEN, E, TOPK = (768, 8, 2)
        EPS = 1e-05

        def _layernorm(x, g, b):
            mu = jnp.mean(x, axis=-1, keepdims=True)
            var = jnp.var(x, axis=-1, keepdims=True)
            return (x - mu) * jax.lax.rsqrt(var + EPS) * g + b
        b, n, d = x.shape
        hd = d // HEADS
        scale = hd ** (-0.5)
        h = _layernorm(x, ln1_g, ln1_b)
        qkv = h @ qkv_w.T
        qkv = qkv.reshape(b, n, 3, HEADS, hd).transpose(2, 0, 3, 1, 4)
        q, k, v = (qkv[0], qkv[1], qkv[2])
        attn = jax.nn.softmax(jnp.einsum('bhnd,bhmd->bhnm', q, k) * scale, axis=-1)
        a = jnp.einsum('bhnm,bhmd->bhnd', attn, v)
        a = a.transpose(0, 2, 1, 3).reshape(b, n, d)
        a = a @ proj_w.T + proj_b
        x = x + a
        h2 = _layernorm(x, ln2_g, ln2_b)
        t = h2.reshape(-1, d)
        T = t.shape[0]
        logits = t @ gate_w.T + gate_b
        top_val, top_idx = jax.lax.top_k(logits, TOPK)
        score = jax.nn.softmax(top_val, axis=-1)
        cw = jnp.zeros((T, E), t.dtype).at[jnp.arange(T)[:, None], top_idx].add(score)
        out = jnp.zeros_like(t)
        for e in range(E):
            he = jax.nn.gelu(t @ w1[e].T + b1[e], approximate=False)
            ye = he @ w2[e].T + b2[e]
            out = out + cw[:, e:e + 1] * ye
        return x + out.reshape(b, n, d)

    def _L1_attn_ref(x, A_w1, A_b1, A_w2, A_b2, B_w1, B_b1, B_w2, B_b2, C_w1, C_b1, C_w2, C_b2, d_w1, d_b1, d_w2, d_b2, D_param, log_dt):
        import jax, jax.numpy as jnp
        import numpy as np
        D_MODEL = 192
        D_STATE = 16
        DT_MIN, DT_MAX = (0.001, 0.1)

        def _mlp(x, w1, b1, w2, b2):
            return jax.nn.silu(x @ w1 + b1) @ w2 + b2

        def _ssm_forward(x, A_w1, A_b1, A_w2, A_b2, B_w1, B_b1, B_w2, B_b2, C_w1, C_b1, C_w2, C_b2, d_w1, d_b1, d_w2, d_b2, D_param, log_dt):
            Bsz, L, Dm = x.shape
            N = A_w2.shape[1]
            A_log = -jnp.abs(_mlp(x, A_w1, A_b1, A_w2, A_b2))
            Bv = _mlp(x, B_w1, B_b1, B_w2, B_b2)
            Cv = _mlp(x, C_w1, C_b1, C_w2, C_b2)
            delta = jax.nn.sigmoid(_mlp(x, d_w1, d_b1, d_w2, d_b2))
            dt = jnp.exp(log_dt)

            def step(state, inp):
                a, b, c, dlt, u_t = inp
                dA = jnp.exp(a[:, None, :] * dt[None, :, None])
                dB = b[:, None, :] * dt[None, :, None]
                cur = u_t[:, :, None] * dB
                state = (dlt[:, :, None] * state + (1.0 - dlt[:, :, None]) * cur) * dA
                y = jnp.sum(state * c[:, None, :], axis=2) + u_t * D_param
                return (state, y)
            init = jnp.zeros((Bsz, Dm, N), x.dtype)
            xs = (jnp.swapaxes(A_log, 0, 1), jnp.swapaxes(Bv, 0, 1), jnp.swapaxes(Cv, 0, 1), jnp.swapaxes(delta, 0, 1), jnp.swapaxes(x, 0, 1))
            _, ys = jax.lax.scan(step, init, xs)
            return jnp.swapaxes(ys, 0, 1)
        return _ssm_forward(x, A_w1, A_b1, A_w2, A_b2, B_w1, B_b1, B_w2, B_b2, C_w1, C_b1, C_w2, C_b2, d_w1, d_b1, d_w2, d_b2, D_param, log_dt)

    def _L1_ffn_ref(x, Wg, bg, W1, W2, W3):
        import jax, jax.numpy as jnp
        import numpy as np
        NUM_EXPERT = 8
        TOP_K = 1
        B, S, D = x.shape
        E = Wg.shape[0]
        xf = x.reshape(B * S, D)
        gate = xf @ Wg.T + bg
        vals, idx = jax.lax.top_k(gate, TOP_K)
        probs = jax.nn.softmax(vals, axis=-1)
        dispatch = jnp.sum(jax.nn.one_hot(idx, E, dtype=x.dtype) * probs[..., None], axis=1)
        h = jax.nn.silu(jnp.einsum('td,efd->tef', xf, W1)) * jnp.einsum('td,efd->tef', xf, W2)
        out = jnp.einsum('tef,edf,te->td', h, W3, dispatch)
        return out.reshape(B, S, D)
    h = _L0_tok_ref(x, L0_tok_a1_n1g, L0_tok_a1_n1b, L0_tok_a1_kqvw, L0_tok_a1_kqvb, L0_tok_a1_projw, L0_tok_a1_projb, L0_tok_a1_n2g, L0_tok_a1_n2b, L0_tok_a1_w1, L0_tok_a1_b1, L0_tok_a1_w2, L0_tok_a1_b2, L0_tok_a1_w, L0_tok_a2_n1g, L0_tok_a2_n1b, L0_tok_a2_kqvw, L0_tok_a2_kqvb, L0_tok_a2_projw, L0_tok_a2_projb, L0_tok_a2_n2g, L0_tok_a2_n2b, L0_tok_a2_w1, L0_tok_a2_b1, L0_tok_a2_w2, L0_tok_a2_b2, L0_tok_a2_w, L0_tok_proj_w, L0_tok_proj_b)
    h = jnp.concatenate([jnp.broadcast_to(cls_tok, (h.shape[0], 1, h.shape[2])), h], axis=1)
    h = h + _L0_attn_ref(_layernorm(h, axis=-1), L0_attn_QW_w, L0_attn_QW_b, L0_attn_KW_w, L0_attn_KW_b, L0_attn_VW_w, L0_attn_VW_b, L0_attn_OW_w, L0_attn_OW_b)
    h = h + _L0_ffn_ref(_layernorm(h, axis=-1), L0_ffn_ln1_g, L0_ffn_ln1_b, L0_ffn_qkv_w, L0_ffn_proj_w, L0_ffn_proj_b, L0_ffn_ln2_g, L0_ffn_ln2_b, L0_ffn_gate_w, L0_ffn_gate_b, L0_ffn_w1, L0_ffn_b1, L0_ffn_w2, L0_ffn_b2)
    h = h + _L1_attn_ref(_layernorm(h, axis=-1), L1_attn_A_w1, L1_attn_A_b1, L1_attn_A_w2, L1_attn_A_b2, L1_attn_B_w1, L1_attn_B_b1, L1_attn_B_w2, L1_attn_B_b2, L1_attn_C_w1, L1_attn_C_b1, L1_attn_C_w2, L1_attn_C_b2, L1_attn_d_w1, L1_attn_d_b1, L1_attn_d_w2, L1_attn_d_b2, L1_attn_D_param, L1_attn_log_dt)
    h = h + _L1_ffn_ref(_layernorm(h, axis=-1), L1_ffn_Wg, L1_ffn_bg, L1_ffn_W1, L1_ffn_W2, L1_ffn_W3)
    return h

_drawn_inputs = setup_inputs


def setup_inputs(seed=0):
    import zlib

    import numpy as np

    out = dict(_drawn_inputs(seed))
    spreads = {'L0_tok_a1_n1g': (1.0, 0.2),
     'L0_tok_a1_n1b': (0.0, 0.1),
     'L0_tok_a1_kqvb': (0.0, 0.1),
     'L0_tok_a1_projb': (0.0, 0.1),
     'L0_tok_a1_n2g': (1.0, 0.6),
     'L0_tok_a1_n2b': (0.0, 0.8),
     'L0_tok_a1_b1': (0.0, 0.288),
     'L0_tok_a1_b2': (0.0, 0.1),
     'L0_tok_a2_n1g': (1.0, 0.2),
     'L0_tok_a2_n1b': (0.0, 0.1),
     'L0_tok_a2_kqvb': (0.0, 0.1),
     'L0_tok_a2_projb': (0.0, 0.1),
     'L0_tok_a2_n2g': (1.0, 0.6),
     'L0_tok_a2_n2b': (0.0, 0.8),
     'L0_tok_a2_b1': (0.0, 0.433),
     'L0_tok_a2_b2': (0.0, 0.1),
     'L0_tok_proj_b': (0.0, 0.1),
     'L0_ffn_ln1_g': (1.0, 0.6),
     'L0_ffn_ln1_b': (0.0, 0.8),
     'L0_ffn_proj_b': (0.0, 0.1),
     'L0_ffn_ln2_g': (1.0, 0.2),
     'L0_ffn_ln2_b': (0.0, 0.376),
     'L0_ffn_gate_b': (0.0, 0.1),
     'L0_ffn_b1': (0.0, 0.459),
     'L0_ffn_b2': (0.0, 0.1),
     'L1_ffn_bg': (0.0, 0.8)}
    factors = {'L0_tok_a1_w': 6.259,
     'L0_attn_QW_w': 8.0,
     'L0_attn_QW_b': 8.0,
     'L0_attn_KW_w': 8.0,
     'L0_attn_KW_b': 64.0,
     'L1_attn_A_w1': 8.0,
     'L1_attn_A_b1': 8.0,
     'L1_attn_A_w2': 8.0,
     'L1_attn_A_b2': 8.0,
     'L1_attn_B_w1': 64.0,
     'L1_attn_B_b1': 64.0,
     'L1_attn_B_w2': 64.0,
     'L1_attn_B_b2': 64.0,
     'L1_attn_C_w1': 64.0,
     'L1_attn_C_b1': 64.0,
     'L1_attn_C_w2': 64.0,
     'L1_attn_C_b2': 64.0,
     'L1_attn_d_w1': 64.0,
     'L1_attn_d_b1': 64.0,
     'L1_attn_d_w2': 64.0,
     'L1_attn_d_b2': 64.0,
     'L1_attn_log_dt': 64.0,
     'L1_ffn_Wg': 5.437,
     'L1_ffn_W1': 5.505,
     'L1_ffn_W2': 5.482,
     'L1_ffn_W3': 5.334}
    for name, (base, spread) in spreads.items():
        noise = np.random.default_rng([zlib.crc32(name.encode()), seed]).standard_normal(out[name].shape)
        drawn = base * np.exp(spread * noise) if base else spread * noise
        out[name] = jnp.asarray(drawn.astype(out[name].dtype))
    for name, factor in factors.items():
        out[name] = (out[name] * factor).astype(out[name].dtype)
    return out
```

```python
from contextlib import ExitStack

import concourse.bass as bass
from concourse import mybir
from concourse.alu_op_type import AluOpType as ALU

ACT = mybir.ActivationFunctionType
F32 = mybir.dt.float32
I32, U32 = mybir.dt.int32, mybir.dt.uint32
AX_X = mybir.AxisListType.X
PARTS = 128
BANK = 512

IMAGES, CHANNELS, SIDE = 32, 3, 128
EMB, FEATS = 64, 32
EPS = 1e-5


def dram(ap, offset, dims):
    return bass.AP(ap.tensor, offset, [list(d) for d in dims])


def spread(ap, axis, n):
    shape = list(ap.shape)
    return ap.unsqueeze(axis).broadcast_to(shape[:axis] + [n] + shape[axis:])


def wait(eng, sem, n):
    if not isinstance(n, int) or n > 0:
        eng.wait_ge(sem, n)


class Stage:

    def __init__(self, nc, ctx, name):
        self.nc, self.ctx, self.name = nc, ctx, name

    def sbuf(self, name, shape, dtype=F32):
        return self.ctx.enter_context(self.nc.sbuf_tensor(f"{self.name}_{name}", shape, dtype))

    def psum(self):
        return self.ctx.enter_context(self.nc.psum_tensor(f"{self.name}_psum", [PARTS, 8 * BANK], F32))

    def sem(self, name):
        return self.nc.alloc_semaphore(name=f"{self.name}_{name}")


def make_identity(nc, pool, ident, done):
    nc.gpsimd.memset(ident[:], 0.0).then_inc(done, 1)
    pool.wait_ge(done, 1)
    nc.gpsimd.affine_select(out=ident[:], in_=ident[:], compare_op=ALU.not_equal, fill=1.0, base=0,
                            pattern=[[-1, PARTS]], channel_multiplier=1).then_inc(done, 1)


PAD_ROWS, PAD_COLS = 132, 132


def pad_image(nc, x, xpad):
    with ExitStack() as ctx:
        st = Stage(nc, ctx, "pad")
        zeros = st.sbuf("zeros", [PARTS, PAD_COLS * 2])
        s_zero, s_edges, s_copy = st.sem("zero"), st.sem("edges"), st.sem("copy")
        planes = IMAGES * CHANNELS
        plane = PAD_ROWS * PAD_COLS
        block = ctx.enter_context(nc.Block())

        @block.vector
        def _(dve):
            nc.vector.memset(zeros[:], 0.0).then_inc(s_zero, 1)

        @block.sync
        def _(sp):
            parts = 4
            step = planes // parts
            for n in range(parts):
                sp.dma_start(dram(xpad, n * step * plane + 2 * PAD_COLS + 2, [(plane, step), (PAD_COLS, SIDE), (1, SIDE)]),
                             dram(x, n * step * SIDE * SIDE, [(SIDE * SIDE, step), (SIDE, SIDE), (1, SIDE)])).then_inc(s_copy, 16)
            sp.wait_ge(s_copy, 16 * parts)

        @block.scalar
        def _(act):
            act.wait_ge(s_zero, 1)
            act.dma_start(dram(xpad, 0, [(plane, planes), (1, 2 * PAD_COLS)]), zeros[0:planes, :]).then_inc(s_edges, 16)
            act.dma_start(dram(xpad, 130 * PAD_COLS, [(plane, planes), (1, 2 * PAD_COLS)]), zeros[0:planes, :]).then_inc(s_edges, 16)
            for c in (0, 130):
                act.dma_start(dram(xpad, 2 * PAD_COLS + c, [(plane, planes), (PAD_COLS, SIDE), (1, 2)]),
                              zeros[0:planes, 0:2 * SIDE].rearrange("p (a b) -> p a b", b=2)).then_inc(s_edges, 16)
            act.wait_ge(s_edges, 16 * 4)



def performer(nc, name, src, dst, w, first):
    quads = 2 if first else 1
    tiles = 4 * quads
    steps = IMAGES if first else IMAGES // 2
    own = 1 if first else 2
    dim = 147 if first else 576
    width = 126 if first else 577
    ktiles = [(0, 126)] if first else [(0, 128), (128, 128), (256, 128), (384, 128), (512, 65)]
    rem = dim - 126
    taps = 9
    COLS = 256

    with ExitStack() as ctx:
        st = Stage(nc, ctx, name)
        ps = st.psum()
        ident = st.sbuf("ident", [PARTS, PARTS])
        W = st.sbuf("W", [PARTS, len(ktiles), COLS])
        Wrem = st.sbuf("Wrem", [PARTS, 4, COLS]) if first else None
        projw1 = st.sbuf("projw1", [EMB + 1, EMB + 1])
        w1 = st.sbuf("w1", [PARTS, PARTS])
        w2 = st.sbuf("w2", [PARTS, PARTS])
        b1 = st.sbuf("b1", [PARTS, 1])
        b2 = st.sbuf("b2", [PARTS, EMB])
        projb = st.sbuf("projb", [PARTS, EMB])
        mask = st.sbuf("mask", [PARTS, 4])
        mhalf = st.sbuf("mhalf", [PARTS, 8])
        epst = st.sbuf("eps", [PARTS, 8])

        with ExitStack() as ctx2:
            s2 = Stage(nc, ctx2, name + "_prep")
            s_w, s_id, s_bias, s_gain, s_kq, s_kqs, s_feat, s_featdone, s_rem, s_ready = (
                s2.sem(n) for n in ("w", "id", "bias", "gain", "kq", "kqs", "feat", "featdone", "rem", "ready"))
            s_bd, s_small, s_zero, s_mv = s2.sem("bd"), s2.sem("small"), s2.sem("zero"), s2.sem("mv")
            gcol = s2.sbuf("gcol", [PARTS, 6])
            bcol = s2.sbuf("bcol", [PARTS, 6])
            Wr = s2.sbuf("Wr", [PARTS, 1, COLS])
            kqvb = s2.sbuf("kqvb", [1, 3 * EMB])
            brow = s2.sbuf("brow", [1, 3 * EMB])
            wr2 = s2.sbuf("wr2", [FEATS, 2 * EMB])
            WB = s2.sbuf("WB", [PARTS, 2 * FEATS])
            WT = s2.sbuf("WT", [PARTS, PARTS])
            g2 = s2.sbuf("g2", [PARTS, 1])
            n2b = s2.sbuf("n2b", [PARTS, 1])
            b1r = s2.sbuf("b1r", [PARTS, 1])
            if first:
                parts_of = [(126, 126, W[:, 0, :]), (rem, rem + 1, Wr[:, 0, :])]
            else:
                parts_of = [(128, 128, W[:, k, :]) for k in range(4)] + [(64, 65, W[:, 4, :])]
            nk = len(parts_of)
            block = ctx2.enter_context(nc.Block())

            @block.sync
            def _(sp):
                n = 0
                ctx2.enter_context(nc.allow_non_contiguous_dma(reason="columns of a few hundred gains and biases"))
                sp.wait_ge(s_zero, 4)
                for k, (rows, _, place) in enumerate(parts_of):
                    if first:
                        sp.dma_start(place[0:rows, 0:3 * EMB], w["kqvw"][126 * k:126 * k + rows, :]).then_inc(s_w, 16)
                        sp.dma_start(gcol[0:rows, k:k + 1], dram(w["n1g"], 126 * k, [(1, rows), (1, 1)])).then_inc(s_w, 16)
                        sp.dma_start(bcol[0:rows, k:k + 1], dram(w["n1b"], 126 * k, [(1, rows), (1, 1)])).then_inc(s_w, 16)
                        n += 3
                    else:
                        for half in range(rows // EMB):
                            tap, p0 = 2 * k + half, EMB * half
                            sp.dma_start(place[p0:p0 + EMB, 0:3 * EMB],
                                         dram(w["kqvw"], tap * 3 * EMB, [(taps * 3 * EMB, EMB), (1, 3 * EMB)])).then_inc(s_w, 16)
                            sp.dma_start(gcol[p0:p0 + EMB, k:k + 1], dram(w["n1g"], tap, [(taps, EMB), (1, 1)])).then_inc(s_w, 16)
                            sp.dma_start(bcol[p0:p0 + EMB, k:k + 1], dram(w["n1b"], tap, [(taps, EMB), (1, 1)])).then_inc(s_w, 16)
                            n += 3
                sp.dma_start(kqvb[0:1, :], dram(w["kqvb"], 0, [(1, 1), (1, 3 * EMB)])).then_inc(s_w, 16)
                for half in range(2):
                    p0 = EMB * half
                    sp.dma_start(wr2[:, p0:p0 + EMB], w["w"]).then_inc(s_w, 16)
                    sp.dma_start(w1[p0:p0 + EMB, p0:p0 + EMB], w["w1"]).then_inc(s_w, 16)
                    sp.dma_start(w2[p0:p0 + EMB, p0:p0 + EMB], w["w2"]).then_inc(s_w, 16)
                    sp.dma_start(g2[p0:p0 + EMB, :], dram(w["n2g"], 0, [(1, EMB), (1, 1)])).then_inc(s_w, 16)
                    sp.dma_start(n2b[p0:p0 + EMB, :], dram(w["n2b"], 0, [(1, EMB), (1, 1)])).then_inc(s_w, 16)
                    sp.dma_start(b1r[p0:p0 + EMB, :], dram(w["b1"], 0, [(1, EMB), (1, 1)])).then_inc(s_w, 16)
                sp.dma_start(projw1[0:EMB, 0:EMB], w["projw"]).then_inc(s_w, 16)
                sp.dma_start(b2[:], dram(w["b2"], 0, [(0, PARTS), (1, EMB)])).then_inc(s_w, 16)
                sp.dma_start(projb[:], dram(w["projb"], 0, [(0, PARTS), (1, EMB)])).then_inc(s_w, 16)
                n += 1 + 12 + 3
                sp.wait_ge(s_w, 16 * n)
                sp.sem_inc(s_ready, 1)
                if first:
                    sp.wait_ge(s_gain, nk + 1)
                    sp.dma_start(Wr[rem:rem + 1, 0, 0:3 * EMB], brow[0:1, :]).then_inc(s_bd, 16)
                    sp.wait_ge(s_featdone, nk)
                    for q in range(4):
                        sp.dma_start(Wrem[32 * q:32 * q + rem + 1, q, :], Wr[0:rem + 1, 0, :]).then_inc(s_rem, 16)
                    sp.wait_ge(s_rem, 64)

            @block.gpsimd
            def _(pool):
                make_identity(nc, pool, ident, s_id)

            @block.vector
            def _(dve):
                nc.vector.memset(w1[:], 0.0).then_inc(s_zero, 1)
                nc.vector.memset(w2[:], 0.0).then_inc(s_zero, 1)
                nc.vector.memset(projw1[:], 0.0).then_inc(s_zero, 1)
                nc.vector.memset(Wr[:], 0.0).then_inc(s_zero, 1)
                nc.vector.memset(WB[:], 0.0).then_inc(s_mv, 1)
                if first:
                    nc.vector.memset(Wrem[:], 0.0).then_inc(s_mv, 1)
                nc.vector.memset(mask[:], 0.0).then_inc(s_small, 1)
                nc.vector.memset(mhalf[:], -0.5)
                nc.vector.memset(epst[:], EPS)
                dve.wait_ge(s_small, 1)
                for q in range(4):
                    nc.vector.memset(mask[32 * q:32 * q + 32, q:q + 1], 1.0)
                dve.wait_ge(s_ready, 1)
                nc.vector.memset(projw1[EMB:EMB + 1, EMB:EMB + 1], 1.0)
                dve.wait_ge(s_bias, 1)
                nc.vector.tensor_tensor(brow[0:1, :], ps[0:1, 0:3 * EMB], kqvb[0:1, :], ALU.add).then_inc(s_gain, 1)
                for k, (rows, _, place) in enumerate(parts_of):
                    nc.vector.tensor_scalar(place[0:rows, 0:3 * EMB], place[0:rows, 0:3 * EMB], gcol[0:rows, k:k + 1],
                                            None, ALU.mult).then_inc(s_gain, 1)
                if not first:
                    dve.wait_ge(s_gain, 1)
                    nc.vector.tensor_copy(W[EMB:EMB + 1, 4, 0:3 * EMB], brow[0:1, :]).then_inc(s_bd, 16)
                dve.wait_ge(s_kq, 1)
                dve.wait_ge(s_mv, 1)
                nc.vector.tensor_copy(WB[0:EMB, 0:FEATS], ps[0:EMB, BANK:BANK + FEATS])
                nc.vector.tensor_copy(WB[EMB:, FEATS:], ps[EMB:, BANK:BANK + FEATS]).then_inc(s_kqs, 1)
                for k, (_, rows, place) in enumerate(parts_of):
                    dve.wait_ge(s_kq, k + 2)
                    nc.vector.tensor_copy(WT[:, 0:rows], ps[:, 2 * BANK:2 * BANK + rows]).then_inc(s_kqs, 1)
                    dve.wait_ge(s_feat, k + 1)
                    nc.vector.tensor_copy(place[0:rows, 3 * EMB:COLS], ps[0:rows, 3 * BANK:3 * BANK + 2 * FEATS]).then_inc(s_featdone, 1)
                dve.wait_ge(s_bias, 2)
                nc.vector.tensor_tensor(b1[:], ps[:, 4 * BANK:4 * BANK + 1], b1r[:], ALU.add)
                nc.vector.tensor_scalar(w1[:], w1[:], g2[:, 0:1], None, ALU.mult)

            @block.tensor
            def _(pe):
                pe.wait_ge(s_ready, 1)
                for k, (rows, _, place) in enumerate(parts_of):
                    last = nc.tensor.matmul(ps[0:1, 0:3 * EMB], bcol[0:rows, k:k + 1], place[0:rows, 0:3 * EMB],
                                            start=(k == 0), stop=(k == nk - 1))
                last.then_inc(s_bias, 1)
                nc.tensor.matmul(ps[:, 4 * BANK:4 * BANK + 1], w1[:], n2b[:, 0:1], start=True, stop=True).then_inc(s_bias, 1)
                pe.wait_ge(s_id, 2)
                nc.tensor.transpose(ps[:, BANK:BANK + FEATS], wr2[:], ident[0:FEATS, 0:FEATS]).then_inc(s_kq, 1)
                pe.wait_ge(s_bd, 16)
                pe.wait_ge(s_gain, nk + 1)
                for k, (_, rows, place) in enumerate(parts_of):
                    wait(pe, s_kqs, k + 1)
                    nc.tensor.transpose(ps[:, 2 * BANK:2 * BANK + rows], place[0:rows, 0:2 * EMB], ident[0:rows, 0:rows]).then_inc(s_kq, 1)
                    pe.wait_ge(s_kqs, k + 2)
                    wait(pe, s_featdone, k)
                    nc.tensor.matmul(ps[0:rows, 3 * BANK:3 * BANK + 2 * FEATS], WT[:, 0:rows], WB[:], start=True, stop=True).then_inc(s_feat, 1)

        X = [st.sbuf(f"X{p}", [PARTS, 21, 35] if first else [PARTS, 4, dim]) for p in range(2)]
        hN = st.sbuf("hN", [PARTS, tiles, width])
        hR = st.sbuf("hR", [PARTS, tiles, 32]) if first else None
        stats = st.sbuf("stats", [PARTS, tiles, 1 if first else 2, 6])
        mv = st.sbuf("mv", [PARTS, tiles, 2])
        rstd = st.sbuf("rstd", [PARTS, tiles])
        nkt = 1 if first else 5
        hT = st.sbuf("hT", [PARTS, quads if first else nkt, BANK])
        RQ = st.sbuf("RQ", [PARTS, BANK])
        sq = st.sbuf("sq", [PARTS, tiles, 2, EMB])
        xd = st.sbuf("xd", [PARTS, tiles, 2])
        v1 = st.sbuf("v1", [PARTS, tiles, EMB + 1])
        z = st.sbuf("z", [PARTS, 2, tiles, FEATS])
        kpq = st.sbuf("kpq", [PARTS, 2, tiles, FEATS])
        kvT = st.sbuf("kvT", [EMB + 1, 4, FEATS])
        BD = st.sbuf("BD", [PARTS, 4, EMB + 1])
        den = st.sbuf("den", [PARTS, tiles])
        rden = st.sbuf("rden", [PARTS, tiles])
        vp = st.sbuf("vp", [PARTS, tiles, EMB])
        y = st.sbuf("y", [PARTS, tiles, EMB])
        yb = st.sbuf("yb", [PARTS, tiles, EMB])
        stats2 = st.sbuf("stats2", [PARTS, tiles, 6])
        mv2 = st.sbuf("mv2", [PARTS, tiles, 2])
        rstd2 = st.sbuf("rstd2", [PARTS, tiles])
        yn = st.sbuf("yn", [PARTS, tiles, EMB])
        yT = st.sbuf("yT", [PARTS, tiles // 2, PARTS])
        G = st.sbuf("G", [PARTS, tiles // 2, PARTS])
        O = [st.sbuf(f"O{p}", [PARTS, tiles, EMB]) for p in range(2)]
        BDz = st.sbuf("BDz", [IMAGES, 33 * EMB])
        half = tiles // 2 * PARTS

        names = ("x_in0", "x_in1", "out0", "out1", "border", "stat", "aggr", "eps1", "rstd1", "norm", "trans", "tback", "rem", "kq", "sq", "v", "xd", "z", "exp",
                 "kv", "kvs", "qt", "rq", "kp", "bd", "num", "den", "rden", "ymul", "y", "vp", "yb", "stat2", "aggr2",
                 "eps2", "rstd2", "norm2", "yt", "yts", "m1", "gelu", "m2", "fin", "ones", "zero", "tail", "load")
        s = {n: st.sem(n) for n in names}
        nq = quads if first else 1
        nt = quads if first else nkt
        out_dmas = 4 if first else 4
        in_dmas = 12 if first else 12

        def bank(b, n=BANK):
            return ps[:, b * BANK:b * BANK + n]

        KQ = [ps[:, (2 + 2 * q) * BANK:(4 + 2 * q) * BANK].rearrange("p (t c) -> p t c", c=COLS) for q in range(quads)]
        KV, KP = ps[0:EMB + 1, 6 * BANK:6 * BANK + own * FEATS], ps[:, 6 * BANK + 64:6 * BANK + 64 + EMB + 1]
        NUM = [ps[:, 6 * BANK + 192:6 * BANK + 192 + 4 * (EMB + 1)].rearrange("p (t c) -> p t c", c=EMB + 1),
               ps[:, 7 * BANK:7 * BANK + 4 * (EMB + 1)].rearrange("p (t c) -> p t c", c=EMB + 1)]

        def window(p, j, n=21):
            return X[p][:, 0:n, 4 * j:4 * j + 7] if first else X[p][:, j, :]

        def twice(each, i, p):
            return each * (i - p + 2) // 2 if isinstance(i, int) else (i - p) * (each // 2) + each

        def live(i):
            return 0 <= i < steps if isinstance(i, int) else True

        def schedule(eng, body):
            for t in range(4):
                body(t, t % 2)
            with eng.Fori(4, steps, 2) as t:
                body(t, 0)
                body(t + 1, 1)
            for t in range(steps, steps + 3):
                body(t, t % 2)

        block = ctx.enter_context(nc.Block())

        @block.sync
        def _(sp):
            sp.wait_ge(s["zero"], 1)
            rows = 33 if first else 17
            pic = rows * rows * EMB
            sp.dma_start(dram(dst, 0, [(pic, IMAGES), (1, rows * EMB)]),
                         BDz[0:IMAGES, 0:rows * EMB]).then_inc(s["border"], 16)
            sp.dma_start(dram(dst, rows * EMB, [(pic, IMAGES), (rows * EMB, rows - 1), (1, EMB)]),
                         BDz[0:IMAGES, 0:(rows - 1) * EMB].rearrange("p (a b) -> p a b", b=EMB)).then_inc(s["border"], 16)

            def load(i, p):
                wait(sp, s["norm"], i - 1)
                if first:
                    sp.sem_inc(s["load"], 1)
                    wait(sp, s["tail"], 2 * (i - 1))
                sp.sem_inc(s["load"], 1)
                if first:
                    for ob in range(4):
                        for c in range(CHANNELS):
                            sp.dma_start(X[p][32 * ob:32 * ob + 32, 7 * c:7 * c + 7, :],
                                         dram(src, (i * CHANNELS + c) * (PAD_ROWS * PAD_COLS) + 32 * ob,
                                              [(4 * PAD_COLS, 32), (PAD_COLS, 7), (1, 35)])).then_inc(s["x_in%d" % p], 16)
                else:
                    for im in range(2):
                        for tl in range(2):
                            for ky in range(3):
                                sp.dma_start(X[p][:, 2 * im + tl, 192 * ky:192 * ky + 192],
                                             dram(src, (2 * i + im) * (33 * 33 * EMB) + (16 * tl + ky) * 33 * EMB,
                                                  [(2 * 33 * EMB, 8), (2 * EMB, 16), (1, 3 * EMB)])).then_inc(s["x_in%d" % p], 16)

            def store(i, p):
                sp.wait_ge(s["fin"], i + 1)
                sp.sem_inc(s["load"], 1)
                if first:
                    for ob in range(4):
                        sp.dma_start(dram(dst, i * pic + (33 + 1 + 8 * ob) * EMB, [(33 * EMB, 32), (1, 8 * EMB)]),
                                     O[p][32 * ob:32 * ob + 32, :, :]).then_inc(s["out%d" % p], 16)
                else:
                    for im in range(2):
                        for tl in range(2):
                            sp.dma_start(dram(dst, (2 * i + im) * pic + (17 * (1 + 8 * tl) + 1) * EMB,
                                              [(17 * EMB, 8), (EMB, 16), (1, EMB)]), O[p][:, 2 * im + tl, :]).then_inc(s["out%d" % p], 16)

            def body(t, p):
                if live(t):
                    load(t, p)
                if live(t - 3):
                    store(t - 3, 1 - p)

            schedule(sp, body)
            sp.wait_ge(s["border"], 32)
            for p in range(2):
                sp.wait_ge(s["out%d" % p], 16 * out_dmas * steps // 2)

        @block.gpsimd
        def _(pool):
            nc.gpsimd.memset(BDz[:], 0.0).then_inc(s["zero"], 1)
            if first:
                nc.gpsimd.memset(hR[:, :, rem + 1:], 0.0)
                nc.gpsimd.memset(hR[:, :, rem:rem + 1], 1.0)
            else:
                nc.gpsimd.memset(hN[:, :, dim:dim + 1], 1.0)
            nc.gpsimd.memset(v1[:, :, EMB:EMB + 1], 1.0).then_inc(s["ones"], 1)

            def inverse_root(i, aggr, eps, done, mvt, out):
                pool.wait_ge(s[aggr], tiles * (i + 1))
                nc.gpsimd.tensor_tensor(out[:], mvt[:, :, 1], epst[:, 0:tiles], ALU.add).then_inc(s[eps], 1)
                pool.wait_ge(s[eps], i + 1)
                nc.gpsimd.tensor_tensor(out[:], out[:], mhalf[:, 0:tiles], ALU.pow).then_inc(s[done], 1)

            def body(t, p):
                if live(t):
                    inverse_root(t, "aggr", "eps1", "rstd1", mv, rstd)
                    if first:
                        tail = bass.AP(X[p][:].tensor, 18 * 35, [list(X[p][:].ap[0]), [4, tiles], [35, 3], [1, 7]])
                        out = hR[:, :, 0:rem].rearrange("p t (a b) -> p t a b", b=7)
                        wait(pool, s["trans"], 3 * t)
                        nc.gpsimd.tensor_tensor(out, tail, spread(spread(mv[:, :, 0], 2, 3), 3, 7), ALU.subtract).then_inc(s["tail"], 1)
                        pool.wait_ge(s["tail"], 2 * t + 1)
                        nc.gpsimd.tensor_tensor(hR[:, :, 0:rem], hR[:, :, 0:rem], spread(rstd[:], 2, rem), ALU.mult).then_inc(s["tail"], 1)
                if live(t - 2):
                    k = t - 2
                    pool.wait_ge(s["y"], k + 1)
                    wait(pool, s["fin"], k)
                    nc.gpsimd.tensor_tensor(yb[:], y[:], spread(b2[:], 1, tiles), ALU.add).then_inc(s["yb"], 1)
                    inverse_root(k, "aggr2", "eps2", "rstd2", mv2, rstd2)
                if live(t - 1):
                    m = t - 1
                    pool.wait_ge(s["v"], quads * (m + 1))
                    wait(pool, s["y"], m)
                    nc.gpsimd.tensor_tensor(vp[:], v1[:, :, 0:EMB], spread(projb[:], 1, tiles), ALU.add).then_inc(s["vp"], 1)

            schedule(pool, body)

        @block.vector
        def _(dve):
            def statistics(i, p):
                if first:
                    wait(dve, s["tail"], 2 * i)
                dve.wait_ge(s["x_in%d" % p], twice(16 * in_dmas, i, p))
                for j in range(tiles):
                    if first:
                        nc.vector.bn_stats(stats[:, j, 0, :], window(p, j)).then_inc(s["stat"], 1)
                    else:
                        for h in range(2):
                            last = nc.vector.bn_stats(stats[:, j, h, :], X[p][:, j, 288 * h:288 * h + 288])
                        last.then_inc(s["stat"], 1)

            def aggregate(i):
                for j in range(tiles):
                    nc.vector.bn_aggr(mv[:, j, :], stats[:, j, :, :].rearrange("p a b -> p (a b)")).then_inc(s["aggr"], 1)

            def normalise(i, p):
                dve.wait_ge(s["rstd1"], i + 1)
                wait(dve, s["trans"], (nt + (1 if first else 0)) * i)
                for j in range(tiles):
                    out = hN[:, j, :].rearrange("p (a b) -> p a b", b=7) if first else hN[:, j, 0:dim]
                    last = nc.vector.tensor_scalar(out, window(p, j, 18), mv[:, j, 0:1], rstd[:, j:j + 1], ALU.subtract, ALU.mult)
                last.then_inc(s["norm"], 1)

            def exponent(i, q):
                tl = slice(4 * q, 4 * q + 4)
                dve.wait_ge(s["sq"], quads * i + q + 1)
                nc.vector.reduce_sum(xd[:, tl, :], sq[:, tl, :, :], axis=AX_X).then_inc(s["xd"], 1)
                dve.wait_ge(s["xd"], quads * i + q + 1)
                wait(dve, s["exp"], i)
                dve.wait_ge(s["v"], quads * i + q + 1)
                nc.vector.tensor_tensor(z[:, :, tl, :].rearrange("p a t f -> p t a f"), KQ[q][:, :, 3 * EMB:COLS].rearrange("p t (a f) -> p t a f", a=2),
                                        spread(xd[:, tl, :], 3, FEATS), ALU.subtract).then_inc(s["z"], 1)

            def block_diagonal(i):
                dve.wait_ge(s["kp"], i + 1)
                wait(dve, s["num"], quads * i)
                nc.vector.tensor_tensor(BD[:], spread(KP, 1, 4), spread(mask[:], 2, EMB + 1), ALU.mult).then_inc(s["bd"], 1)

            def attend(i):
                for q in range(quads):
                    dve.wait_ge(s["num"], quads * i + q + 1)
                    nc.vector.tensor_scalar(den[:, 4 * q:4 * q + 4], NUM[q][:, :, EMB], 1e-8 * FEATS, None, ALU.add).then_inc(s["den"], 1)
                dve.wait_ge(s["den"], quads * (i + 1))
                nc.vector.reciprocal(rden[:], den[:]).then_inc(s["rden"], 1)
                dve.wait_ge(s["rden"], i + 1)
                wait(dve, s["yb"], i)
                for q in range(quads):
                    nc.vector.tensor_tensor(y[:, 4 * q:4 * q + 4, :], NUM[q][:, :, 0:EMB],
                                            spread(rden[:, 4 * q:4 * q + 4], 2, EMB), ALU.mult).then_inc(s["ymul"], 1)
                dve.wait_ge(s["ymul"], quads * (i + 1))
                dve.wait_ge(s["vp"], i + 1)
                nc.vector.tensor_tensor(y[:], y[:], vp[:], ALU.add).then_inc(s["y"], 1)
                dve.wait_ge(s["y"], i + 1)
                for j in range(tiles):
                    nc.vector.bn_stats(stats2[:, j, :], y[:, j, :]).then_inc(s["stat2"], 1)

            def aggregate2(i):
                for j in range(tiles):
                    nc.vector.bn_aggr(mv2[:, j, :], stats2[:, j, :]).then_inc(s["aggr2"], 1)

            def normalise2(i):
                dve.wait_ge(s["rstd2"], i + 1)
                wait(dve, s["yt"], i)
                for j in range(tiles):
                    last = nc.vector.tensor_scalar(yn[:, j, :], y[:, j, :], mv2[:, j, 0:1], rstd2[:, j:j + 1], ALU.subtract, ALU.mult)
                last.then_inc(s["norm2"], 1)

            def finish(i, p):
                dve.wait_ge(s["m2"], i + 1)
                dve.wait_ge(s["yb"], i + 1)
                wait(dve, s["out%d" % p], twice(16 * out_dmas, i - 2, p))
                nc.vector.tensor_tensor(O[p][:].rearrange("p t e -> p (t e)"), bank(1, half), yb[:].rearrange("p t e -> p (t e)"),
                                        ALU.add).then_inc(s["fin"], 1)

            def body(t, p):
                if live(t):
                    statistics(t, p)
                    dve.wait_ge(s["stat"], tiles * (t + 1))
                if live(t - 2):
                    block_diagonal(t - 2)
                if live(t):
                    aggregate(t)
                if live(t - 1) and quads == 2:
                    exponent(t - 1, 0)
                if live(t):
                    normalise(t, p)
                if live(t - 3):
                    finish(t - 3, 1 - p)
                if live(t - 2):
                    attend(t - 2)
                    dve.wait_ge(s["stat2"], tiles * (t - 1))
                if live(t - 1):
                    exponent(t - 1, quads - 1)
                if live(t - 2):
                    aggregate2(t - 2)
                    normalise2(t - 2)

            schedule(dve, body)

        @block.scalar
        def _(act):
            def body(t, p):
                m, k, l = t - 1, t - 2, t - 3
                if live(l):
                    act.wait_ge(s["yt"], l + 1)
                    nc.scalar.copy(yT[:].rearrange("p t c -> p (t c)"), bank(7, half)).then_inc(s["yts"], 1)
                if live(m):
                    for q in range(nt):
                        rows = ktiles[0][1] if first else ktiles[q][1]
                        act.wait_ge(s["trans"], (nt + (1 if first else 0)) * m + q + 1)
                        nc.scalar.copy(hT[0:rows, q, :], ps[0:rows, (q % 2) * BANK:(q % 2 + 1) * BANK]).then_inc(s["tback"], 1)
                if live(k):
                    act.wait_ge(s["kv"], k + 1)
                    kv = KV.rearrange("p (i f) -> p i f", f=FEATS)
                    nc.scalar.copy(kvT[:].rearrange("p (i r) f -> p i r f", i=own), spread(kv, 2, 4 // own)).then_inc(s["kvs"], 1)
                if live(m) and first:
                    act.wait_ge(s["trans"], 3 * (m + 1))
                    if live(k):
                        act.wait_ge(s["qt"], k + 1)
                    nc.scalar.copy(RQ[:, 0:256], bank(7)[:, 0:256]).then_inc(s["rem"], 1)
                if live(k):
                    act.wait_ge(s["qt"], k + 1)
                    nc.scalar.copy(RQ[:, 256:256 + PARTS * quads], bank(7)[:, 256:256 + PARTS * quads]).then_inc(s["rq"], 1)

                def squares(q):
                    tl = slice(4 * q, 4 * q + 4)
                    act.wait_ge(s["kq"], quads * m + q + 1)
                    wait(act, s["xd"], quads * m)
                    nc.scalar.activation(sq[:, tl, :, :].rearrange("p t a e -> p t (a e)"), KQ[q][:, :, 0:2 * EMB], ACT.Square,
                                         scale=0.5 ** 0.5).then_inc(s["sq"], 1)
                    wait(act, s["kv"], m)
                    wait(act, s["vp"], m)
                    if isinstance(m, int) and m == 0:
                        act.wait_ge(s["ones"], 1)
                    nc.scalar.copy(v1[:, tl, 0:EMB], KQ[q][:, :, 2 * EMB:3 * EMB]).then_inc(s["v"], 1)

                if live(m):
                    squares(0)
                if live(l):
                    act.wait_ge(s["m1"], l + 1)
                    nc.scalar.activation(G[:].rearrange("p t c -> p (t c)"), bank(0, half), ACT.Gelu, bias=b1[:, 0:1]).then_inc(s["gelu"], 1)
                if live(m):
                    if quads == 2:
                        squares(1)
                    act.wait_ge(s["z"], quads * (m + 1))
                    wait(act, s["qt"], m)
                    nc.scalar.activation(kpq[:].rearrange("p a t f -> p (a t f)"), z[:].rearrange("p a t f -> p (a t f)"), ACT.Exp).then_inc(s["exp"], 1)

            schedule(act, body)

        @block.tensor
        def _(pe):
            def main_transposes(m):
                pe.wait_ge(s["norm"], m + 1)
                if isinstance(m, int) and m == 0:
                    pe.wait_ge(s["ones"], 1)
                for q in range(nt):
                    c0, rows = ktiles[0] if first else ktiles[q]
                    if q == 0:
                        wait(pe, s["gelu"], m - 2)
                        wait(pe, s["tback"], nt * m)
                    if q == 1:
                        wait(pe, s["fin"], m - 2)
                    if q >= 2:
                        pe.wait_ge(s["tback"], nt * m + q - 1)
                    for j in range(4):
                        tile = 4 * q + j if first else j
                        last = nc.tensor.transpose(ps[0:rows, (q % 2) * BANK + PARTS * j:(q % 2) * BANK + PARTS * j + PARTS],
                                                   hN[:, tile, c0:c0 + rows], ident[:])
                    last.then_inc(s["trans"], 1)

            def matmuls(m, q):
                pe.wait_ge(s["tback"], nt * m + (q + 1 if first else nt))
                if first:
                    pe.wait_ge(s["rem"], m + 1)
                wait(pe, s["z"], quads * (m - 1) + q + 1 if not isinstance(m, int) or m >= 1 else 0)
                wait(pe, s["v"], quads * (m - 1) + q + 1 if not isinstance(m, int) or m >= 1 else 0)
                for j in range(4):
                    out = KQ[q][:, j, :]
                    cols = slice(PARTS * j, PARTS * j + PARTS)
                    if first:
                        nc.tensor.matmul(out, hT[0:126, q, cols], W[0:126, 0, :], start=True, stop=False)
                        last = nc.tensor.matmul(out, RQ[:, PARTS * q:PARTS * q + PARTS], Wrem[:, j, :], start=False, stop=True)
                    else:
                        for kt in range(nkt):
                            rows = ktiles[kt][1]
                            last = nc.tensor.matmul(out, hT[0:rows, kt, cols], W[0:rows, kt, :], start=(kt == 0), stop=(kt == nkt - 1))
                last.then_inc(s["kq"], 1)

            def body(t, p):
                m, k, l = t - 1, t - 2, t - 3
                if live(l):
                    pe.wait_ge(s["norm2"], l + 1)
                    if quads == 2:
                        wait(pe, s["ymul"], quads * (l + 1))
                    for j in range(tiles // 2):
                        last = nc.tensor.transpose(bank(7)[:, PARTS * j:PARTS * j + PARTS],
                                                   yn[:, 2 * j:2 * j + 2, :].rearrange("p t e -> p (t e)"), ident[:])
                    last.then_inc(s["yt"], 1)
                if live(m):
                    main_transposes(m)
                if live(k):
                    pe.wait_ge(s["exp"], k + 1)
                    wait(pe, s["ymul"], quads * (k - 1) + 1 if not isinstance(k, int) or k >= 1 else 0)
                    per = tiles // own
                    for im in range(own):
                        for j in range(per):
                            tile = per * im + j
                            last = nc.tensor.matmul(KV[:, FEATS * im:FEATS * im + FEATS], v1[:, tile, :], kpq[:, 0, tile, :],
                                                    start=(j == 0), stop=(j == per - 1))
                    last.then_inc(s["kv"], 1)
                if live(l):
                    pe.wait_ge(s["yts"], l + 1)
                elif live(k):
                    wait(pe, s["ymul"], quads * k)
                if live(m) and first:
                    pe.wait_ge(s["tail"], 2 * (m + 1))
                    for q in range(quads):
                        rows = hR[:, 4 * q:4 * q + 4, :].rearrange("p t c -> p (t c)")
                        wait(pe, s["rq"], m - 1)
                        last = nc.tensor.transpose(bank(7)[:, PARTS * q:PARTS * q + PARTS], rows, ident[:])
                    last.then_inc(s["trans"], 1)
                if live(k):
                    for q in range(quads):
                        last = nc.tensor.transpose(bank(7)[:, 256 + PARTS * q:256 + PARTS * q + PARTS],
                                                   kpq[:, 1, 4 * q:4 * q + 4, :].rearrange("p t f -> p (t f)"), ident[:])
                    last.then_inc(s["qt"], 1)
                if live(m):
                    matmuls(m, 0)
                if live(k):
                    pe.wait_ge(s["kvs"], k + 1)
                    nc.tensor.matmul(KP, kvT[:].rearrange("p r f -> p (r f)"), projw1[:], start=True, stop=True).then_inc(s["kp"], 1)
                if live(l):
                    if live(m):
                        pe.wait_ge(s["tback"], nt * (m + 1))
                    nc.tensor.matmul(bank(0, half), w1[:], yT[:].rearrange("p t c -> p (t c)"), start=True, stop=True).then_inc(s["m1"], 1)
                if live(m) and quads == 2:
                    matmuls(m, 1)
                if live(k):
                    pe.wait_ge(s["bd"], k + 1)
                    pe.wait_ge(s["rq"], k + 1)
                    if live(m) and first:
                        pe.wait_ge(s["rem"], m + 1)
                    for q in range(quads):
                        last = nc.tensor.matmul(NUM[q].rearrange("p t c -> p (t c)"), RQ[:, 256 + PARTS * q:256 + PARTS * q + PARTS],
                                                BD[:].rearrange("p t c -> p (t c)"), start=True, stop=True)
                        last.then_inc(s["num"], 1)
                if live(l):
                    pe.wait_ge(s["gelu"], l + 1)
                    for j in range(tiles // 2):
                        last = nc.tensor.matmul(bank(1)[:, PARTS * j:PARTS * j + PARTS], G[:, j, :], w2[:], start=True, stop=True)
                    last.then_inc(s["m2"], 1)

            schedule(pe, body)


DIM, SEQ, HALF = 192, 65, 96
TOKENS = IMAGES * SEQ


def project(nc, src, dst, w, b, cls):
    steps, dim, taps = IMAGES // 2, 576, 9
    ktiles = [(128 * k, 128) for k in range(4)] + [(512, 65)]
    with ExitStack() as ctx:
        st = Stage(nc, ctx, "proj")
        ps = st.psum()
        ident = st.sbuf("ident", [PARTS, PARTS])
        W = st.sbuf("W", [PARTS, 5, DIM])
        X = [st.sbuf(f"X{p}", [PARTS, dim + 1]) for p in range(2)]
        XT = st.sbuf("XT", [PARTS, 5, PARTS])
        O = [st.sbuf(f"O{p}", [PARTS, DIM]) for p in range(2)]
        s_w, s_id, s_ones, s_cls = st.sem("w"), st.sem("id"), st.sem("ones"), st.sem("cls")
        s_in = [st.sem(f"in{p}") for p in range(2)]
        s_out = [st.sem(f"out{p}") for p in range(2)]
        s_t, s_ts, s_t5, s_mm, s_o = st.sem("t"), st.sem("ts"), st.sem("t5"), st.sem("mm"), st.sem("o")
        block = ctx.enter_context(nc.Block())

        @block.sync
        def _(sp):
            sp.dma_start(dram(dst, 0, [(SEQ * DIM, IMAGES), (1, DIM)]), dram(cls, 0, [(0, IMAGES), (1, DIM)])).then_inc(s_cls, 16)
            for tap in range(taps):
                p0 = EMB * (tap % 2)
                sp.dma_start(W[p0:p0 + EMB, tap // 2, :], dram(w, tap * DIM, [(taps * DIM, EMB), (1, DIM)])).then_inc(s_w, 16)
            sp.dma_start(W[EMB:EMB + 1, 4, :], dram(b, 0, [(DIM, 1), (1, DIM)])).then_inc(s_w, 16)

            def load(i):
                for im in range(2):
                    for ky in range(3):
                        sp.dma_start(X[i % 2][EMB * im:EMB * im + EMB, 192 * ky:192 * ky + 192],
                                     dram(src, (2 * i + im) * (17 * 17 * EMB) + ky * 17 * EMB,
                                          [(2 * 17 * EMB, 8), (2 * EMB, 8), (1, 3 * EMB)])).then_inc(s_in[i % 2], 16)

            load(0)
            load(1)
            for i in range(steps):
                sp.wait_ge(s_o, i + 1)
                for im in range(2):
                    sp.dma_start(dram(dst, ((2 * i + im) * SEQ + 1) * DIM, [(DIM, EMB), (1, DIM)]),
                                 O[i % 2][EMB * im:EMB * im + EMB, :]).then_inc(s_out[i % 2], 16)
                if i + 2 < steps:
                    load(i + 2)
            sp.wait_ge(s_cls, 16)
            for p in range(2):
                sp.wait_ge(s_out[p], 16 * steps)

        @block.gpsimd
        def _(pool):
            make_identity(nc, pool, ident, s_id)
            nc.gpsimd.memset(X[0][:, dim:], 1.0)
            nc.gpsimd.memset(X[1][:, dim:], 1.0).then_inc(s_ones, 1)

        @block.tensor
        def _(pe):
            pe.wait_ge(s_id, 2)
            pe.wait_ge(s_ones, 1)
            for i in range(steps + 1):
                if i < steps:
                    pe.wait_ge(s_in[i % 2], 96 * (i // 2 + 1))
                    wait(pe, s_ts, i)
                    wait(pe, s_t5, i)
                    for k, (c0, rows) in enumerate(ktiles):
                        nc.tensor.transpose(ps[0:rows, PARTS * k:PARTS * k + PARTS], X[i % 2][:, c0:c0 + rows], ident[:]).then_inc(s_t, 1)
                if i == 0:
                    pe.wait_ge(s_w, 160)
                if i < steps:
                    pe.wait_ge(s_ts, i + 1)
                    pe.wait_ge(s_t5, i + 1)
                    wait(pe, s_o, i - 1)
                    out = ps[:, (2 + i % 2) * BANK:(2 + i % 2) * BANK + DIM]
                    for k, (c0, rows) in enumerate(ktiles):
                        last = nc.tensor.matmul(out, XT[0:rows, k, :], W[0:rows, k, :], start=(k == 0), stop=(k == 4))
                    last.then_inc(s_mm, 1)

        @block.scalar
        def _(act):
            for i in range(steps):
                act.wait_ge(s_t, 5 * i + 4)
                nc.scalar.copy(XT[:, 0:4, :].rearrange("p k c -> p (k c)"), ps[:, 0:BANK]).then_inc(s_ts, 1)

        @block.vector
        def _(dve):
            for i in range(steps):
                dve.wait_ge(s_t, 5 * i + 5)
                nc.vector.tensor_copy(XT[0:EMB + 1, 4, :], ps[0:EMB + 1, BANK:BANK + PARTS]).then_inc(s_t5, 1)
                dve.wait_ge(s_mm, i + 1)
                wait(dve, s_out[i % 2], 32 * (i // 2))
                nc.vector.tensor_copy(O[i % 2][:], ps[:, (2 + i % 2) * BANK:(2 + i % 2) * BANK + DIM]).then_inc(s_o, 1)


def moments(nc, dve, stats, tmp, s, base):
    a = [stats[:, :, n] for n in range(6)]
    nc.vector.tensor_tensor(tmp[0], a[1], a[4], ALU.add).then_inc(s, 1)
    nc.vector.tensor_tensor(tmp[1], a[1], a[4], ALU.subtract).then_inc(s, 1)
    nc.vector.tensor_tensor(tmp[2], a[2], a[5], ALU.add).then_inc(s, 1)
    dve.wait_ge(s, base + 3)
    nc.vector.tensor_scalar(tmp[0], tmp[0], 0.5, None, ALU.mult).then_inc(s, 1)
    nc.vector.tensor_tensor(tmp[1], tmp[1], tmp[1], ALU.mult).then_inc(s, 1)
    nc.vector.tensor_scalar(tmp[2], tmp[2], 1.0 / DIM, EPS, ALU.mult, ALU.add).then_inc(s, 1)
    dve.wait_ge(s, base + 6)
    nc.vector.scalar_tensor_tensor(tmp[2], tmp[1], 0.25, tmp[2], ALU.mult, ALU.add).then_inc(s, 1)


HEADS = 12


def attention(nc, name, h_in, h_out, w, second):
    NB, HG = 2, 6
    with ExitStack() as ctx:
        st = Stage(nc, ctx, name)
        ps = st.psum()
        ident = st.sbuf("ident", [PARTS, PARTS])
        H = st.sbuf("H", [SEQ, IMAGES, DIM])
        WT = st.sbuf("WT", [HALF + 1, 2, 4, DIM])
        mask = st.sbuf("mask", [HALF, HG])
        stats = st.sbuf("stats", [SEQ, IMAGES, 6])
        tmp = st.sbuf("tmp", [SEQ, 3, IMAGES])
        mean, rstd = tmp[:, 0, :], st.sbuf("rstd", [SEQ, IMAGES])
        mhalf = st.sbuf("mhalf", [SEQ, IMAGES])
        xn = st.sbuf("xn", [SEQ, DIM + 1])
        on = st.sbuf("on", [SEQ, DIM + 1])
        v1 = st.sbuf("v1", [SEQ, HEADS, 17])

        with ExitStack() as ctx2:
            s2 = Stage(nc, ctx2, name + "_prep")
            raw = s2.sbuf("raw", [HALF, 4, 2, DIM])
            bpad = s2.sbuf("bpad", [HALF, 2, HALF + 1]) if second else None
            g = s2.sbuf("g", [HALF, 2]) if second else None
            s_h, s_w, s_id, s_mask, s_st, s_mo, s_pow, s_t, s_ts, s_b, s_c, s_u = (
                s2.sem(n) for n in ("h", "w", "id", "mask", "st", "mo", "pow", "t", "ts", "b", "c", "u"))
            rounds = 2 if second else 1
            block = ctx2.enter_context(nc.Block())

            @block.sync
            def _(sp):
                sp.dma_start(H[:], dram(h_in, 0, [(DIM, SEQ), (SEQ * DIM, IMAGES), (1, DIM)])).then_inc(s_h, 16)
                for m in range(4):
                    sp.dma_start(raw[:, m, :, :], dram(w["w"]["qkvo"[m]][0], w["w"]["qkvo"[m]][1] * DIM,
                                                       [(DIM, HALF), (HALF * DIM, 2), (1, DIM)])).then_inc(s_w, 16)
                n = 4
                for m in range(4):
                    if not second or m == 3:
                        sp.dma_start(WT[HALF:HALF + 1, 1, m, :], dram(w["b"]["qkvo"[m]], 0, [(DIM, 1), (1, DIM)])).then_inc(s_w, 16)
                        n += 1
                if second:
                    with nc.allow_non_contiguous_dma(reason="columns of the norm's gain and bias"):
                        sp.wait_ge(s_c, 1)
                        for kb in range(2):
                            sp.dma_start(bpad[:, kb, HALF:], dram(w["lnb"], HALF * kb, [(1, HALF), (1, 1)])).then_inc(s_w, 16)
                            sp.dma_start(g[:, kb:kb + 1], dram(w["lng"], HALF * kb, [(1, HALF), (1, 1)])).then_inc(s_w, 16)
                    n += 4
                sp.wait_ge(s_w, 16 * n)
                sp.sem_inc(s_b, 1)

            @block.gpsimd
            def _(pool):
                make_identity(nc, pool, ident, s_id)
                nc.gpsimd.memset(mask[:], 1.0).then_inc(s_mask, 1)
                pool.wait_ge(s_mask, 1)
                nc.gpsimd.affine_select(out=mask[:], in_=mask[:], compare_op=ALU.is_ge, fill=0.0, base=0,
                                        pattern=[[-16, HG]], channel_multiplier=1).then_inc(s_mask, 1)
                pool.wait_ge(s_mask, 2)
                nc.gpsimd.affine_select(out=mask[:], in_=mask[:], compare_op=ALU.is_ge, fill=0.0, base=15,
                                        pattern=[[16, HG]], channel_multiplier=-1).then_inc(s_mask, 1)
                nc.gpsimd.memset(xn[:, DIM:], 1.0)
                nc.gpsimd.memset(on[:, DIM:], 1.0)
                nc.gpsimd.memset(v1[:, :, 16:], 1.0)
                nc.gpsimd.memset(mhalf[:], -0.5).then_inc(s_mask, 1)
                pool.wait_ge(s_mask, 4)
                for r in range(rounds):
                    pool.wait_ge(s_mo, 7 * (r + 1))
                    nc.gpsimd.tensor_tensor(rstd[:], tmp[:, 2, :], mhalf[:], ALU.pow).then_inc(s_pow, 1)

            @block.vector
            def _(dve):
                if second:
                    nc.vector.memset(bpad[:], 0.0).then_inc(s_c, 1)
                dve.wait_ge(s_h, 16)
                for r in range(rounds):
                    with dve.Fori(0, IMAGES) as i:
                        nc.vector.bn_stats(stats[:, bass.ds(i, 1), :].rearrange("p a b -> p (a b)"), H[:, bass.ds(i, 1), :].rearrange("p a b -> p (a b)")).then_inc(s_st, 1)
                    dve.wait_ge(s_st, IMAGES * (r + 1))
                    moments(nc, dve, stats[:], [tmp[:, n, :] for n in range(3)], s_mo, 7 * r)
                    if second and r == 0:
                        dve.wait_ge(s_pow, 1)
                        with dve.Fori(0, IMAGES) as i:
                            row = H[:, bass.ds(i, 1), :].rearrange("p a b -> p (a b)")
                            nc.vector.tensor_scalar(row, row, mean[:, bass.ds(i, 1)], rstd[:, bass.ds(i, 1)], ALU.subtract, ALU.mult).then_inc(s_u, 1)
                        dve.wait_ge(s_u, IMAGES)
                for m in range(4):
                    dve.wait_ge(s_t, m + 1)
                    nc.vector.tensor_copy(WT[0:HALF, :, m, :].rearrange("p k (e c) -> p k e c", e=2),
                                          ps[0:HALF, m * BANK:m * BANK + 384].rearrange("p (k e c) -> p k e c", k=2, e=2)).then_inc(s_ts, 1)
                if second:
                    dve.wait_ge(s_t, 5)
                    for m in range(3):
                        nc.vector.tensor_copy(WT[HALF:HALF + 1, 1, m, :], ps[HALF:HALF + 1, (4 + m) * BANK:(4 + m) * BANK + DIM])
                    for kb in range(2):
                        nc.vector.tensor_scalar(WT[0:HALF, kb, 0:3, :], WT[0:HALF, kb, 0:3, :], g[:, kb:kb + 1], None, ALU.mult)

            @block.tensor
            def _(pe):
                pe.wait_ge(s_id, 2)
                pe.wait_ge(s_b, 1)
                for m in range(4):
                    for kb in range(2):
                        for eb in range(2):
                            c = m * BANK + (2 * kb + eb) * HALF
                            last = nc.tensor.transpose(ps[0:HALF, c:c + HALF], raw[:, m, eb, HALF * kb:HALF * kb + HALF], ident[0:HALF, 0:HALF])
                    last.then_inc(s_t, 1)
                if second:
                    pe.wait_ge(s_ts, 4)
                    for m in range(3):
                        for kb in range(2):
                            last = nc.tensor.matmul(ps[0:HALF + 1, (4 + m) * BANK:(4 + m) * BANK + DIM], bpad[:, kb, :],
                                                    WT[0:HALF, kb, m, :], start=(kb == 0), stop=(kb == 1))
                    last.then_inc(s_t, 1)

        xT = st.sbuf("xT", [HALF + 1, 2, SEQ])
        oT = st.sbuf("oT", [HALF + 1, 2, SEQ])
        qT = st.sbuf("qT", [HALF, 2, SEQ])
        kbd = st.sbuf("kbd", [HALF, 2, HG, SEQ])
        mx = st.sbuf("mx", [SEQ, 2, HG])
        S = st.sbuf("S", [SEQ, 2, HG, SEQ])
        P = st.sbuf("P", [SEQ, HEADS, SEQ])
        pT = st.sbuf("pT", [SEQ, HEADS, SEQ])
        rs = st.sbuf("rs", [SEQ, HEADS])
        names = ("norm", "xt", "xts", "qkv", "qs", "vs", "kbd", "sc", "mx", "sub", "exp", "pt", "pts", "av", "rs", "on", "ot",
                 "ots", "pr", "res", "out")
        s = {n: st.sem(n) for n in names}
        bXT = ps[0:HALF + 1, 0:2 * SEQ]
        bQ = ps[0:HALF, BANK:BANK + 2 * SEQ]
        bV = ps[0:SEQ, BANK + 256:BANK + 256 + DIM]
        bK = ps[0:HALF, 2 * BANK:2 * BANK + 2 * SEQ]
        bS = ps[0:SEQ, 3 * BANK:5 * BANK].rearrange("p (g c) -> p g c", g=2)[:, :, 0:HG * SEQ].rearrange("p g (h k) -> p g h k", h=HG)
        bP = ps[0:SEQ, 5 * BANK:7 * BANK].rearrange("p (g c) -> p g c", g=2)
        bA = ps[0:SEQ, 7 * BANK:7 * BANK + HEADS * 17].rearrange("p (h c) -> p h c", c=17)
        bO = ps[0:SEQ, 7 * BANK + 256:7 * BANK + 256 + DIM]

        def live(i):
            return 0 <= i < IMAGES if isinstance(i, int) else True

        def schedule(eng, body):
            for t in range(5):
                body(t)
            with eng.Fori(5, IMAGES) as t:
                body(t)
            for t in range(IMAGES, IMAGES + 3):
                body(t)

        block = ctx.enter_context(nc.Block())

        @block.vector
        def _(dve):
            def body(t):
                m, k, l = t - 1, t - 2, t - 3
                if live(l):
                    dve.wait_ge(s["pr"], l + 1)
                    row = H[:, bass.ds(l, 1), :].rearrange("p a b -> p (a b)")
                    nc.vector.tensor_tensor(row, bO, row, ALU.add).then_inc(s["res"], 1)
                if live(m):
                    dve.wait_ge(s["qkv"], m + 1)
                    wait(dve, s["sc"], m)
                    for g_ in range(2):
                        last = nc.vector.tensor_tensor(kbd[:, g_, :, :], spread(bK[:, SEQ * g_:SEQ * g_ + SEQ], 1, HG),
                                                       spread(mask[:], 2, SEQ), ALU.mult)
                    last.then_inc(s["kbd"], 1)
                if live(k):
                    dve.wait_ge(s["av"], k + 1)
                    nc.vector.reciprocal(rs[:], bA[:, :, 16]).then_inc(s["rs"], 1)
                    dve.wait_ge(s["rs"], k + 1)
                    wait(dve, s["ot"], k)
                    nc.vector.tensor_tensor(on[:, 0:DIM].rearrange("p (h c) -> p h c", c=16), bA[:, :, 0:16],
                                            spread(rs[:], 2, 16), ALU.mult).then_inc(s["on"], 1)
                if live(m):
                    dve.wait_ge(s["sc"], m + 1)
                    nc.vector.reduce_max(mx[:], bS, axis=AX_X).then_inc(s["mx"], 1)
                    dve.wait_ge(s["mx"], m + 1)
                    wait(dve, s["exp"], m)
                    nc.vector.tensor_tensor(S[:], bS, spread(mx[:], 3, SEQ), ALU.subtract).then_inc(s["sub"], 1)
                if live(t):
                    wait(dve, s["xt"], t)
                    row = H[:, bass.ds(t, 1), :].rearrange("p a b -> p (a b)")
                    nc.vector.tensor_scalar(xn[:, 0:DIM], row, mean[:, bass.ds(t, 1)], rstd[:, bass.ds(t, 1)],
                                            ALU.subtract, ALU.mult).then_inc(s["norm"], 1)

            schedule(dve, body)

        @block.scalar
        def _(act):
            def body(t):
                m, k = t - 1, t - 2
                if live(m):
                    act.wait_ge(s["xt"], m + 1)
                    nc.scalar.copy(xT[:].rearrange("p k c -> p (k c)"), bXT).then_inc(s["xts"], 1)
                if live(k):
                    act.wait_ge(s["pt"], k + 1)
                    nc.scalar.copy(pT[:].rearrange("p (g h) k -> p g (h k)", g=2), bP[:, :, 0:HG * SEQ]).then_inc(s["pts"], 1)
                if live(m):
                    act.wait_ge(s["qkv"], m + 1)
                    nc.scalar.copy(qT[:].rearrange("p k c -> p (k c)"), bQ).then_inc(s["qs"], 1)
                    wait(act, s["av"], m)
                    nc.scalar.copy(v1[:, :, 0:16], bV.rearrange("p (h c) -> p h c", c=16)).then_inc(s["vs"], 1)
                if live(k):
                    act.wait_ge(s["ot"], k + 1)
                    nc.scalar.copy(oT[:].rearrange("p k c -> p (k c)"), bXT).then_inc(s["ots"], 1)
                if live(m):
                    act.wait_ge(s["sub"], m + 1)
                    wait(act, s["pt"], m)
                    nc.scalar.activation(P[:].rearrange("p h k -> p (h k)"), S[:].rearrange("p g h k -> p (g h k)"), ACT.Exp,
                                         scale=0.25).then_inc(s["exp"], 1)

            schedule(act, body)

        @block.tensor
        def _(pe):
            def body(t):
                m, k, l = t - 1, t - 2, t - 3
                if live(l):
                    pe.wait_ge(s["ots"], l + 1)
                    for kb in range(2):
                        rows = HALF + kb
                        last = nc.tensor.matmul(bO, oT[0:rows, kb, :], WT[0:rows, kb, 3, :], start=(kb == 0), stop=(kb == 1))
                    last.then_inc(s["pr"], 1)
                if live(m):
                    pe.wait_ge(s["norm"], m + 1)
                    for kb in range(2):
                        last = nc.tensor.transpose(bXT[:, SEQ * kb:SEQ * kb + SEQ], xn[:, HALF * kb:HALF * kb + HALF + 1], ident[0:SEQ, 0:SEQ])
                    last.then_inc(s["xt"], 1)
                if live(k):
                    pe.wait_ge(s["exp"], k + 1)
                    wait(pe, s["pts"], k)
                    for h in range(HEADS):
                        c = SEQ * (h % HG)
                        last = nc.tensor.transpose(bP[:, h // HG, c:c + SEQ], P[:, h, :], ident[0:SEQ, 0:SEQ])
                    last.then_inc(s["pt"], 1)
                if live(m):
                    pe.wait_ge(s["xts"], m + 1)
                    wait(pe, s["kbd"], m)
                    wait(pe, s["vs"], m)
                    for mat, out in ((0, bQ), (1, bK)):
                        for g_ in range(2):
                            for kb in range(2):
                                rows = HALF + kb
                                nc.tensor.matmul(out[:, SEQ * g_:SEQ * g_ + SEQ], WT[0:rows, kb, mat, HALF * g_:HALF * g_ + HALF],
                                                 xT[0:rows, kb, :], start=(kb == 0), stop=(kb == 1))
                    for kb in range(2):
                        rows = HALF + kb
                        last = nc.tensor.matmul(bV, xT[0:rows, kb, :], WT[0:rows, kb, 2, :], start=(kb == 0), stop=(kb == 1))
                    last.then_inc(s["qkv"], 1)
                if live(k):
                    pe.wait_ge(s["pts"], k + 1)
                    if live(l):
                        pe.wait_ge(s["res"], l + 1)
                    pe.wait_ge(s["vs"], k + 1)
                    for h in range(HEADS):
                        last = nc.tensor.matmul(bA[:, h, :], pT[:, h, :], v1[:, h, :], start=True, stop=True)
                    last.then_inc(s["av"], 1)
                if live(m):
                    pe.wait_ge(s["kbd"], m + 1)
                    pe.wait_ge(s["qs"], m + 1)
                    wait(pe, s["sub"], m)
                    for g_ in range(2):
                        last = nc.tensor.matmul(bS[:, g_, :, :].rearrange("p h k -> p (h k)"), qT[:, g_, :],
                                                kbd[:, g_, :, :].rearrange("p h k -> p (h k)"), start=True, stop=True)
                    last.then_inc(s["sc"], 1)
                if live(k):
                    pe.wait_ge(s["on"], k + 1)
                    for kb in range(2):
                        last = nc.tensor.transpose(bXT[:, SEQ * kb:SEQ * kb + SEQ], on[:, HALF * kb:HALF * kb + HALF + 1], ident[0:SEQ, 0:SEQ])
                    last.then_inc(s["ot"], 1)

            schedule(pe, body)

        @block.sync
        def _(sp):
            sp.wait_ge(s["res"], IMAGES)
            sp.dma_start(dram(h_out, 0, [(DIM, SEQ), (SEQ * DIM, IMAGES), (1, DIM)]), H[:]).then_inc(s["out"], 16)
            sp.wait_ge(s["out"], 16)


TILE, NTILE = 104, 20
CHUNK, NCHUNK, LANES = 64, 3, TOKENS // 2
STATE = 16


def normed_columns(nc, name, src, rows, xT, xn_keep=None, affine=None):
    with ExitStack() as ctx:
        st = Stage(nc, ctx, name)
        ps = st.psum()
        ident = st.sbuf("ident", [PARTS, PARTS])
        stats = st.sbuf("stats", [TILE, NTILE, 6])
        tmp = st.sbuf("tmp", [TILE, 3, NTILE])
        rstd = st.sbuf("rstd", [TILE, NTILE])
        mhalf = st.sbuf("mhalf", [TILE, NTILE])
        xn = xn_keep if xn_keep is not None else st.sbuf("xn", [TILE, NTILE, DIM])
        gb = st.sbuf("gb", [HALF, 2, 2])
        s_h, s_g, s_id, s_c, s_st, s_mo, s_pow, s_n, s_t, s_e = (
            st.sem(n) for n in ("h", "g", "id", "c", "st", "mo", "pow", "n", "t", "e"))
        per = 4
        groups = NTILE // per
        block = ctx.enter_context(nc.Block())

        @block.sync
        def _(sp):
            sp.dma_start(rows[:], dram(src, 0, [(DIM, TILE), (TILE * DIM, NTILE), (1, DIM)])).then_inc(s_h, 16)
            if affine:
                with nc.allow_non_contiguous_dma(reason="columns of the norm's gain and bias"):
                    for n in range(2):
                        for kb in range(2):
                            sp.dma_start(gb[:, n, kb:kb + 1], dram(affine[n], HALF * kb, [(1, HALF), (1, 1)])).then_inc(s_g, 16)

        @block.gpsimd
        def _(pool):
            make_identity(nc, pool, ident, s_id)
            nc.gpsimd.memset(mhalf[:], -0.5).then_inc(s_c, 1)
            pool.wait_ge(s_c, 1)
            pool.wait_ge(s_mo, 7)
            nc.gpsimd.tensor_tensor(rstd[:], tmp[:, 2, :], mhalf[:], ALU.pow).then_inc(s_pow, 1)

        @block.vector
        def _(dve):
            nc.vector.memset(xT[HALF:HALF + 1, :, :], 1.0)
            dve.wait_ge(s_h, 16)
            for i in range(NTILE):
                nc.vector.bn_stats(stats[:, i, :], rows[:, i, :]).then_inc(s_st, 1)
            dve.wait_ge(s_st, NTILE)
            moments(nc, dve, stats[:], [tmp[:, n, :] for n in range(3)], s_mo, 0)
            dve.wait_ge(s_pow, 1)
            for i in range(NTILE):
                nc.vector.tensor_scalar(xn[:, i, :], rows[:, i, :], tmp[:, 0, i:i + 1], rstd[:, i:i + 1], ALU.subtract, ALU.mult).then_inc(s_n, 1)

        @block.tensor
        def _(pe):
            pe.wait_ge(s_id, 2)
            for g in range(groups):
                for kb in range(2):
                    n = 2 * g + kb
                    wait(pe, s_e, n - 3)
                    for j in range(per):
                        tile = per * g + j
                        pe.wait_ge(s_n, tile + 1)
                        c = (n % 4) * BANK + TILE * j
                        last = nc.tensor.transpose(ps[0:HALF, c:c + TILE], xn[:, tile, HALF * kb:HALF * kb + HALF], ident[0:TILE, 0:TILE])
                    last.then_inc(s_t, 1)

        @block.scalar
        def _(act):
            if affine:
                act.wait_ge(s_g, 64)
            for g in range(groups):
                for kb in range(2):
                    n = 2 * g + kb
                    act.wait_ge(s_t, n + 1)
                    out = xT[0:HALF, kb, per * TILE * g:per * TILE * (g + 1)]
                    got = ps[0:HALF, (n % 4) * BANK:(n % 4) * BANK + per * TILE]
                    if affine:
                        nc.scalar.activation(out, got, ACT.Identity, scale=gb[:, 0, kb:kb + 1], bias=gb[:, 1, kb:kb + 1]).then_inc(s_e, 1)
                    else:
                        nc.scalar.copy(out, got).then_inc(s_e, 1)


def state_space(nc, name, h_in, h_out, abc, w):
    GROUP = 4 * SEQ
    groups = TOKENS // GROUP
    NL1 = 11
    with ExitStack() as ctx:
        st = Stage(nc, ctx, name)
        rows = st.sbuf("rows", [TILE, NTILE, DIM])
        delta = st.sbuf("delta", [PARTS, NCHUNK, LANES])
        u = st.sbuf("u", [PARTS, NCHUNK, LANES])
        dt = st.sbuf("dt", [PARTS, NCHUNK])
        mdt = st.sbuf("mdt", [PARTS, NCHUNK])
        ident = st.sbuf("ident", [PARTS, PARTS])
        diag = st.sbuf("diag", [PARTS, NCHUNK, PARTS])
        with ExitStack() as ctx2:
            s2 = Stage(nc, ctx2, name + "_mlp")
            xT = s2.sbuf("xT", [HALF + 1, 2, TOKENS])
            W1 = s2.sbuf("W1", [HALF + 1, 2, 1344])
            W2 = s2.sbuf("W2", [PARTS, 9, HALF])
            W2d = s2.sbuf("W2d", [HALF, 2, DIM])
            b2 = s2.sbuf("b2", [HALF, 1])
            b2d = s2.sbuf("b2d", [PARTS, NCHUNK])
            Dc = s2.sbuf("D", [PARTS, NCHUNK])
            ldt = s2.sbuf("ldt", [PARTS, NCHUNK])
            hid = [s2.sbuf(f"hid{p}", [PARTS, NL1, GROUP]) for p in range(2)]
            ABC = s2.sbuf("ABC", [HALF, TOKENS])
            normed_columns(nc, name + "_norm", h_in, rows, xT)
            ps = s2.psum()
            s_w, s_z, s_id, s_l1, s_act, s_l2, s_e2, s_u, s_abc, s_dt, s_dg, s_c = (
                s2.sem(n) for n in ("w", "z", "id", "l1", "act", "l2", "e2", "u", "abc", "dt", "dg", "c"))
            block = ctx2.enter_context(nc.Block())
            NB2 = 6
            wload = [0]

            @block.sync
            def _(sp):
                ctx2.enter_context(nc.allow_non_contiguous_dma(reason="columns of biases"))
                n = 0
                sp.wait_ge(s_z, 1)
                c = 0
                for m in "ABCd":
                    wide = DIM if m == "d" else 2 * DIM
                    sp.dma_start(W1[0:HALF, :, c:c + wide], dram(w[m + "_w1"], 0, [(wide, HALF), (HALF * wide, 2), (1, wide)])).then_inc(s_w, 16)
                    sp.dma_start(W1[HALF:HALF + 1, 1, c:c + wide], dram(w[m + "_b1"], 0, [(wide, 1), (1, wide)])).then_inc(s_w, 16)
                    c += wide
                    n += 2
                for i, m in enumerate("ABC"):
                    sp.dma_start(W2[:, 3 * i:3 * i + 3, 32 * i:32 * i + STATE], dram(w[m + "_w2"], 0, [(STATE, PARTS), (PARTS * STATE, 3), (1, STATE)])).then_inc(s_w, 16)
                    sp.dma_start(b2[32 * i:32 * i + STATE, :], dram(w[m + "_b2"], 0, [(1, STATE), (1, 1)])).then_inc(s_w, 16)
                    n += 2
                sp.dma_start(W2d[:], dram(w["d_w2"], 0, [(DIM, HALF), (HALF * DIM, 2), (1, DIM)])).then_inc(s_w, 16)
                n += 1
                for half in range(2):
                    p = slice(CHUNK * half, CHUNK * half + CHUNK)
                    for to, frm in ((b2d, "d_b2"), (Dc, "D_param"), (ldt, "log_dt")):
                        sp.dma_start(to[p, :].unsqueeze(2), dram(w[frm], 0, [(1, CHUNK), (CHUNK, NCHUNK), (1, 1)])).then_inc(s_w, 16)
                        n += 1
                for half in range(2):
                    for c in range(NCHUNK):
                        d = c * CHUNK
                        while d < (c + 1) * CHUNK:
                            kb, r = divmod(d, HALF)
                            k = min((c + 1) * CHUNK - d, HALF - r)
                            p0 = CHUNK * half + d - c * CHUNK
                            sp.dma_start(u[p0:p0 + k, c, :], xT[r:r + k, kb, LANES * half:LANES * half + LANES]).then_inc(s_u, 16)
                            d += k
                sp.wait_ge(s_w, 16 * n)
                sp.sem_inc(s_c, 1)
                sp.wait_ge(s_e2, NB2 * groups)
                for i in range(3):
                    sp.dma_start(dram(abc, i * STATE * TOKENS, [(TOKENS, STATE), (1, TOKENS)]), ABC[32 * i:32 * i + STATE, :]).then_inc(s_abc, 16)
                sp.wait_ge(s_abc, 48)
                sp.wait_ge(s_u, 16 * 8)

            @block.gpsimd
            def _(pool):
                nc.gpsimd.memset(W2[:], 0.0).then_inc(s_z, 1)
                make_identity(nc, pool, ident, s_id)

            @block.vector
            def _(dve):
                dve.wait_ge(s_dt, 1)
                nc.vector.tensor_scalar(mdt[:], dt[:], -1.0, None, ALU.mult)
                dve.wait_ge(s_id, 2)
                for c in range(NCHUNK):
                    nc.vector.tensor_scalar(diag[:, c, :], ident[:], Dc[:, c:c + 1], None, ALU.mult).then_inc(s_dg, 1)

            def l1(ft):
                return (PARTS * ft, PARTS) if ft < 9 else (9 * PARTS + HALF * (ft - 9), HALF)

            @block.tensor
            def _(pe):
                pe.wait_ge(s_c, 1)

                def layer2(g):
                    half = g // (groups // 2)
                    pe.wait_ge(s_act, NL1 * (g + 1))
                    wait(pe, s_e2, NB2 * g)
                    for ft in range(9):
                        last = nc.tensor.matmul(ps[0:HALF, 4 * BANK:4 * BANK + GROUP], W2[:, ft, :], hid[g % 2][:, ft, :],
                                                start=(ft == 0), stop=(ft == 8))
                    last.then_inc(s_l2, 1)
                    p = slice(CHUNK * half, CHUNK * half + CHUNK)
                    for c in range(NCHUNK):
                        for kb in range(2):
                            last = nc.tensor.matmul(ps[p, (5 + c) * BANK:(5 + c) * BANK + GROUP], W2d[:, kb, CHUNK * c:CHUNK * c + CHUNK],
                                                    hid[g % 2][0:HALF, 9 + kb, :], start=(kb == 0), stop=(kb == 1))
                        last.then_inc(s_l2, 1)

                for g in range(groups):
                    for ft in range(NL1):
                        c0, rows_ = l1(ft)
                        n = NL1 * g + ft
                        wait(pe, s_act, n - 3)
                        for kb in range(2):
                            k = HALF + kb
                            last = nc.tensor.matmul(ps[0:rows_, (n % 4) * BANK:(n % 4) * BANK + GROUP], W1[0:k, kb, c0:c0 + rows_],
                                                    xT[0:k, kb, GROUP * g:GROUP * g + GROUP], start=(kb == 0), stop=(kb == 1))
                        last.then_inc(s_l1, 1)
                    if g >= 1:
                        layer2(g - 1)
                layer2(groups - 1)

            @block.scalar
            def _(act):
                act.wait_ge(s_c, 1)
                nc.scalar.activation(dt[:], ldt[:], ACT.Exp).then_inc(s_dt, 1)

                def evacuate2(g):
                    half = g // (groups // 2)
                    cols = slice(GROUP * g, GROUP * g + GROUP)
                    act.wait_ge(s_l2, 4 * g + 1)
                    for i in range(3):
                        p = slice(32 * i, 32 * i + STATE)
                        nc.scalar.activation(ABC[p, cols], ps[p, 4 * BANK:4 * BANK + GROUP], ACT.Abs if i == 0 else ACT.Identity,
                                             bias=b2[p, 0:1]).then_inc(s_e2, 1)
                    p = slice(CHUNK * half, CHUNK * half + CHUNK)
                    here = slice(GROUP * (g % (groups // 2)), GROUP * (g % (groups // 2) + 1))
                    for c in range(NCHUNK):
                        act.wait_ge(s_l2, 4 * g + 2 + c)
                        nc.scalar.activation(delta[p, c, here], ps[p, (5 + c) * BANK:(5 + c) * BANK + GROUP], ACT.Identity,
                                             bias=b2d[p, c:c + 1]).then_inc(s_e2, 1)

                for g in range(groups):
                    for ft in range(NL1):
                        _, rows_ = l1(ft)
                        n = NL1 * g + ft
                        act.wait_ge(s_l1, n + 1)
                        if g >= 2 and ft == 0:
                            act.wait_ge(s_l2, 4 * (g - 1))
                        nc.scalar.activation(hid[g % 2][0:rows_, ft, :], ps[0:rows_, (n % 4) * BANK:(n % 4) * BANK + GROUP],
                                             ACT.Silu).then_inc(s_act, 1)
                    if g >= 1:
                        evacuate2(g - 1)
                evacuate2(groups - 1)
                act.wait_ge(s_e2, NB2 * groups)
                nc.scalar.activation(delta[:].rearrange("p c t -> p (c t)"), delta[:].rearrange("p c t -> p (c t)"), ACT.Sigmoid)

        with ExitStack() as ctx2:
            s2 = Stage(nc, ctx2, name + "_scan")
            ps = s2.psum()
            bc = [s2.sbuf(f"bc{p}", [PARTS, 3, LANES]) for p in range(2)]
            gain = s2.sbuf("gain", [PARTS, NCHUNK, LANES])
            dA = [s2.sbuf(f"dA{p}", [PARTS, LANES]) for p in range(2)]
            wb = [s2.sbuf(f"wb{p}", [PARTS, LANES]) for p in range(2)]
            coef = [s2.sbuf(f"coef{p}", [PARTS, LANES]) for p in range(2)]
            inp = [s2.sbuf(f"inp{p}", [PARTS, LANES]) for p in range(2)]
            S = [s2.sbuf(f"S{p}", [PARTS, LANES]) for p in range(2)]
            prod = [s2.sbuf(f"prod{p}", [PARTS, LANES]) for p in range(2)]
            s_bc = [s2.sem(f"bc{p}") for p in range(2)]
            s_g, s_d0, s_da, s_w, s_coef, s_inp, s_scan, s_prod, s_acc, s_ys, s_t, s_res, s_out, s_ld = (
                s2.sem(n) for n in ("g", "d0", "da", "w", "coef", "inp", "scan", "prod", "acc", "ys", "t", "res", "out", "ld"))
            yS = gain

            def pieces(c):
                at = c * LANES
                while at < (c + 1) * LANES:
                    to = min((c + 1) * LANES, (at // BANK + 1) * BANK)
                    yield at, to
                    at = to

            def schedule(eng, body, tail=0):
                for n in range(4):
                    body(n, n % 2)
                with eng.Fori(4, STATE, 2) as n:
                    body(n, 0)
                    body(n + 1, 1)

            block = ctx2.enter_context(nc.Block())

            @block.sync
            def _(sp):
                def body(n, p):
                    wait(sp, s_da, 3 * (n - 1))
                    wait(sp, s_w, 3 * (n - 1))
                    wait(sp, s_prod, 3 * (n - 1))
                    sp.sem_inc(s_ld, 1)
                    for i in range(3):
                        sp.dma_start(bc[p][:, i, :], dram(abc, (i * STATE + n) * TOKENS, [(LANES, 2), (0, CHUNK), (1, LANES)])).then_inc(s_bc[p], 16)

                schedule(sp, body)
                sp.wait_ge(s_res, 10)
                sp.dma_start(dram(h_out, 0, [(DIM, TILE), (TILE * DIM, NTILE), (1, DIM)]), rows[:]).then_inc(s_out, 16)
                sp.wait_ge(s_out, 16)

            def loaded(eng, n, p):
                eng.wait_ge(s_bc[p], 48 * (n - p + 2) // 2 if isinstance(n, int) else (n - p) * 24 + 48)

            @block.scalar
            def _(act):
                def body(n, p):
                    loaded(act, n, p)
                    for c in range(NCHUNK):
                        j = 3 * n + c
                        q = (3 * p + c) % 2
                        wait(act, s_inp, j - 1)
                        nc.scalar.activation(dA[q][:], bc[p][:, 0, :], ACT.Exp, scale=mdt[:, c:c + 1]).then_inc(s_da, 1)

                schedule(act, body)
                act.wait_ge(s_acc, 3 * STATE)
                for c in range(NCHUNK):
                    nc.scalar.copy(yS[:, c, :], ps[:, LANES * c:LANES * c + LANES]).then_inc(s_ys, 1)

            @block.gpsimd
            def _(pool):
                def prods(j, p, q):
                    pool.wait_ge(s_scan, j + 1)
                    wait(pool, s_acc, j - 1)
                    nc.gpsimd.tensor_tensor(prod[q][:], S[q][:], bc[p][:, 2, :], ALU.mult).then_inc(s_prod, 1)

                pool.wait_ge(s_g, 5)

                def body(n, p):
                    loaded(pool, n, p)
                    for c in range(NCHUNK):
                        j = 3 * n + c
                        q = (3 * p + c) % 2
                        wait(pool, s_inp, j - 1)
                        nc.gpsimd.tensor_tensor(wb[q][:], gain[:, c, :], bc[p][:, 1, :], ALU.mult).then_inc(s_w, 1)
                        if not isinstance(n, int) or j >= 1:
                            prods(j - 1, p if c else 1 - p, 1 - q)

                schedule(pool, body)
                prods(3 * STATE - 1, 1, (3 * STATE - 1) % 2)

            @block.vector
            def _(dve):
                nc.vector.tensor_scalar(gain[:], delta[:], -1.0, 1.0, ALU.mult, ALU.add).then_inc(s_g, 1)
                dve.wait_ge(s_g, 1)
                nc.vector.tensor_tensor(gain[:], gain[:], u[:], ALU.mult).then_inc(s_g, 1)
                dve.wait_ge(s_g, 2)
                for c in range(NCHUNK):
                    nc.vector.tensor_scalar(gain[:, c, :], gain[:, c, :], dt[:, c:c + 1], None, ALU.mult).then_inc(s_g, 1)
                nc.vector.memset(delta[:].rearrange("p c (b l) -> p (c b) l", l=SEQ)[:, :, 0:1], 0.0).then_inc(s_d0, 1)
                dve.wait_ge(s_d0, 1)

                def body(n, p):
                    for c in range(NCHUNK):
                        j = 3 * n + c
                        q = (3 * p + c) % 2
                        dve.wait_ge(s_da, j + 1)
                        wait(dve, s_scan, j - 1)
                        nc.vector.tensor_tensor(coef[q][:], delta[:, c, :], dA[q][:], ALU.mult).then_inc(s_coef, 1)
                        dve.wait_ge(s_w, j + 1)
                        nc.vector.tensor_tensor(inp[q][:], wb[q][:], dA[q][:], ALU.mult).then_inc(s_inp, 1)
                        dve.wait_ge(s_coef, j + 1)
                        dve.wait_ge(s_inp, j + 1)
                        wait(dve, s_prod, j - 1)
                        nc.vector.tensor_tensor_scan(S[q][:], coef[q][:], inp[q][:], 0.0, ALU.mult, ALU.add).then_inc(s_scan, 1)

                schedule(dve, body)
                for t in range(10):
                    dve.wait_ge(s_t, t + 1)
                    out = rows[:, t::10, :].rearrange("p h (c d) -> p c h d", c=NCHUNK)
                    nc.vector.tensor_tensor(out, ps[0:TILE, (t % 8) * BANK:(t % 8) * BANK + 384].rearrange("p (c h d) -> p c h d", c=NCHUNK, h=2),
                                            out, ALU.add).then_inc(s_res, 1)

            @block.tensor
            def _(pe):
                begun = set()
                for c in range(NCHUNK):
                    for a, b in pieces(c):
                        nc.tensor.matmul(ps[:, a:b], diag[:, c, :], u[:, c, a - LANES * c:b - LANES * c], start=(a // BANK not in begun),
                                         stop=True, skip_group_check=True)
                        begun.add(a // BANK)

                def body(n, p):
                    for c in range(NCHUNK):
                        j = 3 * n + c
                        q = (3 * p + c) % 2
                        pe.wait_ge(s_prod, j + 1)
                        for a, b in pieces(c):
                            last = nc.tensor.matmul(ps[:, a:b], ident[:], prod[q][:, a - LANES * c:b - LANES * c], start=False, stop=True,
                                                    skip_group_check=True)
                        last.then_inc(s_acc, 1)

                schedule(pe, body)
                pe.wait_ge(s_ys, 3)
                for t in range(10):
                    wait(pe, s_res, t - 7)
                    for c in range(NCHUNK):
                        last = nc.tensor.transpose(ps[0:TILE, (t % 8) * BANK + PARTS * c:(t % 8) * BANK + PARTS * c + PARTS],
                                                   yS[:, c, TILE * t:TILE * t + TILE], ident[:])
                    last.then_inc(s_t, 1)


EXPERTS = 8


def experts(nc, name, a_in, base, h_out, xs, ys, w, gated):
    slots = 1 if gated else 2
    ntiles = (slots * TOKENS + PARTS - 1) // PARTS + EXPERTS - 1
    ntiles += ntiles % 2
    hidden = 469 if gated else 768
    fts = [(c, min(PARTS, hidden - c)) for c in range(0, hidden, PARTS)]
    nft = len(fts)
    wide = 2 * hidden if gated else hidden
    cut = hidden if gated else hidden // 2
    with ExitStack() as ctx:
        st = Stage(nc, ctx, name)
        rows = st.sbuf("rows", [TILE, NTILE, DIM])
        pos = [st.sbuf(f"pos{k}", [TILE, NTILE], U32) for k in range(slots)]
        score = [st.sbuf(f"score{k}", [TILE, NTILE]) for k in range(slots)]
        texp = st.sbuf("texp", [1, ntiles], I32)
        ident = st.sbuf("ident", [PARTS, PARTS])

        with ExitStack() as ctx2:
            s2 = Stage(nc, ctx2, name + "_route")
            xT = s2.sbuf("xT", [HALF + 1, 2, TOKENS])
            xn = s2.sbuf("xn", [TILE, NTILE, DIM])
            normed_columns(nc, name + "_norm", a_in, rows, xT, xn, None if gated else (w["lng"], w["lnb"]))
            ps = s2.psum()
            zeros = s2.sbuf("zeros", [PARTS, 4 * DIM])
            graw = s2.sbuf("graw", [EXPERTS, DIM + 1])
            GT = s2.sbuf("GT", [HALF + 1, 2, EXPERTS])
            L = s2.sbuf("L", [TILE, NTILE, EXPERTS])
            best = [s2.sbuf(f"best{k}", [TILE, NTILE]) for k in range(slots)]
            OH = [s2.sbuf(f"OH{k}", [TILE, NTILE, EXPERTS]) for k in range(slots)]
            both = s2.sbuf("both", [TILE, NTILE, EXPERTS])
            key = s2.sbuf("key", [TILE, NTILE, EXPERTS])
            top = s2.sbuf("top", [TILE, NTILE])
            order_i, order = s2.sbuf("order_i", [TILE, EXPERTS], I32), s2.sbuf("order", [TILE, EXPERTS])
            NTH = TOKENS // PARTS + 1
            thr_i, thr = s2.sbuf("thr_i", [TILE, NTH], I32), s2.sbuf("thr", [TILE, NTH])
            tn_i, tn = s2.sbuf("tn_i", [1, ntiles], I32), s2.sbuf("tn", [1, ntiles])
            upper = s2.sbuf("upper", [TILE, TILE])
            ones = s2.sbuf("ones", [TILE, TILE])
            chain0 = s2.sbuf("chain0", [TILE, EXPERTS, NTILE])
            tot = s2.sbuf("tot", [TILE, EXPERTS, NTILE])
            incl = s2.sbuf("incl", [TILE, EXPERTS, NTILE])
            over = s2.sbuf("over", [TILE, EXPERTS, NTH])
            nt, ntin = s2.sbuf("nt", [TILE, EXPERTS]), s2.sbuf("ntin", [TILE, EXPERTS])
            start = s2.sbuf("start", [TILE, EXPERTS])
            place = s2.sbuf("place", [TILE, NTILE, EXPERTS])
            pf = s2.sbuf("pf", [TILE, NTILE])
            tge = s2.sbuf("tge", [1, ntiles, EXPERTS])
            te = s2.sbuf("te", [1, ntiles])
            s_g, s_fill, s_id, s_zero, s_gt, s_gts, s_lg, s_cst, s_v, s_oh, s_rank, s_pos, s_exp, s_sc, s_up = (
                s2.sem(n) for n in ("g", "fill", "id", "zero", "gt", "gts", "lg", "cst", "v", "oh", "rank", "pos", "exp", "sc", "up"))
            block = ctx2.enter_context(nc.Block())

            @block.sync
            def _(sp):
                with nc.allow_non_contiguous_dma(reason="eight biases"):
                    sp.dma_start(graw[:, 0:DIM], w["gate_w"]).then_inc(s_g, 16)
                    sp.dma_start(graw[:, DIM:], dram(w["gate_b"], 0, [(1, EXPERTS), (1, 1)])).then_inc(s_g, 16)
                sp.wait_ge(s_zero, 1)
                for n in range(0, ntiles, 4):
                    sp.dma_start(dram(xs, n * PARTS * DIM, [(4 * DIM, PARTS), (1, 4 * DIM)]), zeros[:]).then_inc(s_fill, 16)
                sp.wait_ge(s_fill, 16 * (ntiles // 4))

            @block.gpsimd
            def _(pool):
                nc.gpsimd.iota(order_i[:], pattern=[[-1, EXPERTS]], base=EXPERTS, channel_multiplier=0)
                nc.gpsimd.iota(thr_i[:], pattern=[[PARTS, NTH]], base=0, channel_multiplier=0)
                nc.gpsimd.iota(tn_i[:], pattern=[[1, ntiles]], base=0, channel_multiplier=0).then_inc(s_cst, 1)
                pool.wait_ge(s_cst, 1)
                nc.gpsimd.memset(upper[:], 1.0).then_inc(s_up, 1)
                nc.gpsimd.memset(ones[:], 1.0)
                pool.wait_ge(s_up, 1)
                nc.gpsimd.affine_select(out=upper[:], in_=upper[:], compare_op=ALU.is_gt, fill=0.0, base=0,
                                        pattern=[[1, TILE]], channel_multiplier=-1).then_inc(s_up, 1)
                make_identity(nc, pool, ident, s_id)
                pool.wait_ge(s_fill, 16 * (ntiles // 4))
                for k in range(slots):
                    pool.wait_ge(s_pos, k + 1)
                    for i in range(NTILE):
                        nc.gpsimd.indirect_dma_start(out=xs, out_offset=bass.IndirectOffsetOnAxis(ap=pos[k][:, i:i + 1], axis=0),
                                                     in_=xn[:, i, :], in_offset=None).then_inc(s_sc, 16)
                pool.wait_ge(s_sc, 16 * NTILE * slots)

            @block.tensor
            def _(pe):
                pe.wait_ge(s_id, 2)
                pe.wait_ge(s_g, 32)
                for kb in range(2):
                    last = nc.tensor.transpose(ps[0:HALF + kb, kb * EXPERTS:(kb + 1) * EXPERTS], graw[:, HALF * kb:HALF * kb + HALF + kb],
                                               ident[0:EXPERTS, 0:EXPERTS])
                last.then_inc(s_gt, 1)
                pe.wait_ge(s_gts, 1)
                for i in range(NTILE):
                    for kb in range(2):
                        last = nc.tensor.matmul(ps[0:TILE, BANK + EXPERTS * i:BANK + EXPERTS * i + EXPERTS],
                                                xT[0:HALF + kb, kb, TILE * i:TILE * i + TILE], GT[0:HALF + kb, kb, :], start=(kb == 0), stop=(kb == 1))
                last.then_inc(s_lg, 1)
                pe.wait_ge(s_oh, 1)
                pe.wait_ge(s_up, 2)
                flat = both[:].rearrange("p t e -> p (t e)")
                nc.tensor.matmul(ps[0:TILE, 2 * BANK:2 * BANK + NTILE * EXPERTS], upper[:], flat, start=True, stop=True)
                nc.tensor.matmul(ps[0:TILE, 3 * BANK:3 * BANK + NTILE * EXPERTS], ones[:], flat, start=True, stop=True).then_inc(s_rank, 1)

            @block.vector
            def _(dve):
                count = [0]

                def link(ins):
                    count[0] += 1
                    ins.then_inc(s_v, 1)
                    dve.wait_ge(s_v, count[0])

                nc.vector.memset(zeros[:], 0.0).then_inc(s_zero, 1)
                nc.vector.memset(chain0[:], 1.0)
                link(nc.vector.memset(start[:], 1.0))
                link(nc.vector.memset(chain0[:, :, 0:1], 0.0))
                dve.wait_ge(s_cst, 1)
                nc.vector.tensor_copy(order[:], order_i[:])
                nc.vector.tensor_copy(thr[:], thr_i[:])
                link(nc.vector.tensor_copy(tn[:], tn_i[:]))
                dve.wait_ge(s_gt, 1)
                nc.vector.tensor_copy(GT[0:HALF, 0, :], ps[0:HALF, 0:EXPERTS])
                nc.vector.tensor_copy(GT[:, 1, :], ps[0:HALF + 1, EXPERTS:2 * EXPERTS]).then_inc(s_gts, 1)
                dve.wait_ge(s_lg, 1)
                link(nc.vector.tensor_copy(L[:].rearrange("p t e -> p (t e)"), ps[0:TILE, BANK:BANK + NTILE * EXPERTS]))
                for k in range(slots):
                    link(nc.vector.reduce_max(best[k][:], L[:], axis=AX_X))
                    link(nc.vector.tensor_tensor(key[:], L[:], spread(best[k][:], 2, EXPERTS), ALU.is_equal))
                    link(nc.vector.tensor_tensor(key[:], key[:], spread(order[:], 1, NTILE), ALU.mult))
                    link(nc.vector.reduce_max(top[:], key[:], axis=AX_X))
                    link(nc.vector.tensor_tensor(OH[k][:], key[:], spread(top[:], 2, EXPERTS), ALU.is_equal))
                    if k + 1 < slots:
                        link(nc.vector.scalar_tensor_tensor(L[:].rearrange("p t e -> p (t e)"), OH[k][:].rearrange("p t e -> p (t e)"), -3.0e38,
                                                            L[:].rearrange("p t e -> p (t e)"), ALU.mult, ALU.add))
                if slots == 2:
                    nc.vector.tensor_tensor(both[:], OH[0][:], OH[1][:], ALU.add).then_inc(s_oh, 1)
                    link(nc.vector.tensor_tensor(score[1][:], best[1][:], best[0][:], ALU.subtract))
                else:
                    nc.vector.tensor_copy(both[:], OH[0][:]).then_inc(s_oh, 1)
                dve.wait_ge(s_rank, 1)
                link(nc.vector.tensor_copy(tot[:].rearrange("p e t -> p t e"), ps[0:TILE, 3 * BANK:3 * BANK + NTILE * EXPERTS].rearrange("p (t e) -> p t e", e=EXPERTS)))
                link(nc.vector.tensor_tensor_scan(incl[:].rearrange("p e t -> p (e t)"), chain0[:].rearrange("p e t -> p (e t)"),
                                                  tot[:].rearrange("p e t -> p (e t)"), 0.0, ALU.mult, ALU.add))
                link(nc.vector.tensor_tensor(over[:], spread(incl[:, :, NTILE - 1], 2, NTH), spread(thr[:], 1, EXPERTS), ALU.is_gt))
                link(nc.vector.reduce_sum(nt[:], over[:], axis=AX_X))
                link(nc.vector.tensor_tensor_scan(ntin[:], start[:], nt[:], 0.0, ALU.mult, ALU.add))
                link(nc.vector.tensor_tensor(start[:], ntin[:], nt[:], ALU.subtract))
                link(nc.vector.tensor_scalar(start[:], start[:], float(PARTS), None, ALU.mult))
                link(nc.vector.tensor_tensor(incl[:], incl[:], tot[:], ALU.subtract))
                link(nc.vector.tensor_tensor(place[:], spread(start[:], 1, NTILE), incl[:].rearrange("p e t -> p t e"), ALU.add))
                link(nc.vector.tensor_tensor(place[:], place[:], ps[0:TILE, 2 * BANK:2 * BANK + NTILE * EXPERTS].rearrange("p (t e) -> p t e", e=EXPERTS), ALU.add))
                for k in range(slots):
                    link(nc.vector.tensor_tensor(key[:], place[:], OH[k][:], ALU.mult))
                    link(nc.vector.reduce_sum(pf[:], key[:], axis=AX_X))
                    nc.vector.tensor_copy(pos[k][:], pf[:]).then_inc(s_pos, 1)
                    dve.wait_ge(s_pos, k + 1)
                link(nc.vector.tensor_tensor(tge[:], spread(tn[:], 2, EXPERTS), spread(ntin[0:1, :], 1, ntiles), ALU.is_ge))
                link(nc.vector.reduce_sum(te[:], tge[:], axis=AX_X))
                link(nc.vector.tensor_scalar(te[:], te[:], float(EXPERTS - 1), None, ALU.min))
                nc.vector.tensor_copy(texp[:], te[:])
                if slots == 2:
                    dve.wait_ge(s_exp, 1)
                    link(nc.vector.tensor_scalar(score[0][:], score[1][:], 1.0, None, ALU.add))
                    link(nc.vector.reciprocal(score[0][:], score[0][:]))
                    link(nc.vector.tensor_tensor(score[1][:], score[1][:], score[0][:], ALU.mult))

            @block.scalar
            def _(act):
                if slots == 2:
                    act.wait_ge(s_rank, 1)
                    act.wait_ge(s_oh, 1)
                    act.wait_ge(s_pos, 1)
                    nc.scalar.activation(score[1][:], score[1][:], ACT.Exp).then_inc(s_exp, 1)

        W1 = st.sbuf("W1", [HALF + 1, 2, EXPERTS, wide])
        W2 = st.sbuf("W2", [PARTS, nft, EXPERTS, DIM])
        B2 = None if gated else st.sbuf("B2", [1, EXPERTS, DIM])
        with ExitStack() as ctx2:
            s2 = Stage(nc, ctx2, name + "_turn")
            ps = s2.psum()
            parts1 = 2 if gated else 1
            raw1 = [s2.sbuf(f"raw1{p}", [PARTS, parts1, nft, DIM]) for p in range(2)]
            raw2 = [s2.sbuf(f"raw2{p}", [HALF, 2, hidden]) for p in range(2)]
            s_in = [s2.sem(f"in{p}") for p in range(2)]
            s_b, s_t, s_e, s_gate = s2.sem("b"), s2.sem("t"), s2.sem("e"), s2.sem("gate")
            whole = hidden // PARTS
            left = hidden - whole * PARTS
            jobs = []
            for part in range(parts1):
                for kb in range(2):
                    for f0 in range(0, nft, 4):
                        jobs.append((1, part, kb, fts[f0:f0 + 4]))
            for f0, (c0, k) in enumerate(fts):
                jobs.append((2, f0, 0, [(c0, k)]))
            njobs = len(jobs)
            nbanks = njobs // 2
            ndma = (parts1 * (2 if left else 1)) + 1

            def schedule(eng, body):
                for e in range(4):
                    body(e, e % 2)
                with eng.Fori(4, EXPERTS - 1, 2) as e:
                    body(e, 0)
                    body(e + 1, 1)

            block = ctx2.enter_context(nc.Block())

            @block.sync
            def _(sp):
                if not gated:
                    sp.dma_start(W1[HALF:HALF + 1, 1, :, :].rearrange("p e c -> p (e c)"), dram(w["b1"], 0, [(EXPERTS * hidden, 1), (1, EXPERTS * hidden)])).then_inc(s_b, 16)
                    sp.dma_start(B2[:].rearrange("p e c -> p (e c)"), dram(w["b2"], 0, [(EXPERTS * DIM, 1), (1, EXPERTS * DIM)])).then_inc(s_b, 16)

                def body(e, p):
                    wait(sp, s_t, njobs * (e - 1))
                    sp.sem_inc(s_gate, 1)
                    for part in range(parts1):
                        frm = w["w1"][part]
                        sp.dma_start(raw1[p][:, part, 0:whole, :], dram(frm, e * (hidden * DIM), [(DIM, PARTS), (PARTS * DIM, whole), (1, DIM)])).then_inc(s_in[p], 16)
                        if left:
                            sp.dma_start(raw1[p][0:left, part, whole, :], dram(frm, e * (hidden * DIM) + whole * PARTS * DIM, [(DIM, left), (1, DIM)])).then_inc(s_in[p], 16)
                    sp.dma_start(raw2[p][:], dram(w["w2"], e * (hidden * DIM), [(hidden, HALF), (HALF * hidden, 2), (1, hidden)])).then_inc(s_in[p], 16)

                schedule(sp, body)
                if not gated:
                    sp.wait_ge(s_b, 32)

            @block.tensor
            def _(pe):
                def body(e, p):
                    pe.wait_ge(s_in[p], 16 * ndma * (e - p + 2) // 2 if isinstance(e, int) else (e - p) * (8 * ndma) + 16 * ndma)
                    for n, (kind, a, kb, ts) in enumerate(jobs):
                        wait(pe, s_e, njobs * e + n - (nbanks - 1))
                        b = (n % nbanks) * BANK
                        if kind == 1:
                            for f, (c0, k) in enumerate(ts):
                                last = nc.tensor.transpose(ps[0:HALF, b + PARTS * f:b + PARTS * f + k],
                                                           raw1[p][0:k, a, c0 // PARTS, HALF * kb:HALF * kb + HALF], ident[0:k, 0:k])
                        else:
                            c0, k = ts[0]
                            for h in range(2):
                                last = nc.tensor.transpose(ps[0:k, b + HALF * h:b + HALF * h + HALF], raw2[p][:, h, c0:c0 + k], ident[0:HALF, 0:HALF])
                        last.then_inc(s_t, 1)

                schedule(pe, body)

            def evacuate(eng, mine, copy):
                def body(e, p):
                    for n, (kind, a, kb, ts) in enumerate(jobs):
                        if n % 2 != mine:
                            continue
                        eng.wait_ge(s_t, njobs * e + n + 1)
                        if n >= 1 or not isinstance(e, int) or e:
                            wait(eng, s_e, njobs * e + n)
                        b = (n % nbanks) * BANK
                        if kind == 1:
                            c0 = a * hidden + ts[0][0]
                            k = sum(x[1] for x in ts)
                            to = W1[0:HALF, kb, bass.ds(e, 1), c0:c0 + k].rearrange("p a c -> p (a c)")
                            copy(to, ps[0:HALF, b:b + k]).then_inc(s_e, 1)
                        else:
                            k = ts[0][1]
                            to = W2[0:k, a, bass.ds(e, 1), :].rearrange("p a c -> p (a c)")
                            copy(to, ps[0:k, b:b + DIM]).then_inc(s_e, 1)

                schedule(eng, body)

            @block.vector
            def _(dve):
                evacuate(dve, 0, lambda o, i: nc.vector.tensor_copy(o, i))

            @block.scalar
            def _(act):
                evacuate(act, 1, lambda o, i: nc.scalar.copy(o, i))

        with ExitStack() as ctx2:
            s2 = Stage(nc, ctx2, name + "_tiles")
            ps = s2.psum()
            X = [s2.sbuf(f"X{p}", [PARTS, DIM]) for p in range(2)]
            XT = s2.sbuf("XT", [HALF + 1, 2, PARTS])
            G = s2.sbuf("G", [PARTS, hidden])
            act_out = s2.sbuf("act_out", [PARTS, hidden]) if gated else G
            GT = s2.sbuf("GT", [PARTS, nft, PARTS])
            Y = [s2.sbuf(f"Y{p}", [PARTS, DIM]) for p in range(2)]
            one = s2.sbuf("one", [1, PARTS])
            gb = s2.sbuf("gb", [HALF, 2, 2])
            s_in = [s2.sem(f"in{p}") for p in range(2)]
            s_out = [s2.sem(f"out{p}") for p in range(2)]
            s_one, s_gb, s_xt, s_xts, s_l1, s_g1, s_g2, s_gt, s_gts, s_l2, s_y, s_gate = (
                s2.sem(n) for n in ("one", "gb", "xt", "xts", "l1", "g1", "g2", "gt", "gts", "l2", "y", "gate"))
            s_g = s_g2 if gated else s_g1
            gper = 1 if gated else 2

            def live(i):
                return 0 <= i < ntiles if isinstance(i, int) else True

            def schedule(eng, body):
                for t in range(4):
                    body(t, t % 2)
                with eng.Fori(4, ntiles - 1, 2) as t:
                    body(t, 0)
                    body(t + 1, 1)
                body(ntiles, 0)

            def paired(each, i, p):
                return each * (i - p + 2) // 2 if isinstance(i, int) else (i - p) * (each // 2) + each

            block = ctx2.enter_context(nc.Block())

            @block.sync
            def _(sp):
                if not gated:
                    with nc.allow_non_contiguous_dma(reason="columns of the norm's gain and bias"):
                        for n, m in enumerate(("lng", "lnb")):
                            for kb in range(2):
                                sp.dma_start(gb[:, n, kb:kb + 1], dram(w[m], HALF * kb, [(1, HALF), (1, 1)])).then_inc(s_gb, 16)

                def body(t, p):
                    if live(t):
                        wait(sp, s_xt, t - 1)
                        sp.sem_inc(s_gate, 1)
                        sp.dma_start(X[p][:], dram(xs, t * (PARTS * DIM), [(DIM, PARTS), (1, DIM)])).then_inc(s_in[p], 16)
                    if live(t - 1):
                        sp.wait_ge(s_y, t)
                        sp.sem_inc(s_gate, 1)
                        sp.dma_start(dram(ys, (t - 1) * (PARTS * DIM), [(DIM, PARTS), (1, DIM)]), Y[1 - p][:]).then_inc(s_out[1 - p], 16)

                schedule(sp, body)
                for p in range(2):
                    sp.wait_ge(s_out[p], 16 * ntiles // 2)

            @block.gpsimd
            def _(pool):
                nc.gpsimd.memset(one[:], 1.0).then_inc(s_one, 1)

            @block.tensor
            def _(pe):
                pe.wait_ge(s_one, 1)

                def body(t, p):
                    m = t - 1
                    if live(t):
                        pe.wait_ge(s_in[p], paired(16, t, p))
                        wait(pe, s_xts, t)
                        for kb in range(2):
                            last = nc.tensor.transpose(ps[0:HALF, PARTS * kb:PARTS * kb + PARTS], X[p][:, HALF * kb:HALF * kb + HALF], ident[:])
                        last.then_inc(s_xt, 1)
                    if live(m):
                        pe.wait_ge(s_g, gper * t)
                        wait(pe, s_gts, 2 * m)
                        for f, (c0, k) in enumerate(fts):
                            last = nc.tensor.transpose(ps[0:k, BANK + PARTS * f:BANK + PARTS * f + PARTS], G[:, c0:c0 + k], ident[:])
                        last.then_inc(s_gt, 1)
                    if live(t):
                        e = pe.value_load(texp[0:1, t:t + 1] if isinstance(t, int) else texp[0:1, bass.ds(t, 1)], min_val=0, max_val=EXPERTS - 1)
                        pe.wait_ge(s_xts, t + 1)
                        wait(pe, s_g1, 2 // (1 if not gated else 2) * t)
                        if gated:
                            wait(pe, s_g2, t)
                        for c in range(2):
                            for kb in range(2):
                                k = HALF if kb == 0 or gated else HALF + 1
                                last = nc.tensor.matmul(ps[:, (3 + c) * BANK:(3 + c) * BANK + cut], XT[0:k, kb, :],
                                                        W1[0:k, kb, bass.ds(e, 1), cut * c:cut * c + cut].rearrange("p a c -> p (a c)"),
                                                        start=(kb == 0), stop=(kb == 1))
                            last.then_inc(s_l1, 1)
                    if live(m):
                        e = pe.value_load(texp[0:1, m:m + 1] if isinstance(m, int) else texp[0:1, bass.ds(m, 1)], min_val=0, max_val=EXPERTS - 1)
                        pe.wait_ge(s_gts, 2 * t)
                        wait(pe, s_y, m)
                        out = ps[:, 5 * BANK:5 * BANK + DIM]
                        if not gated:
                            nc.tensor.matmul(out, one[:], B2[0:1, bass.ds(e, 1), :].rearrange("p a c -> p (a c)"), start=True, stop=False)
                        for f, (c0, k) in enumerate(fts):
                            last = nc.tensor.matmul(out, GT[0:k, f, :], W2[0:k, f, bass.ds(e, 1), :].rearrange("p a c -> p (a c)"),
                                                    start=(gated and f == 0), stop=(f == nft - 1))
                        last.then_inc(s_l2, 1)

                schedule(pe, body)

            @block.scalar
            def _(act):
                if not gated:
                    act.wait_ge(s_gb, 64)

                def body(t, p):
                    m = t - 1
                    if live(m):
                        act.wait_ge(s_gt, t)
                        wait(act, s_l2, m)
                        if nft > 4:
                            nc.scalar.copy(GT[:, 4:, :].rearrange("p f c -> p (f c)"), ps[:, 2 * BANK:2 * BANK + PARTS * (nft - 4)]).then_inc(s_gts, 1)
                    if live(t):
                        for c in range(2 if not gated else 1):
                            act.wait_ge(s_l1, 2 * t + c + 1)
                            if c == 0:
                                wait(act, s_gt if not gated else s_g2, t)
                            nc.scalar.activation(act_out[:, cut * c:cut * c + cut], ps[:, (3 + c) * BANK:(3 + c) * BANK + cut],
                                                 ACT.Silu if gated else ACT.Gelu).then_inc(s_g1, 1)

                schedule(act, body)

            @block.vector
            def _(dve):
                dve.wait_ge(s_one, 1)
                if not gated:
                    nc.vector.memset(XT[HALF:HALF + 1, :, :], 1.0)
                    dve.wait_ge(s_gb, 64)

                def body(t, p):
                    m = t - 1
                    if live(t):
                        dve.wait_ge(s_xt, t + 1)
                        wait(dve, s_l1, 2 * t)
                        for kb in range(2):
                            got = ps[0:HALF, PARTS * kb:PARTS * kb + PARTS]
                            if gated:
                                last = nc.vector.tensor_copy(XT[0:HALF, kb, :], got)
                            else:
                                last = nc.vector.tensor_scalar(XT[0:HALF, kb, :], got, gb[:, 0, kb:kb + 1], gb[:, 1, kb:kb + 1], ALU.mult, ALU.add)
                        last.then_inc(s_xts, 1)
                    if live(m):
                        dve.wait_ge(s_gt, t)
                        wait(dve, s_l2, m)
                        if gated:
                            nc.vector.tensor_copy(GT[:, 0:3, :].rearrange("p f c -> p (f c)"), ps[:, BANK:BANK + 3 * PARTS]).then_inc(s_gts, 1)
                            k = fts[3][1]
                            nc.vector.tensor_copy(GT[0:k, 3, :], ps[0:k, BANK + 3 * PARTS:BANK + 4 * PARTS]).then_inc(s_gts, 1)
                        else:
                            nc.vector.tensor_copy(GT[:, 0:4, :].rearrange("p f c -> p (f c)"), ps[:, BANK:BANK + 4 * PARTS]).then_inc(s_gts, 1)
                    if live(t) and gated:
                        dve.wait_ge(s_l1, 2 * t + 2)
                        dve.wait_ge(s_g1, t + 1)
                        wait(dve, s_gt, t)
                        nc.vector.tensor_tensor(G[:], act_out[:], ps[:, 4 * BANK:4 * BANK + cut], ALU.mult).then_inc(s_g2, 1)
                    if live(m):
                        dve.wait_ge(s_l2, t)
                        if isinstance(m, int) and m < 2:
                            pass
                        else:
                            dve.wait_ge(s_out[1 - p], paired(16, m - 2, 1 - p))
                        nc.vector.tensor_copy(Y[1 - p][:], ps[:, 5 * BANK:5 * BANK + DIM]).then_inc(s_y, 1)

                schedule(dve, body)

        with ExitStack() as ctx2:
            s2 = Stage(nc, ctx2, name + "_sum")
            more = s2.sbuf("more", [TILE, NTILE, DIM]) if base is not None else None
            Yg = [s2.sbuf(f"Y{k}", [TILE, NTILE, DIM]) for k in range(slots)]
            s_ga = [[s2.sem(f"ga{k}{i}") for i in range(4)] for k in range(slots)]
            s_m, s_v, s_out = s2.sem("m"), s2.sem("v"), s2.sem("out")
            per = NTILE // 4
            block = ctx2.enter_context(nc.Block())

            @block.sync
            def _(sp):
                if base is not None:
                    sp.dma_start(more[:], dram(base, 0, [(DIM, TILE), (TILE * DIM, NTILE), (1, DIM)])).then_inc(s_m, 16)
                steps = slots + (base is not None)
                for q in range(4):
                    sp.wait_ge(s_v, steps * per * (q + 1))
                    sp.dma_start(dram(h_out, q * per * TILE * DIM, [(DIM, TILE), (TILE * DIM, per), (1, DIM)]), rows[:, per * q:per * q + per, :]).then_inc(s_out, 16)
                sp.wait_ge(s_out, 64)

            @block.gpsimd
            def _(pool):
                for i in range(NTILE):
                    for k in range(slots):
                        nc.gpsimd.indirect_dma_start(out=Yg[k][:, i, :], out_offset=None, in_=dram(ys, 0, [(DIM, ntiles * PARTS), (1, DIM)]),
                                                     in_offset=bass.IndirectOffsetOnAxis(ap=pos[k][:, i:i + 1], axis=0)).then_inc(s_ga[k][i // per], 16)

            @block.vector
            def _(dve):
                n = 0
                for q in range(4):
                    for k in range(slots):
                        dve.wait_ge(s_ga[k][q], 16 * per)
                    if base is not None and q == 0:
                        dve.wait_ge(s_m, 16)
                    for i in range(per * q, per * q + per):
                        if base is not None:
                            nc.vector.tensor_tensor(rows[:, i, :], rows[:, i, :], more[:, i, :], ALU.add).then_inc(s_v, 1)
                            n += 1
                            dve.wait_ge(s_v, n)
                        for k in range(slots):
                            if slots == 1:
                                ins = nc.vector.tensor_tensor(rows[:, i, :], rows[:, i, :], Yg[k][:, i, :], ALU.add)
                            else:
                                ins = nc.vector.scalar_tensor_tensor(rows[:, i, :], Yg[k][:, i, :], score[k][:, i:i + 1], rows[:, i, :], ALU.mult, ALU.add)
                            ins.then_inc(s_v, 1)
                            n += 1
                            dve.wait_ge(s_v, n)



def tower(nc, a, out):
    def scratch(name, shape):
        return nc.dram_tensor(name, shape, F32, kind="Internal").ap()

    def under(prefix, names):
        return {n: a[prefix + n] for n in names}

    xpad = scratch("xpad", [IMAGES, CHANNELS, PAD_ROWS, PAD_COLS])
    t1 = scratch("t1", [IMAGES, 33, 33, EMB])
    t2 = scratch("t2", [IMAGES, 17, 17, EMB])
    h0, h1, ffn_x, h2, h3 = (scratch(n, [TOKENS, DIM]) for n in ("h0", "h1", "ffn_x", "h2", "h3"))
    abc = scratch("abc", [48, TOKENS])
    xs = scratch("xs", [5120, DIM])
    ys = scratch("ys", [5120, DIM])

    performer_names = ("n1g", "n1b", "kqvw", "kqvb", "projw", "projb", "n2g", "n2b", "w1", "b1", "w2", "b2", "w")
    ssm_names = [m + s for m in "ABCd" for s in ("_w1", "_b1", "_w2", "_b2")] + ["D_param", "log_dt"]
    first = {"w": {c: (a["L0_attn_" + c.upper() + "W_w"], 0) for c in "qkvo"}, "b": {c: a["L0_attn_" + c.upper() + "W_b"] for c in "qkvo"}}
    second = {"w": {c: (a["L0_ffn_qkv_w"], DIM * i) for i, c in enumerate("qkv")}, "b": {"o": a["L0_ffn_proj_b"]},
              "lng": a["L0_ffn_ln1_g"], "lnb": a["L0_ffn_ln1_b"]}
    second["w"]["o"] = (a["L0_ffn_proj_w"], 0)
    moe = {"gate_w": a["L0_ffn_gate_w"], "gate_b": a["L0_ffn_gate_b"], "w1": [a["L0_ffn_w1"]], "b1": a["L0_ffn_b1"],
           "w2": a["L0_ffn_w2"], "b2": a["L0_ffn_b2"], "lng": a["L0_ffn_ln2_g"], "lnb": a["L0_ffn_ln2_b"]}
    glu = {"gate_w": a["L1_ffn_Wg"], "gate_b": a["L1_ffn_bg"], "w1": [a["L1_ffn_W1"], a["L1_ffn_W2"]], "w2": a["L1_ffn_W3"]}

    with nc.cleanup_on_exit():
        pad_image(nc, a["x"], xpad)
        performer(nc, "a1", xpad, t1, under("L0_tok_a1_", performer_names), True)
    with nc.cleanup_on_exit():
        performer(nc, "a2", t1, t2, under("L0_tok_a2_", performer_names), False)
    with nc.cleanup_on_exit():
        project(nc, t2, h0, a["L0_tok_proj_w"], a["L0_tok_proj_b"], a["cls_tok"])
    with nc.cleanup_on_exit():
        attention(nc, "at", h0, h1, first, False)
    with nc.cleanup_on_exit():
        attention(nc, "fa", h1, ffn_x, second, True)
    with nc.cleanup_on_exit():
        experts(nc, "moe", ffn_x, h1, h2, xs, ys, moe, False)
    with nc.cleanup_on_exit():
        state_space(nc, "ssm", h2, h3, abc, under("L1_attn_", ssm_names))
    with nc.cleanup_on_exit():
        experts(nc, "glu", h3, None, out, xs, ys, glu, True)



def kernel(**inputs):
    import numpy as np
    from concourse import bacc
    from concourse.bass_utils import run_bass_kernel_spmd

    nc = bacc.Bacc("TRN2", target_bir_lowering=False, num_devices=1)
    arrays = {"in_" + n: np.ascontiguousarray(v) for n, v in inputs.items()}
    a = {n: nc.dram_tensor("in_" + n, v.shape, F32, kind="ExternalInput").ap() for n, v in inputs.items()}
    out = nc.dram_tensor("out", (IMAGES, TOKENS // IMAGES, DIM), F32, kind="ExternalOutput").ap()
    tower(nc, a, dram(out, 0, [(DIM, TOKENS), (1, DIM)]))
    return run_bass_kernel_spmd(nc, [arrays], core_ids=[0]).results[0]["out"]
```

```python
from contextlib import ExitStack

import concourse.bass as bass
from concourse import mybir
from concourse.alu_op_type import AluOpType as ALU

ACT = mybir.ActivationFunctionType
F32 = mybir.dt.float32
I32, U32 = mybir.dt.int32, mybir.dt.uint32
AX_X = mybir.AxisListType.X
PARTS = 128
BANK = 512

IMAGES, CHANNELS, SIDE = 32, 3, 128
EMB, FEATS = 64, 32
EPS = 1e-5


def dram(ap, offset, dims):
    return bass.AP(ap.tensor, offset, [list(d) for d in dims])


def spread(ap, axis, n):
    shape = list(ap.shape)
    return ap.unsqueeze(axis).broadcast_to(shape[:axis] + [n] + shape[axis:])


def wait(eng, sem, n):
    if not isinstance(n, int) or n > 0:
        eng.wait_ge(sem, n)


class Stage:

    def __init__(self, nc, ctx, name):
        self.nc, self.ctx, self.name = nc, ctx, name

    def sbuf(self, name, shape, dtype=F32):
        return self.ctx.enter_context(self.nc.sbuf_tensor(f"{self.name}_{name}", shape, dtype))

    def psum(self):
        return self.ctx.enter_context(self.nc.psum_tensor(f"{self.name}_psum", [PARTS, 8 * BANK], F32))

    def sem(self, name):
        return self.nc.alloc_semaphore(name=f"{self.name}_{name}")


def make_identity(nc, pool, ident, done):
    nc.gpsimd.memset(ident[:], 0.0).then_inc(done, 1)
    pool.wait_ge(done, 1)
    nc.gpsimd.affine_select(out=ident[:], in_=ident[:], compare_op=ALU.not_equal, fill=1.0, base=0,
                            pattern=[[-1, PARTS]], channel_multiplier=1).then_inc(done, 1)


PAD_ROWS, PAD_COLS = 132, 132


def pad_image(nc, x, xpad):
    with ExitStack() as ctx:
        st = Stage(nc, ctx, "pad")
        zeros = st.sbuf("zeros", [PARTS, PAD_COLS * 2])
        s_zero, s_edges, s_copy = st.sem("zero"), st.sem("edges"), st.sem("copy")
        planes = IMAGES * CHANNELS
        plane = PAD_ROWS * PAD_COLS
        block = ctx.enter_context(nc.Block())

        @block.vector
        def _(dve):
            nc.vector.memset(zeros[:], 0.0).then_inc(s_zero, 1)

        @block.sync
        def _(sp):
            parts = 4
            step = planes // parts
            for n in range(parts):
                sp.dma_start(dram(xpad, n * step * plane + 2 * PAD_COLS + 2, [(plane, step), (PAD_COLS, SIDE), (1, SIDE)]),
                             dram(x, n * step * SIDE * SIDE, [(SIDE * SIDE, step), (SIDE, SIDE), (1, SIDE)])).then_inc(s_copy, 16)
            sp.wait_ge(s_copy, 16 * parts)

        @block.scalar
        def _(act):
            act.wait_ge(s_zero, 1)
            act.dma_start(dram(xpad, 0, [(plane, planes), (1, 2 * PAD_COLS)]), zeros[0:planes, :]).then_inc(s_edges, 16)
            act.dma_start(dram(xpad, 130 * PAD_COLS, [(plane, planes), (1, 2 * PAD_COLS)]), zeros[0:planes, :]).then_inc(s_edges, 16)
            for c in (0, 130):
                act.dma_start(dram(xpad, 2 * PAD_COLS + c, [(plane, planes), (PAD_COLS, SIDE), (1, 2)]),
                              zeros[0:planes, 0:2 * SIDE].rearrange("p (a b) -> p a b", b=2)).then_inc(s_edges, 16)
            act.wait_ge(s_edges, 16 * 4)



def performer(nc, name, src, dst, w, first):
    quads = 2 if first else 1
    tiles = 4 * quads
    steps = IMAGES if first else IMAGES // 2
    own = 1 if first else 2
    dim = 147 if first else 576
    width = 126 if first else 577
    ktiles = [(0, 126)] if first else [(0, 128), (128, 128), (256, 128), (384, 128), (512, 65)]
    rem = dim - 126
    taps = 9
    COLS = 256

    with ExitStack() as ctx:
        st = Stage(nc, ctx, name)
        ps = st.psum()
        ident = st.sbuf("ident", [PARTS, PARTS])
        W = st.sbuf("W", [PARTS, len(ktiles), COLS])
        Wrem = st.sbuf("Wrem", [PARTS, 4, COLS]) if first else None
        projw1 = st.sbuf("projw1", [EMB + 1, EMB + 1])
        w1 = st.sbuf("w1", [PARTS, PARTS])
        w2 = st.sbuf("w2", [PARTS, PARTS])
        b1 = st.sbuf("b1", [PARTS, 1])
        b2 = st.sbuf("b2", [PARTS, EMB])
        projb = st.sbuf("projb", [PARTS, EMB])
        mask = st.sbuf("mask", [PARTS, 4])
        mhalf = st.sbuf("mhalf", [PARTS, 8])
        epst = st.sbuf("eps", [PARTS, 8])

        with ExitStack() as ctx2:
            s2 = Stage(nc, ctx2, name + "_prep")
            s_w, s_id, s_bias, s_gain, s_kq, s_kqs, s_feat, s_featdone, s_rem, s_ready = (
                s2.sem(n) for n in ("w", "id", "bias", "gain", "kq", "kqs", "feat", "featdone", "rem", "ready"))
            s_bd, s_small, s_zero, s_mv = s2.sem("bd"), s2.sem("small"), s2.sem("zero"), s2.sem("mv")
            gcol = s2.sbuf("gcol", [PARTS, 6])
            bcol = s2.sbuf("bcol", [PARTS, 6])
            Wr = s2.sbuf("Wr", [PARTS, 1, COLS])
            kqvb = s2.sbuf("kqvb", [1, 3 * EMB])
            brow = s2.sbuf("brow", [1, 3 * EMB])
            wr2 = s2.sbuf("wr2", [FEATS, 2 * EMB])
            WB = s2.sbuf("WB", [PARTS, 2 * FEATS])
            WT = s2.sbuf("WT", [PARTS, PARTS])
            g2 = s2.sbuf("g2", [PARTS, 1])
            n2b = s2.sbuf("n2b", [PARTS, 1])
            b1r = s2.sbuf("b1r", [PARTS, 1])
            if first:
                parts_of = [(126, 126, W[:, 0, :]), (rem, rem + 1, Wr[:, 0, :])]
            else:
                parts_of = [(128, 128, W[:, k, :]) for k in range(4)] + [(64, 65, W[:, 4, :])]
            nk = len(parts_of)
            block = ctx2.enter_context(nc.Block())

            @block.sync
            def _(sp):
                n = 0
                ctx2.enter_context(nc.allow_non_contiguous_dma(reason="columns of a few hundred gains and biases"))
                sp.wait_ge(s_zero, 4)
                for k, (rows, _, place) in enumerate(parts_of):
                    if first:
                        sp.dma_start(place[0:rows, 0:3 * EMB], w["kqvw"][126 * k:126 * k + rows, :]).then_inc(s_w, 16)
                        sp.dma_start(gcol[0:rows, k:k + 1], dram(w["n1g"], 126 * k, [(1, rows), (1, 1)])).then_inc(s_w, 16)
                        sp.dma_start(bcol[0:rows, k:k + 1], dram(w["n1b"], 126 * k, [(1, rows), (1, 1)])).then_inc(s_w, 16)
                        n += 3
                    else:
                        for half in range(rows // EMB):
                            tap, p0 = 2 * k + half, EMB * half
                            sp.dma_start(place[p0:p0 + EMB, 0:3 * EMB],
                                         dram(w["kqvw"], tap * 3 * EMB, [(taps * 3 * EMB, EMB), (1, 3 * EMB)])).then_inc(s_w, 16)
                            sp.dma_start(gcol[p0:p0 + EMB, k:k + 1], dram(w["n1g"], tap, [(taps, EMB), (1, 1)])).then_inc(s_w, 16)
                            sp.dma_start(bcol[p0:p0 + EMB, k:k + 1], dram(w["n1b"], tap, [(taps, EMB), (1, 1)])).then_inc(s_w, 16)
                            n += 3
                sp.dma_start(kqvb[0:1, :], dram(w["kqvb"], 0, [(1, 1), (1, 3 * EMB)])).then_inc(s_w, 16)
                for half in range(2):
                    p0 = EMB * half
                    sp.dma_start(wr2[:, p0:p0 + EMB], w["w"]).then_inc(s_w, 16)
                    sp.dma_start(w1[p0:p0 + EMB, p0:p0 + EMB], w["w1"]).then_inc(s_w, 16)
                    sp.dma_start(w2[p0:p0 + EMB, p0:p0 + EMB], w["w2"]).then_inc(s_w, 16)
                    sp.dma_start(g2[p0:p0 + EMB, :], dram(w["n2g"], 0, [(1, EMB), (1, 1)])).then_inc(s_w, 16)
                    sp.dma_start(n2b[p0:p0 + EMB, :], dram(w["n2b"], 0, [(1, EMB), (1, 1)])).then_inc(s_w, 16)
                    sp.dma_start(b1r[p0:p0 + EMB, :], dram(w["b1"], 0, [(1, EMB), (1, 1)])).then_inc(s_w, 16)
                sp.dma_start(projw1[0:EMB, 0:EMB], w["projw"]).then_inc(s_w, 16)
                sp.dma_start(b2[:], dram(w["b2"], 0, [(0, PARTS), (1, EMB)])).then_inc(s_w, 16)
                sp.dma_start(projb[:], dram(w["projb"], 0, [(0, PARTS), (1, EMB)])).then_inc(s_w, 16)
                n += 1 + 12 + 3
                sp.wait_ge(s_w, 16 * n)
                sp.sem_inc(s_ready, 1)
                if first:
                    sp.wait_ge(s_gain, nk + 1)
                    sp.dma_start(Wr[rem:rem + 1, 0, 0:3 * EMB], brow[0:1, :]).then_inc(s_bd, 16)
                    sp.wait_ge(s_featdone, nk)
                    for q in range(4):
                        sp.dma_start(Wrem[32 * q:32 * q + rem + 1, q, :], Wr[0:rem + 1, 0, :]).then_inc(s_rem, 16)
                    sp.wait_ge(s_rem, 64)

            @block.gpsimd
            def _(pool):
                make_identity(nc, pool, ident, s_id)

            @block.vector
            def _(dve):
                nc.vector.memset(w1[:], 0.0).then_inc(s_zero, 1)
                nc.vector.memset(w2[:], 0.0).then_inc(s_zero, 1)
                nc.vector.memset(projw1[:], 0.0).then_inc(s_zero, 1)
                nc.vector.memset(Wr[:], 0.0).then_inc(s_zero, 1)
                nc.vector.memset(WB[:], 0.0).then_inc(s_mv, 1)
                if first:
                    nc.vector.memset(Wrem[:], 0.0).then_inc(s_mv, 1)
                nc.vector.memset(mask[:], 0.0).then_inc(s_small, 1)
                nc.vector.memset(mhalf[:], -0.5)
                nc.vector.memset(epst[:], EPS)
                dve.wait_ge(s_small, 1)
                for q in range(4):
                    nc.vector.memset(mask[32 * q:32 * q + 32, q:q + 1], 1.0)
                dve.wait_ge(s_ready, 1)
                nc.vector.memset(projw1[EMB:EMB + 1, EMB:EMB + 1], 1.0)
                dve.wait_ge(s_bias, 1)
                nc.vector.tensor_tensor(brow[0:1, :], ps[0:1, 0:3 * EMB], kqvb[0:1, :], ALU.add).then_inc(s_gain, 1)
                for k, (rows, _, place) in enumerate(parts_of):
                    nc.vector.tensor_scalar(place[0:rows, 0:3 * EMB], place[0:rows, 0:3 * EMB], gcol[0:rows, k:k + 1],
                                            None, ALU.mult).then_inc(s_gain, 1)
                if not first:
                    dve.wait_ge(s_gain, 1)
                    nc.vector.tensor_copy(W[EMB:EMB + 1, 4, 0:3 * EMB], brow[0:1, :]).then_inc(s_bd, 16)
                dve.wait_ge(s_kq, 1)
                dve.wait_ge(s_mv, 1)
                nc.vector.tensor_copy(WB[0:EMB, 0:FEATS], ps[0:EMB, BANK:BANK + FEATS])
                nc.vector.tensor_copy(WB[EMB:, FEATS:], ps[EMB:, BANK:BANK + FEATS]).then_inc(s_kqs, 1)
                for k, (_, rows, place) in enumerate(parts_of):
                    dve.wait_ge(s_kq, k + 2)
                    nc.vector.tensor_copy(WT[:, 0:rows], ps[:, 2 * BANK:2 * BANK + rows]).then_inc(s_kqs, 1)
                    dve.wait_ge(s_feat, k + 1)
                    nc.vector.tensor_copy(place[0:rows, 3 * EMB:COLS], ps[0:rows, 3 * BANK:3 * BANK + 2 * FEATS]).then_inc(s_featdone, 1)
                dve.wait_ge(s_bias, 2)
                nc.vector.tensor_tensor(b1[:], ps[:, 4 * BANK:4 * BANK + 1], b1r[:], ALU.add)
                nc.vector.tensor_scalar(w1[:], w1[:], g2[:, 0:1], None, ALU.mult)

            @block.tensor
            def _(pe):
                pe.wait_ge(s_ready, 1)
                for k, (rows, _, place) in enumerate(parts_of):
                    last = nc.tensor.matmul(ps[0:1, 0:3 * EMB], bcol[0:rows, k:k + 1], place[0:rows, 0:3 * EMB],
                                            start=(k == 0), stop=(k == nk - 1))
                last.then_inc(s_bias, 1)
                nc.tensor.matmul(ps[:, 4 * BANK:4 * BANK + 1], w1[:], n2b[:, 0:1], start=True, stop=True).then_inc(s_bias, 1)
                pe.wait_ge(s_id, 2)
                nc.tensor.transpose(ps[:, BANK:BANK + FEATS], wr2[:], ident[0:FEATS, 0:FEATS]).then_inc(s_kq, 1)
                pe.wait_ge(s_bd, 16)
                pe.wait_ge(s_gain, nk + 1)
                for k, (_, rows, place) in enumerate(parts_of):
                    wait(pe, s_kqs, k + 1)
                    nc.tensor.transpose(ps[:, 2 * BANK:2 * BANK + rows], place[0:rows, 0:2 * EMB], ident[0:rows, 0:rows]).then_inc(s_kq, 1)
                    pe.wait_ge(s_kqs, k + 2)
                    wait(pe, s_featdone, k)
                    nc.tensor.matmul(ps[0:rows, 3 * BANK:3 * BANK + 2 * FEATS], WT[:, 0:rows], WB[:], start=True, stop=True).then_inc(s_feat, 1)

        X = [st.sbuf(f"X{p}", [PARTS, 21, 35] if first else [PARTS, 4, dim]) for p in range(2)]
        hN = st.sbuf("hN", [PARTS, tiles, width])
        hR = st.sbuf("hR", [PARTS, tiles, 32]) if first else None
        stats = st.sbuf("stats", [PARTS, tiles, 1 if first else 2, 6])
        mv = st.sbuf("mv", [PARTS, tiles, 2])
        rstd = st.sbuf("rstd", [PARTS, tiles])
        nkt = 1 if first else 5
        hT = st.sbuf("hT", [PARTS, quads if first else nkt, BANK])
        RQ = st.sbuf("RQ", [PARTS, BANK])
        sq = st.sbuf("sq", [PARTS, tiles, 2, EMB])
        xd = st.sbuf("xd", [PARTS, tiles, 2])
        v1 = st.sbuf("v1", [PARTS, tiles, EMB + 1])
        z = st.sbuf("z", [PARTS, 2, tiles, FEATS])
        kpq = st.sbuf("kpq", [PARTS, 2, tiles, FEATS])
        kvT = st.sbuf("kvT", [EMB + 1, 4, FEATS])
        BD = st.sbuf("BD", [PARTS, 4, EMB + 1])
        den = st.sbuf("den", [PARTS, tiles])
        rden = st.sbuf("rden", [PARTS, tiles])
        vp = st.sbuf("vp", [PARTS, tiles, EMB])
        y = st.sbuf("y", [PARTS, tiles, EMB])
        yb = st.sbuf("yb", [PARTS, tiles, EMB])
        stats2 = st.sbuf("stats2", [PARTS, tiles, 6])
        mv2 = st.sbuf("mv2", [PARTS, tiles, 2])
        rstd2 = st.sbuf("rstd2", [PARTS, tiles])
        yn = st.sbuf("yn", [PARTS, tiles, EMB])
        yT = st.sbuf("yT", [PARTS, tiles // 2, PARTS])
        G = st.sbuf("G", [PARTS, tiles // 2, PARTS])
        O = [st.sbuf(f"O{p}", [PARTS, tiles, EMB]) for p in range(2)]
        BDz = st.sbuf("BDz", [IMAGES, 33 * EMB])
        half = tiles // 2 * PARTS

        names = ("x_in0", "x_in1", "out0", "out1", "border", "stat", "aggr", "eps1", "rstd1", "norm", "trans", "tback", "rem", "kq", "sq", "v", "xd", "z", "exp",
                 "kv", "kvs", "qt", "rq", "kp", "bd", "num", "den", "rden", "ymul", "y", "vp", "yb", "stat2", "aggr2",
                 "eps2", "rstd2", "norm2", "yt", "yts", "m1", "gelu", "m2", "fin", "ones", "zero", "tail", "load", "gate")
        s = {n: st.sem(n) for n in names}
        nq = quads if first else 1
        nt = quads if first else nkt
        out_dmas = 4 if first else 4
        in_dmas = 12 if first else 12

        def bank(b, n=BANK):
            return ps[:, b * BANK:b * BANK + n]

        KQ = [ps[:, (2 + 2 * q) * BANK:(4 + 2 * q) * BANK].rearrange("p (t c) -> p t c", c=COLS) for q in range(quads)]
        KV, KP = ps[0:EMB + 1, 6 * BANK:6 * BANK + own * FEATS], ps[:, 6 * BANK + 64:6 * BANK + 64 + EMB + 1]
        NUM = [ps[:, 6 * BANK + 192:6 * BANK + 192 + 4 * (EMB + 1)].rearrange("p (t c) -> p t c", c=EMB + 1),
               ps[:, 7 * BANK:7 * BANK + 4 * (EMB + 1)].rearrange("p (t c) -> p t c", c=EMB + 1)]

        def window(p, j, n=21):
            return X[p][:, 0:n, 4 * j:4 * j + 7] if first else X[p][:, j, :]

        def twice(each, i, p):
            return each * (i - p + 2) // 2 if isinstance(i, int) else (i - p) * (each // 2) + each

        def live(i):
            return 0 <= i < steps if isinstance(i, int) else True

        def schedule(eng, body):
            for t in range(6):
                body(t, t % 2)
            with eng.Fori(6, steps, 2) as t:
                body(t, 0)
                body(t + 1, 1)
            for t in range(steps, steps + 4):
                body(t, t % 2)

        block = ctx.enter_context(nc.Block())

        @block.sync
        def _(sp):
            sp.wait_ge(s["zero"], 1)
            rows = 33 if first else 17
            pic = rows * rows * EMB
            sp.dma_start(dram(dst, 0, [(pic, IMAGES), (1, rows * EMB)]),
                         BDz[0:IMAGES, 0:rows * EMB]).then_inc(s["border"], 16)
            sp.dma_start(dram(dst, rows * EMB, [(pic, IMAGES), (rows * EMB, rows - 1), (1, EMB)]),
                         BDz[0:IMAGES, 0:(rows - 1) * EMB].rearrange("p (a b) -> p a b", b=EMB)).then_inc(s["border"], 16)

            def load(i, p):
                wait(sp, s["norm"], i - 1)
                if first:
                    sp.sem_inc(s["load"], 1)
                    wait(sp, s["tail"], 2 * (i - 1))
                sp.sem_inc(s["load"], 1)
                if first:
                    for ob in range(4):
                        for c in range(CHANNELS):
                            sp.dma_start(X[p][32 * ob:32 * ob + 32, 7 * c:7 * c + 7, :],
                                         dram(src, (i * CHANNELS + c) * (PAD_ROWS * PAD_COLS) + 32 * ob,
                                              [(4 * PAD_COLS, 32), (PAD_COLS, 7), (1, 35)])).then_inc(s["x_in%d" % p], 16)
                else:
                    for im in range(2):
                        for tl in range(2):
                            for ky in range(3):
                                sp.dma_start(X[p][:, 2 * im + tl, 192 * ky:192 * ky + 192],
                                             dram(src, (2 * i + im) * (33 * 33 * EMB) + (16 * tl + ky) * 33 * EMB,
                                                  [(2 * 33 * EMB, 8), (2 * EMB, 16), (1, 3 * EMB)])).then_inc(s["x_in%d" % p], 16)

            def store(i, p):
                sp.wait_ge(s["fin"], i + 1)
                sp.sem_inc(s["load"], 1)
                if first:
                    for ob in range(4):
                        sp.dma_start(dram(dst, i * pic + (33 + 1 + 8 * ob) * EMB, [(33 * EMB, 32), (1, 8 * EMB)]),
                                     O[p][32 * ob:32 * ob + 32, :, :]).then_inc(s["out%d" % p], 16)
                else:
                    for im in range(2):
                        for tl in range(2):
                            sp.dma_start(dram(dst, (2 * i + im) * pic + (17 * (1 + 8 * tl) + 1) * EMB,
                                              [(17 * EMB, 8), (EMB, 16), (1, EMB)]), O[p][:, 2 * im + tl, :]).then_inc(s["out%d" % p], 16)

            def body(t, p):
                if live(t):
                    load(t, p)
                if live(t - 4):
                    store(t - 4, p)

            schedule(sp, body)
            sp.wait_ge(s["border"], 32)
            for p in range(2):
                sp.wait_ge(s["out%d" % p], 16 * out_dmas * steps // 2)

        @block.gpsimd
        def _(pool):
            nc.gpsimd.memset(BDz[:], 0.0).then_inc(s["zero"], 1)
            if first:
                nc.gpsimd.memset(hR[:, :, rem + 1:], 0.0)
                nc.gpsimd.memset(hR[:, :, rem:rem + 1], 1.0)
            else:
                nc.gpsimd.memset(hN[:, :, dim:dim + 1], 1.0)
            nc.gpsimd.memset(v1[:, :, EMB:EMB + 1], 1.0).then_inc(s["ones"], 1)

            def inverse_root(i, aggr, eps, done, mvt, out):
                pool.wait_ge(s[aggr], tiles * (i + 1))
                nc.gpsimd.tensor_tensor(out[:], mvt[:, :, 1], epst[:, 0:tiles], ALU.add).then_inc(s[eps], 1)
                pool.wait_ge(s[eps], i + 1)
                nc.gpsimd.tensor_tensor(out[:], out[:], mhalf[:, 0:tiles], ALU.pow).then_inc(s[done], 1)

            def body(t, p):
                l = t - 3
                if live(t - 2):
                    pool.wait_ge(s["v"], quads * (t - 1))
                    wait(pool, s["y"], t - 2)
                    nc.gpsimd.tensor_tensor(vp[:], v1[:, :, 0:EMB], spread(projb[:], 1, tiles), ALU.add).then_inc(s["vp"], 1)
                if live(l):
                    inverse_root(l, "aggr2", "eps2", "rstd2", mv2, rstd2)
                    pool.wait_ge(s["y"], l + 1)
                    wait(pool, s["fin"], l)
                    nc.gpsimd.tensor_tensor(yb[:], y[:], spread(b2[:], 1, tiles), ALU.add).then_inc(s["yb"], 1)
                if live(t):
                    inverse_root(t, "aggr", "eps1", "rstd1", mv, rstd)
                    if first:
                        tail = bass.AP(X[p][:].tensor, 18 * 35, [list(X[p][:].ap[0]), [4, tiles], [35, 3], [1, 7]])
                        out = hR[:, :, 0:rem].rearrange("p t (a b) -> p t a b", b=7)
                        wait(pool, s["trans"], 3 * t)
                        nc.gpsimd.tensor_tensor(out, tail, spread(spread(mv[:, :, 0], 2, 3), 3, 7), ALU.subtract).then_inc(s["tail"], 1)
                        pool.wait_ge(s["tail"], 2 * t + 1)
                        nc.gpsimd.tensor_tensor(hR[:, :, 0:rem], hR[:, :, 0:rem], spread(rstd[:], 2, rem), ALU.mult).then_inc(s["tail"], 1)

            schedule(pool, body)

        @block.vector
        def _(dve):
            def statistics(i, p):
                if first:
                    wait(dve, s["tail"], 2 * i)
                dve.wait_ge(s["x_in%d" % p], twice(16 * in_dmas, i, p))
                for j in range(tiles):
                    if first:
                        nc.vector.bn_stats(stats[:, j, 0, :], window(p, j)).then_inc(s["stat"], 1)
                    else:
                        for h in range(2):
                            last = nc.vector.bn_stats(stats[:, j, h, :], X[p][:, j, 288 * h:288 * h + 288])
                        last.then_inc(s["stat"], 1)

            def aggregate(i):
                for j in range(tiles):
                    nc.vector.bn_aggr(mv[:, j, :], stats[:, j, :, :].rearrange("p a b -> p (a b)")).then_inc(s["aggr"], 1)

            def normalise(i, p):
                dve.wait_ge(s["rstd1"], i + 1)
                wait(dve, s["trans"], (nt + (1 if first else 0)) * i)
                for j in range(tiles):
                    out = hN[:, j, :].rearrange("p (a b) -> p a b", b=7) if first else hN[:, j, 0:dim]
                    last = nc.vector.tensor_scalar(out, window(p, j, 18), mv[:, j, 0:1], rstd[:, j:j + 1], ALU.subtract, ALU.mult)
                last.then_inc(s["norm"], 1)

            def exponent(i, q):
                tl = slice(4 * q, 4 * q + 4)
                dve.wait_ge(s["sq"], quads * i + q + 1)
                nc.vector.reduce_sum(xd[:, tl, :], sq[:, tl, :, :], axis=AX_X).then_inc(s["xd"], 1)
                dve.wait_ge(s["xd"], quads * i + q + 1)
                wait(dve, s["exp"], i)
                dve.wait_ge(s["v"], quads * i + q + 1)
                nc.vector.tensor_tensor(z[:, :, tl, :].rearrange("p a t f -> p t a f"), KQ[q][:, :, 3 * EMB:COLS].rearrange("p t (a f) -> p t a f", a=2),
                                        spread(xd[:, tl, :], 3, FEATS), ALU.subtract).then_inc(s["z"], 1)

            def block_diagonal(i):
                dve.wait_ge(s["kp"], i + 1)
                wait(dve, s["num"], quads * i)
                nc.vector.tensor_tensor(BD[:], spread(KP, 1, 4), spread(mask[:], 2, EMB + 1), ALU.mult).then_inc(s["bd"], 1)

            def attend(i):
                for q in range(quads):
                    dve.wait_ge(s["num"], quads * i + q + 1)
                    nc.vector.tensor_scalar(den[:, 4 * q:4 * q + 4], NUM[q][:, :, EMB], 1e-8 * FEATS, None, ALU.add).then_inc(s["den"], 1)
                dve.wait_ge(s["den"], quads * (i + 1))
                nc.vector.reciprocal(rden[:], den[:]).then_inc(s["rden"], 1)
                dve.wait_ge(s["rden"], i + 1)
                wait(dve, s["yb"], i)
                for q in range(quads):
                    nc.vector.tensor_tensor(y[:, 4 * q:4 * q + 4, :], NUM[q][:, :, 0:EMB],
                                            spread(rden[:, 4 * q:4 * q + 4], 2, EMB), ALU.mult).then_inc(s["ymul"], 1)
                dve.wait_ge(s["ymul"], quads * (i + 1))
                dve.wait_ge(s["vp"], i + 1)
                nc.vector.tensor_tensor(y[:], y[:], vp[:], ALU.add).then_inc(s["y"], 1)
                dve.wait_ge(s["y"], i + 1)
                for j in range(tiles):
                    nc.vector.bn_stats(stats2[:, j, :], y[:, j, :]).then_inc(s["stat2"], 1)

            def aggregate2(i):
                for j in range(tiles):
                    nc.vector.bn_aggr(mv2[:, j, :], stats2[:, j, :]).then_inc(s["aggr2"], 1)

            def normalise2(i):
                dve.wait_ge(s["rstd2"], i + 1)
                wait(dve, s["yt"], i)
                for j in range(tiles):
                    last = nc.vector.tensor_scalar(yn[:, j, :], y[:, j, :], mv2[:, j, 0:1], rstd2[:, j:j + 1], ALU.subtract, ALU.mult)
                last.then_inc(s["norm2"], 1)

            def finish(i, p):
                dve.wait_ge(s["m2"], i + 1)
                dve.wait_ge(s["yb"], i + 1)
                wait(dve, s["out%d" % p], twice(16 * out_dmas, i - 2, p))
                nc.vector.tensor_tensor(O[p][:].rearrange("p t e -> p (t e)"), bank(1, half), yb[:].rearrange("p t e -> p (t e)"),
                                        ALU.add).then_inc(s["fin"], 1)

            def body(t, p):
                l = t - 3
                if live(t - 2):
                    exponent(t - 2, quads - 1)
                if live(t - 4):
                    finish(t - 4, p)
                if live(l):
                    attend(l)
                    dve.wait_ge(s["stat2"], tiles * (l + 1))
                    dve.sem_inc(s["gate"], 1)
                    aggregate2(l)
                if live(t):
                    statistics(t, p)
                    dve.wait_ge(s["stat"], tiles * (t + 1))
                    dve.sem_inc(s["gate"], 1)
                    aggregate(t)
                if live(l):
                    normalise2(l)
                if live(t - 1) and quads == 2:
                    exponent(t - 1, 0)
                if live(t):
                    normalise(t, p)
                if live(t - 2):
                    block_diagonal(t - 2)

            schedule(dve, body)

        @block.scalar
        def _(act):
            def body(t, p):
                m, k, l = t - 1, t - 2, t - 3
                if live(m):
                    for q in range(nt):
                        rows = ktiles[0][1] if first else ktiles[q][1]
                        act.wait_ge(s["trans"], (nt + (1 if first else 0)) * m + q + 1)
                        nc.scalar.copy(hT[0:rows, q, :], ps[0:rows, (q % 2) * BANK:(q % 2 + 1) * BANK]).then_inc(s["tback"], 1)
                    if first:
                        act.wait_ge(s["trans"], 3 * (m + 1))
                        nc.scalar.copy(RQ[:, 0:256], bank(7)[:, 0:256]).then_inc(s["rem"], 1)
                if live(k):
                    act.wait_ge(s["z"], quads * (k + 1))
                    wait(act, s["qt"], k)
                    nc.scalar.activation(kpq[:].rearrange("p a t f -> p (a t f)"), z[:].rearrange("p a t f -> p (a t f)"), ACT.Exp).then_inc(s["exp"], 1)

                def squares(q):
                    tl = slice(4 * q, 4 * q + 4)
                    act.wait_ge(s["kq"], quads * m + q + 1)
                    wait(act, s["xd"], quads * m)
                    nc.scalar.activation(sq[:, tl, :, :].rearrange("p t a e -> p t (a e)"), KQ[q][:, :, 0:2 * EMB], ACT.Square,
                                         scale=0.5 ** 0.5).then_inc(s["sq"], 1)
                    wait(act, s["kv"], m)
                    wait(act, s["vp"], m)
                    if isinstance(m, int) and m == 0:
                        act.wait_ge(s["ones"], 1)
                    nc.scalar.copy(v1[:, tl, 0:EMB], KQ[q][:, :, 2 * EMB:3 * EMB]).then_inc(s["v"], 1)

                if live(m) and quads == 2:
                    squares(0)
                if live(k):
                    act.wait_ge(s["kv"], k + 1)
                    kv = KV.rearrange("p (i f) -> p i f", f=FEATS)
                    nc.scalar.copy(kvT[:].rearrange("p (i r) f -> p i r f", i=own), spread(kv, 2, 4 // own)).then_inc(s["kvs"], 1)
                if live(l):
                    act.wait_ge(s["yt"], l + 1)
                    nc.scalar.copy(yT[:].rearrange("p t c -> p (t c)"), bank(7, half)).then_inc(s["yts"], 1)
                if live(k):
                    act.wait_ge(s["qt"], k + 1)
                    nc.scalar.copy(RQ[:, 256:256 + PARTS * quads], bank(7)[:, 256:256 + PARTS * quads]).then_inc(s["rq"], 1)
                if live(l):
                    act.wait_ge(s["m1"], l + 1)
                    nc.scalar.activation(G[:].rearrange("p t c -> p (t c)"), bank(0, half), ACT.Gelu, bias=b1[:, 0:1]).then_inc(s["gelu"], 1)
                if live(m):
                    squares(quads - 1)

            schedule(act, body)

        @block.tensor
        def _(pe):
            def main_transposes(m):
                pe.wait_ge(s["norm"], m + 1)
                if isinstance(m, int) and m == 0:
                    pe.wait_ge(s["ones"], 1)
                for q in range(nt):
                    c0, rows = ktiles[0] if first else ktiles[q]
                    if q == 0:
                        wait(pe, s["gelu"], m - 2)
                        wait(pe, s["tback"], nt * m)
                    if q == 1:
                        wait(pe, s["fin"], m - 2)
                    if q >= 2:
                        pe.wait_ge(s["tback"], nt * m + q - 1)
                    for j in range(4):
                        tile = 4 * q + j if first else j
                        last = nc.tensor.transpose(ps[0:rows, (q % 2) * BANK + PARTS * j:(q % 2) * BANK + PARTS * j + PARTS],
                                                   hN[:, tile, c0:c0 + rows], ident[:])
                    last.then_inc(s["trans"], 1)

            cuts = [[(0, 0), (0, 1), (0, 2), (0, 3)], [(1, 0), (1, 1)], [(1, 2), (1, 3)]] if quads == 2 else \
                   [[(0, 0), (0, 1)], [(0, 2)], [(0, 3)]]

            def matmuls(m, cut):
                for q, j in cuts[cut]:
                    if j == 0:
                        pe.wait_ge(s["tback"], nt * m + (q + 1 if first else nt))
                        if first:
                            pe.wait_ge(s["rem"], m + 1)
                        wait(pe, s["z"], quads * (m - 1) + q + 1 if not isinstance(m, int) or m >= 1 else 0)
                        wait(pe, s["v"], quads * (m - 1) + q + 1 if not isinstance(m, int) or m >= 1 else 0)
                    out = KQ[q][:, j, :]
                    cols = slice(PARTS * j, PARTS * j + PARTS)
                    if first:
                        nc.tensor.matmul(out, hT[0:126, q, cols], W[0:126, 0, :], start=True, stop=False)
                        last = nc.tensor.matmul(out, RQ[:, PARTS * q:PARTS * q + PARTS], Wrem[:, j, :], start=False, stop=True)
                    else:
                        for kt in range(nkt):
                            rows = ktiles[kt][1]
                            last = nc.tensor.matmul(out, hT[0:rows, kt, cols], W[0:rows, kt, :], start=(kt == 0), stop=(kt == nkt - 1))
                    if j == 3:
                        last.then_inc(s["kq"], 1)

            def body(t, p):
                m, k, l = t - 1, t - 2, t - 3
                if live(m):
                    main_transposes(m)
                    if first:
                        pe.wait_ge(s["tail"], 2 * (m + 1))
                        wait(pe, s["ymul"], quads * k)
                        for q in range(quads):
                            rows = hR[:, 4 * q:4 * q + 4, :].rearrange("p t c -> p (t c)")
                            last = nc.tensor.transpose(bank(7)[:, PARTS * q:PARTS * q + PARTS], rows, ident[:])
                        last.then_inc(s["trans"], 1)
                    matmuls(m, 0)
                if live(k):
                    pe.wait_ge(s["exp"], k + 1)
                    wait(pe, s["ymul"], quads * (k - 1) + 1 if not isinstance(k, int) or k >= 1 else 0)
                    per = tiles // own
                    for im in range(own):
                        for j in range(per):
                            tile = per * im + j
                            last = nc.tensor.matmul(KV[:, FEATS * im:FEATS * im + FEATS], v1[:, tile, :], kpq[:, 0, tile, :],
                                                    start=(j == 0), stop=(j == per - 1))
                    last.then_inc(s["kv"], 1)
                if live(l):
                    pe.wait_ge(s["norm2"], l + 1)
                    if quads == 2:
                        wait(pe, s["ymul"], quads * (l + 1))
                    if live(m) and first:
                        pe.wait_ge(s["rem"], m + 1)
                    for j in range(tiles // 2):
                        last = nc.tensor.transpose(bank(7)[:, PARTS * j:PARTS * j + PARTS],
                                                   yn[:, 2 * j:2 * j + 2, :].rearrange("p t e -> p (t e)"), ident[:])
                    last.then_inc(s["yt"], 1)
                if live(m):
                    matmuls(m, 1)
                if live(k):
                    if live(l):
                        pe.wait_ge(s["yts"], l + 1)
                    else:
                        wait(pe, s["ymul"], quads * k)
                        if live(m) and first:
                            pe.wait_ge(s["rem"], m + 1)
                    for q in range(quads):
                        last = nc.tensor.transpose(bank(7)[:, 256 + PARTS * q:256 + PARTS * q + PARTS],
                                                   kpq[:, 1, 4 * q:4 * q + 4, :].rearrange("p t f -> p (t f)"), ident[:])
                    last.then_inc(s["qt"], 1)
                    pe.wait_ge(s["kvs"], k + 1)
                    nc.tensor.matmul(KP, kvT[:].rearrange("p r f -> p (r f)"), projw1[:], start=True, stop=True).then_inc(s["kp"], 1)
                if live(l):
                    pe.wait_ge(s["yts"], l + 1)
                    if live(m):
                        pe.wait_ge(s["tback"], nt * (m + 1))
                    nc.tensor.matmul(bank(0, half), w1[:], yT[:].rearrange("p t c -> p (t c)"), start=True, stop=True).then_inc(s["m1"], 1)
                if live(m):
                    matmuls(m, 2)
                if live(k):
                    pe.wait_ge(s["bd"], k + 1)
                    pe.wait_ge(s["rq"], k + 1)
                    for q in range(quads):
                        last = nc.tensor.matmul(NUM[q].rearrange("p t c -> p (t c)"), RQ[:, 256 + PARTS * q:256 + PARTS * q + PARTS],
                                                BD[:].rearrange("p t c -> p (t c)"), start=True, stop=True)
                        last.then_inc(s["num"], 1)
                if live(l):
                    pe.wait_ge(s["gelu"], l + 1)
                    for j in range(tiles // 2):
                        last = nc.tensor.matmul(bank(1)[:, PARTS * j:PARTS * j + PARTS], G[:, j, :], w2[:], start=True, stop=True)
                    last.then_inc(s["m2"], 1)

            schedule(pe, body)


DIM, SEQ, HALF = 192, 65, 96
TOKENS = IMAGES * SEQ
TILE, NTILE = 104, 20


def project(nc, src, dst, w, b, cls):
    steps, dim, taps = IMAGES // 2, 576, 9
    ktiles = [(128 * k, 128) for k in range(4)] + [(512, 65)]
    with ExitStack() as ctx:
        st = Stage(nc, ctx, "proj")
        ps = st.psum()
        ident = st.sbuf("ident", [PARTS, PARTS])
        W = st.sbuf("W", [PARTS, 5, DIM])
        DEPTH = 4
        X = [st.sbuf(f"X{p}", [PARTS, dim + 1]) for p in range(DEPTH)]
        XT = st.sbuf("XT", [PARTS, 5, PARTS])
        O = [st.sbuf(f"O{p}", [PARTS, DIM]) for p in range(2)]
        s_w, s_id, s_ones, s_cls = st.sem("w"), st.sem("id"), st.sem("ones"), st.sem("cls")
        s_in = [st.sem(f"in{p}") for p in range(DEPTH)]
        s_out = [st.sem(f"out{p}") for p in range(2)]
        s_t, s_ts, s_t5, s_mm, s_o = st.sem("t"), st.sem("ts"), st.sem("t5"), st.sem("mm"), st.sem("o")
        block = ctx.enter_context(nc.Block())

        @block.sync
        def _(sp):
            sp.dma_start(dram(dst, 0, [(SEQ * DIM, IMAGES), (1, DIM)]), dram(cls, 0, [(0, IMAGES), (1, DIM)])).then_inc(s_cls, 16)
            for tap in range(taps):
                p0 = EMB * (tap % 2)
                sp.dma_start(W[p0:p0 + EMB, tap // 2, :], dram(w, tap * DIM, [(taps * DIM, EMB), (1, DIM)])).then_inc(s_w, 16)
            sp.dma_start(W[EMB:EMB + 1, 4, :], dram(b, 0, [(DIM, 1), (1, DIM)])).then_inc(s_w, 16)

            def load(i):
                for im in range(2):
                    for ky in range(3):
                        sp.dma_start(X[i % DEPTH][EMB * im:EMB * im + EMB, 192 * ky:192 * ky + 192],
                                     dram(src, (2 * i + im) * (17 * 17 * EMB) + ky * 17 * EMB,
                                          [(2 * 17 * EMB, 8), (2 * EMB, 8), (1, 3 * EMB)])).then_inc(s_in[i % DEPTH], 16)

            for i in range(DEPTH - 1):
                load(i)
            for i in range(steps):
                if i + DEPTH - 1 < steps:
                    wait(sp, s_t, 5 * i)
                    load(i + DEPTH - 1)
                sp.wait_ge(s_o, i + 1)
                sp.dma_start(dram(dst, (2 * i * SEQ + 1) * DIM, [(SEQ * DIM, 2), (DIM, EMB), (1, DIM)]), O[i % 2][:]).then_inc(s_out[i % 2], 16)
            sp.wait_ge(s_cls, 16)
            for p in range(2):
                sp.wait_ge(s_out[p], 8 * steps)

        @block.gpsimd
        def _(pool):
            make_identity(nc, pool, ident, s_id)
            for x in X:
                last = nc.gpsimd.memset(x[:, dim:], 1.0)
            last.then_inc(s_ones, 1)

        @block.tensor
        def _(pe):
            pe.wait_ge(s_id, 2)
            pe.wait_ge(s_ones, 1)
            for i in range(steps + 1):
                if i < steps:
                    pe.wait_ge(s_in[i % DEPTH], 96 * (i // DEPTH + 1))
                    wait(pe, s_ts, i)
                    wait(pe, s_t5, i)
                    for k, (c0, rows) in enumerate(ktiles):
                        nc.tensor.transpose(ps[0:rows, PARTS * k:PARTS * k + PARTS], X[i % DEPTH][:, c0:c0 + rows], ident[:]).then_inc(s_t, 1)
                if i == 0:
                    pe.wait_ge(s_w, 160)
                if i < steps:
                    pe.wait_ge(s_ts, i + 1)
                    pe.wait_ge(s_t5, i + 1)
                    wait(pe, s_o, i - 1)
                    out = ps[:, (2 + i % 2) * BANK:(2 + i % 2) * BANK + DIM]
                    for k, (c0, rows) in enumerate(ktiles):
                        last = nc.tensor.matmul(out, XT[0:rows, k, :], W[0:rows, k, :], start=(k == 0), stop=(k == 4))
                    last.then_inc(s_mm, 1)

        @block.scalar
        def _(act):
            for i in range(steps):
                act.wait_ge(s_t, 5 * i + 4)
                nc.scalar.copy(XT[:, 0:4, :].rearrange("p k c -> p (k c)"), ps[:, 0:BANK]).then_inc(s_ts, 1)

        @block.vector
        def _(dve):
            for i in range(steps):
                dve.wait_ge(s_t, 5 * i + 5)
                nc.vector.tensor_copy(XT[0:EMB + 1, 4, :], ps[0:EMB + 1, BANK:BANK + PARTS]).then_inc(s_t5, 1)
                dve.wait_ge(s_mm, i + 1)
                wait(dve, s_out[i % 2], 16 * (i // 2))
                nc.vector.tensor_copy(O[i % 2][:], ps[:, (2 + i % 2) * BANK:(2 + i % 2) * BANK + DIM]).then_inc(s_o, 1)


def moments(nc, dve, stats, tmp, s, base):
    a = [stats[:, :, n] for n in range(6)]
    nc.vector.tensor_tensor(tmp[0], a[1], a[4], ALU.add).then_inc(s, 1)
    nc.vector.tensor_tensor(tmp[1], a[1], a[4], ALU.subtract).then_inc(s, 1)
    nc.vector.tensor_tensor(tmp[2], a[2], a[5], ALU.add).then_inc(s, 1)
    dve.wait_ge(s, base + 3)
    nc.vector.tensor_scalar(tmp[0], tmp[0], 0.5, None, ALU.mult).then_inc(s, 1)
    nc.vector.tensor_tensor(tmp[1], tmp[1], tmp[1], ALU.mult).then_inc(s, 1)
    nc.vector.tensor_scalar(tmp[2], tmp[2], 1.0 / DIM, EPS, ALU.mult, ALU.add).then_inc(s, 1)
    dve.wait_ge(s, base + 6)
    nc.vector.scalar_tensor_tensor(tmp[2], tmp[1], 0.25, tmp[2], ALU.mult, ALU.add).then_inc(s, 1)


HEADS = 12


def attention(nc, name, h_in, h_out, w, second):
    HG = 6
    with ExitStack() as ctx:
        st = Stage(nc, ctx, name)
        rows = st.sbuf("rows", [TILE, NTILE, DIM])
        xT = st.sbuf("xT", [HALF + 1, 2, TOKENS])
        ident = st.sbuf("ident", [PARTS, PARTS])
        WT = st.sbuf("WT", [HALF + 1, 2, 4, DIM])
        mask = st.sbuf("mask", [HALF, HG])
        qT = st.sbuf("qT", [HALF, 2, TOKENS])
        kT = st.sbuf("kT", [HALF, 2, TOKENS])
        oT = st.sbuf("oT", [HALF + 1, 2, TOKENS])
        xi = st.sbuf("xi", [HALF + 1, 2, SEQ])
        qi = st.sbuf("qi", [HALF, 2, SEQ])
        on = st.sbuf("on", [SEQ, DIM])
        v1 = st.sbuf("v1", [SEQ, HEADS, 17])

        with ExitStack() as ctx2:
            s2 = Stage(nc, ctx2, name + "_prep")
            ps = s2.psum()
            xn = s2.sbuf("xn", [TILE, NTILE, DIM])
            norm = NormedColumns(nc, s2, ps, h_in, rows, xT, ident, xn, twice=second)
            raw = s2.sbuf("raw", [HALF, 4, 2, DIM])
            bpad = s2.sbuf("bpad", [HALF, 2, HALF + 1]) if second else None
            g = s2.sbuf("g", [HALF, 2]) if second else None
            s_w, s_mask, s_t, s_ts, s_b, s_c, s_g, s_qk, s_e = (
                s2.sem(n) for n in ("w", "mask", "t", "ts", "b", "c", "g", "qk", "e"))
            COLS, NCH, WB = 416, 5, 4
            jobs = [(mat, g_, c) for c in range(NCH) for mat in range(2) for g_ in range(2)]
            block = ctx2.enter_context(nc.Block())

            @block.sync
            def _(sp):
                norm.load(sp)
                for m in range(4):
                    sp.dma_start(raw[:, m, :, :], dram(w["w"]["qkvo"[m]][0], w["w"]["qkvo"[m]][1] * DIM,
                                                       [(DIM, HALF), (HALF * DIM, 2), (1, DIM)])).then_inc(s_w, 16)
                n = 4
                for m in range(4):
                    if not second or m == 3:
                        sp.dma_start(WT[HALF:HALF + 1, 1, m, :], dram(w["b"]["qkvo"[m]], 0, [(DIM, 1), (1, DIM)])).then_inc(s_w, 16)
                        n += 1
                if second:
                    with nc.allow_non_contiguous_dma(reason="columns of the norm's gain and bias"):
                        sp.wait_ge(s_c, 1)
                        for kb in range(2):
                            sp.dma_start(bpad[:, kb, HALF:], dram(w["lnb"], HALF * kb, [(1, HALF), (1, 1)])).then_inc(s_w, 16)
                            sp.dma_start(g[:, kb:kb + 1], dram(w["lng"], HALF * kb, [(1, HALF), (1, 1)])).then_inc(s_w, 16)
                    n += 4
                sp.wait_ge(s_w, 16 * n)
                sp.sem_inc(s_b, 1)

            @block.gpsimd
            def _(pool):
                norm.constants(pool)
                nc.gpsimd.memset(mask[:], 1.0).then_inc(s_mask, 1)
                pool.wait_ge(s_mask, 1)
                nc.gpsimd.affine_select(out=mask[:], in_=mask[:], compare_op=ALU.is_ge, fill=0.0, base=0,
                                        pattern=[[-16, HG]], channel_multiplier=1).then_inc(s_mask, 1)
                pool.wait_ge(s_mask, 2)
                nc.gpsimd.affine_select(out=mask[:], in_=mask[:], compare_op=ALU.is_ge, fill=0.0, base=15,
                                        pattern=[[16, HG]], channel_multiplier=-1)
                nc.gpsimd.memset(v1[:, :, 16:], 1.0)
                norm.roots(pool)

            @block.tensor
            def _(pe):
                pe.wait_ge(norm.ident_done, 2)
                pe.wait_ge(s_b, 1)
                for m in range(4):
                    for kb in range(2):
                        for eb in range(2):
                            c = (WB + m) * BANK + (2 * kb + eb) * HALF
                            last = nc.tensor.transpose(ps[0:HALF, c:c + HALF], raw[:, m, eb, HALF * kb:HALF * kb + HALF], ident[0:HALF, 0:HALF])
                    last.then_inc(s_t, 1)
                pe.wait_ge(s_ts, 4)
                if second:
                    for m in range(3):
                        for kb in range(2):
                            last = nc.tensor.matmul(ps[0:HALF + 1, (WB + m) * BANK:(WB + m) * BANK + DIM], bpad[:, kb, :],
                                                    WT[0:HALF, kb, m, :], start=(kb == 0), stop=(kb == 1))
                    last.then_inc(s_t, 1)
                norm.turn(pe)
                if second:
                    pe.wait_ge(s_g, 5)
                for n, (mat, g_, c) in enumerate(jobs):
                    pe.wait_ge(norm.turned, 2 * (c + 1))
                    wait(pe, s_e, n - 3)
                    for kb in range(2):
                        last = nc.tensor.matmul(ps[0:HALF, (WB + n % 4) * BANK:(WB + n % 4) * BANK + COLS], WT[0:HALF + kb, kb, mat, HALF * g_:HALF * g_ + HALF],
                                                xT[0:HALF + kb, kb, COLS * c:COLS * c + COLS], start=(kb == 0), stop=(kb == 1))
                    last.then_inc(s_qk, 1)

            @block.scalar
            def _(act):
                for m in range(4):
                    act.wait_ge(s_t, m + 1)
                    nc.scalar.copy(WT[0:HALF, :, m, :].rearrange("p k (e c) -> p k e c", e=2),
                                   ps[0:HALF, (WB + m) * BANK:(WB + m) * BANK + 384].rearrange("p (k e c) -> p k e c", k=2, e=2)).then_inc(s_ts, 1)
                if second:
                    act.wait_ge(s_t, 5)
                    for m in range(3):
                        nc.scalar.copy(WT[HALF:HALF + 1, 1, m, :], ps[HALF:HALF + 1, (WB + m) * BANK:(WB + m) * BANK + DIM]).then_inc(s_g, 1)
                    for kb in range(2):
                        nc.scalar.activation(WT[0:HALF, kb, 0:3, :], WT[0:HALF, kb, 0:3, :], ACT.Identity, scale=g[:, kb:kb + 1]).then_inc(s_g, 1)
                norm.copy(act)

            @block.vector
            def _(dve):
                if second:
                    nc.vector.memset(bpad[:], 0.0).then_inc(s_c, 1)
                nc.vector.memset(oT[HALF:HALF + 1, :, :], 1.0)
                norm.normalise(dve)
                for n, (mat, g_, c) in enumerate(jobs):
                    dve.wait_ge(s_qk, n + 1)
                    nc.vector.tensor_copy((qT, kT)[mat][:, g_, COLS * c:COLS * c + COLS], ps[0:HALF, (WB + n % 4) * BANK:(WB + n % 4) * BANK + COLS]).then_inc(s_e, 1)

        with ExitStack() as ctx2:
            s2 = Stage(nc, ctx2, name + "_images")
            ps = s2.psum()
            kbd = s2.sbuf("kbd", [HALF, 2, HG, SEQ])
            mx = s2.sbuf("mx", [SEQ, 2, HG])
            rs = s2.sbuf("rs", [SEQ, HEADS])
            S = s2.sbuf("S", [SEQ, 2, HG, SEQ])
            P = s2.sbuf("P", [SEQ, HEADS, SEQ])
            pT = s2.sbuf("pT", [SEQ, HEADS, SEQ])
            names = ("q", "x", "kbd", "sc", "mx", "sub", "exp", "pt", "pts", "v", "vs", "av", "rs", "on", "ot", "ots")
            s = {n: s2.sem(n) for n in names}
            bS = ps[0:SEQ, 0:2 * BANK].rearrange("p (g c) -> p g c", g=2)[:, :, 0:HG * SEQ].rearrange("p g (h k) -> p g h k", h=HG)
            bP = ps[0:SEQ, 2 * BANK:4 * BANK].rearrange("p (g c) -> p g c", g=2)
            bV = ps[0:SEQ, 4 * BANK:4 * BANK + DIM]
            bA = ps[0:SEQ, 5 * BANK:5 * BANK + HEADS * 17].rearrange("p (h c) -> p h c", c=17)
            bO = ps[0:HALF, 6 * BANK:6 * BANK + 2 * SEQ].rearrange("p (k c) -> p k c", k=2)

            def live(i):
                return 0 <= i < IMAGES if isinstance(i, int) else True

            def columns(i):
                return bass.ds(i * SEQ, SEQ)

            def schedule(eng, body):
                for t in range(5):
                    body(t)
                with eng.Fori(5, IMAGES) as t:
                    body(t)
                for t in range(IMAGES, IMAGES + 3):
                    body(t)

            block = ctx2.enter_context(nc.Block())

            @block.gpsimd
            def _(pool):
                def body(t):
                    if live(t):
                        wait(pool, s["sc"], t)
                        nc.gpsimd.tensor_copy(qi[:], qT[:, :, columns(t)]).then_inc(s["q"], 1)
                        wait(pool, s["v"], t)
                        nc.gpsimd.tensor_copy(xi[:], xT[:, :, columns(t)]).then_inc(s["x"], 1)

                schedule(pool, body)

            @block.vector
            def _(dve):
                def body(t):
                    m, k = t - 1, t - 2
                    if live(m):
                        dve.wait_ge(s["sc"], m + 1)
                        nc.vector.reduce_max(mx[:], bS, axis=AX_X).then_inc(s["mx"], 1)
                        dve.wait_ge(s["mx"], m + 1)
                        wait(dve, s["exp"], m)
                        nc.vector.tensor_tensor(S[:], bS, spread(mx[:], 3, SEQ), ALU.subtract).then_inc(s["sub"], 1)
                    if live(t):
                        wait(dve, s["sc"], t)
                        for g_ in range(2):
                            last = nc.vector.tensor_tensor(kbd[:, g_, :, :], spread(kT[:, g_, columns(t)], 1, HG), spread(mask[:], 2, SEQ), ALU.mult)
                        last.then_inc(s["kbd"], 1)
                    if live(k):
                        dve.wait_ge(s["av"], k + 1)
                        nc.vector.reciprocal(rs[:], bA[:, :, 16]).then_inc(s["rs"], 1)
                        dve.wait_ge(s["rs"], k + 1)
                        wait(dve, s["ot"], k)
                        nc.vector.tensor_tensor(on[:].rearrange("p (h c) -> p h c", c=16), bA[:, :, 0:16],
                                                spread(rs[:], 2, 16), ALU.mult).then_inc(s["on"], 1)

                schedule(dve, body)

            @block.scalar
            def _(act):
                def body(t):
                    m, k, l = t - 1, t - 2, t - 3
                    if live(k):
                        act.wait_ge(s["pt"], k + 1)
                        wait(act, s["av"], k)
                        nc.scalar.copy(pT[:].rearrange("p (g h) k -> p g (h k)", g=2), bP[:, :, 0:HG * SEQ]).then_inc(s["pts"], 1)
                    if live(m):
                        act.wait_ge(s["sub"], m + 1)
                        wait(act, s["pt"], m)
                        nc.scalar.activation(P[:].rearrange("p h k -> p (h k)"), S[:].rearrange("p g h k -> p (g h k)"), ACT.Exp,
                                             scale=0.25).then_inc(s["exp"], 1)
                    if live(l):
                        act.wait_ge(s["ot"], l + 1)
                        nc.scalar.copy(oT[0:HALF, :, columns(l)], bO).then_inc(s["ots"], 1)
                    if live(m):
                        act.wait_ge(s["v"], m + 1)
                        wait(act, s["av"], m)
                        nc.scalar.copy(v1[:, :, 0:16], bV.rearrange("p (h c) -> p h c", c=16)).then_inc(s["vs"], 1)

                schedule(act, body)

            @block.tensor
            def _(pe):
                def body(t):
                    m, k, l = t - 1, t - 2, t - 3
                    if live(m):
                        pe.wait_ge(s["kbd"], m + 1)
                        pe.wait_ge(s["q"], m + 1)
                        wait(pe, s["sub"], m)
                        for g_ in range(2):
                            last = nc.tensor.matmul(bS[:, g_, :, :].rearrange("p h k -> p (h k)"), qi[:, g_, :],
                                                    kbd[:, g_, :, :].rearrange("p h k -> p (h k)"), start=True, stop=True)
                        last.then_inc(s["sc"], 1)
                    if live(k):
                        pe.wait_ge(s["exp"], k + 1)
                        wait(pe, s["pts"], k)
                        for h in range(HEADS):
                            c = SEQ * (h % HG)
                            last = nc.tensor.transpose(bP[:, h // HG, c:c + SEQ], P[:, h, :], ident[0:SEQ, 0:SEQ])
                        last.then_inc(s["pt"], 1)
                    if live(m):
                        pe.wait_ge(s["x"], m + 1)
                        wait(pe, s["vs"], m)
                        for kb in range(2):
                            last = nc.tensor.matmul(bV, xi[0:HALF + kb, kb, :], WT[0:HALF + kb, kb, 2, :], start=(kb == 0), stop=(kb == 1))
                        last.then_inc(s["v"], 1)
                    if live(l):
                        pe.wait_ge(s["on"], l + 1)
                        wait(pe, s["ots"], l)
                        for kb in range(2):
                            last = nc.tensor.transpose(bO[:, kb, :], on[:, HALF * kb:HALF * kb + HALF], ident[0:SEQ, 0:SEQ])
                        last.then_inc(s["ot"], 1)
                    if live(k):
                        pe.wait_ge(s["pts"], k + 1)
                        pe.wait_ge(s["vs"], k + 1)
                        wait(pe, s["on"], k)
                        for h in range(HEADS):
                            last = nc.tensor.matmul(bA[:, h, :], pT[:, h, :], v1[:, h, :], start=True, stop=True)
                        last.then_inc(s["av"], 1)

                schedule(pe, body)

        with ExitStack() as ctx2:
            s2 = Stage(nc, ctx2, name + "_last")
            ps = s2.psum()
            s_pr, s_res, s_out = s2.sem("pr"), s2.sem("res"), s2.sem("out")
            block = ctx2.enter_context(nc.Block())

            @block.tensor
            def _(pe):
                for i in range(NTILE):
                    wait(pe, s_res, i - 7)
                    for kb in range(2):
                        last = nc.tensor.matmul(ps[0:TILE, (i % 8) * BANK:(i % 8) * BANK + DIM], oT[0:HALF + kb, kb, TILE * i:TILE * i + TILE],
                                                WT[0:HALF + kb, kb, 3, :], start=(kb == 0), stop=(kb == 1))
                    last.then_inc(s_pr, 1)

            @block.vector
            def _(dve):
                for i in range(NTILE):
                    dve.wait_ge(s_pr, i + 1)
                    nc.vector.tensor_tensor(rows[:, i, :], ps[0:TILE, (i % 8) * BANK:(i % 8) * BANK + DIM], rows[:, i, :], ALU.add).then_inc(s_res, 1)

            @block.sync
            def _(sp):
                per = NTILE // 4
                for q in range(4):
                    sp.wait_ge(s_res, per * (q + 1))
                    sp.dma_start(dram(h_out, q * per * TILE * DIM, [(DIM, TILE), (TILE * DIM, per), (1, DIM)]), rows[:, per * q:per * q + per, :]).then_inc(s_out, 16)
                sp.wait_ge(s_out, 64)

CHUNK, NCHUNK, LANES = 64, 3, TOKENS // 2
STATE = 16


class NormedColumns:
    BANKS = 3
    PER = 4
    COPIES = 2 * (NTILE // PER)

    def __init__(self, nc, st, ps, src, rows, xT, ident, xn, affine=None, twice=False):
        self.nc, self.ps, self.src, self.rows, self.xT, self.ident, self.xn = nc, ps, src, rows, xT, ident, xn
        self.affine, self.rounds = affine, 2 if twice else 1
        self.stats = st.sbuf("norm_stats", [TILE, NTILE, 6])
        self.tmp = st.sbuf("norm_tmp", [TILE, 3, NTILE])
        self.rstd = st.sbuf("norm_rstd", [TILE, NTILE])
        self.mhalf = st.sbuf("norm_mhalf", [TILE, NTILE])
        self.gb = st.sbuf("norm_gb", [HALF, 2, 2])
        self.loaded, self.gains, self.ident_done, self.consts, self.stat, self.moment, self.root, self.normed, self.in_psum, self.turned = (
            st.sem("norm_" + n) for n in ("loaded", "gains", "ident", "consts", "stat", "moment", "root", "normed", "in_psum", "turned"))

    def load(self, sp):
        sp.dma_start(self.rows[:], dram(self.src, 0, [(DIM, TILE), (TILE * DIM, NTILE), (1, DIM)])).then_inc(self.loaded, 16)
        if self.affine:
            with self.nc.allow_non_contiguous_dma(reason="columns of the norm's gain and bias"):
                for n in range(2):
                    for kb in range(2):
                        sp.dma_start(self.gb[:, n, kb:kb + 1], dram(self.affine[n], HALF * kb, [(1, HALF), (1, 1)])).then_inc(self.gains, 16)

    def constants(self, pool):
        make_identity(self.nc, pool, self.ident, self.ident_done)
        self.nc.gpsimd.memset(self.mhalf[:], -0.5).then_inc(self.consts, 1)

    def roots(self, pool):
        pool.wait_ge(self.consts, 1)
        for r in range(self.rounds):
            pool.wait_ge(self.moment, 7 * (r + 1))
            self.nc.gpsimd.tensor_tensor(self.rstd[:], self.tmp[:, 2, :], self.mhalf[:], ALU.pow).then_inc(self.root, 1)

    def normalise(self, dve):
        nc, rows, tmp = self.nc, self.rows, self.tmp
        nc.vector.memset(self.xT[HALF:HALF + 1, :, :], 1.0)
        dve.wait_ge(self.loaded, 16)
        for r in range(self.rounds):
            for i in range(NTILE):
                wait(dve, self.normed, i + 1 if r else 0)
                nc.vector.bn_stats(self.stats[:, i, :], rows[:, i, :]).then_inc(self.stat, 1)
            dve.wait_ge(self.stat, NTILE * (r + 1))
            moments(nc, dve, self.stats[:], [tmp[:, n, :] for n in range(3)], self.moment, 7 * r)
            dve.wait_ge(self.root, r + 1)
            to = self.xn if r == self.rounds - 1 else rows
            for i in range(NTILE):
                nc.vector.tensor_scalar(to[:, i, :], rows[:, i, :], tmp[:, 0, i:i + 1], self.rstd[:, i:i + 1], ALU.subtract, ALU.mult).then_inc(self.normed, 1)

    def turn(self, pe):
        for n in range(self.COPIES):
            g, kb = n // 2, n % 2
            wait(pe, self.turned, n - self.BANKS + 1)
            for j in range(self.PER):
                tile = self.PER * g + j
                pe.wait_ge(self.normed, NTILE * (self.rounds - 1) + tile + 1)
                c = (n % self.BANKS) * BANK + TILE * j
                last = self.nc.tensor.transpose(self.ps[0:HALF, c:c + TILE], self.xn[:, tile, HALF * kb:HALF * kb + HALF], self.ident[0:TILE, 0:TILE])
            last.then_inc(self.in_psum, 1)

    def copy(self, act):
        if self.affine:
            act.wait_ge(self.gains, 64)
        for n in range(self.COPIES):
            g, kb = n // 2, n % 2
            act.wait_ge(self.in_psum, n + 1)
            out = self.xT[0:HALF, kb, self.PER * TILE * g:self.PER * TILE * (g + 1)]
            got = self.ps[0:HALF, (n % self.BANKS) * BANK:(n % self.BANKS) * BANK + self.PER * TILE]
            if self.affine:
                self.nc.scalar.activation(out, got, ACT.Identity, scale=self.gb[:, 0, kb:kb + 1], bias=self.gb[:, 1, kb:kb + 1]).then_inc(self.turned, 1)
            else:
                self.nc.scalar.copy(out, got).then_inc(self.turned, 1)


def state_space(nc, name, h_in, h_out, abc, w):
    GROUP = 4 * SEQ
    groups = TOKENS // GROUP
    NL1 = 11
    with ExitStack() as ctx:
        st = Stage(nc, ctx, name)
        rows = st.sbuf("rows", [TILE, NTILE, DIM])
        delta = st.sbuf("delta", [PARTS, NCHUNK, LANES])
        u = st.sbuf("u", [PARTS, NCHUNK, LANES])
        dt = st.sbuf("dt", [PARTS, NCHUNK])
        mdt = st.sbuf("mdt", [PARTS, NCHUNK])
        ident = st.sbuf("ident", [PARTS, PARTS])
        diag = st.sbuf("diag", [PARTS, NCHUNK, PARTS])
        with ExitStack() as ctx2:
            s2 = Stage(nc, ctx2, name + "_mlp")
            xT = s2.sbuf("xT", [HALF + 1, 2, TOKENS])
            W1 = s2.sbuf("W1", [HALF + 1, 2, 1344])
            W2 = s2.sbuf("W2", [PARTS, 9, HALF])
            W2d = s2.sbuf("W2d", [HALF, 2, DIM])
            b2 = s2.sbuf("b2", [HALF, 1])
            b2d = s2.sbuf("b2d", [PARTS, NCHUNK])
            Dc = s2.sbuf("D", [PARTS, NCHUNK])
            ldt = s2.sbuf("ldt", [PARTS, NCHUNK])
            hid = [s2.sbuf(f"hid{p}", [PARTS, NL1, GROUP]) for p in range(2)]
            ABC = s2.sbuf("ABC", [HALF, TOKENS])
            xn = s2.sbuf("xn", [TILE, NTILE, DIM])
            ps = s2.psum()
            norm = NormedColumns(nc, s2, ps, h_in, rows, xT, ident, xn)
            s_w, s_z, s_l1, s_act, s_l2, s_e2, s_u, s_abc, s_dt, s_dg, s_c = (
                s2.sem(n) for n in ("w", "z", "l1", "act", "l2", "e2", "u", "abc", "dt", "dg", "c"))
            block = ctx2.enter_context(nc.Block())
            NB2 = 6
            wload = [0]

            @block.sync
            def _(sp):
                ctx2.enter_context(nc.allow_non_contiguous_dma(reason="columns of biases"))
                norm.load(sp)
                n = 0
                sp.wait_ge(s_z, 1)
                c = 0
                for m in "ABCd":
                    wide = DIM if m == "d" else 2 * DIM
                    sp.dma_start(W1[0:HALF, :, c:c + wide], dram(w[m + "_w1"], 0, [(wide, HALF), (HALF * wide, 2), (1, wide)])).then_inc(s_w, 16)
                    sp.dma_start(W1[HALF:HALF + 1, 1, c:c + wide], dram(w[m + "_b1"], 0, [(wide, 1), (1, wide)])).then_inc(s_w, 16)
                    c += wide
                    n += 2
                for i, m in enumerate("ABC"):
                    sp.dma_start(W2[:, 3 * i:3 * i + 3, 32 * i:32 * i + STATE], dram(w[m + "_w2"], 0, [(STATE, PARTS), (PARTS * STATE, 3), (1, STATE)])).then_inc(s_w, 16)
                    sp.dma_start(b2[32 * i:32 * i + STATE, :], dram(w[m + "_b2"], 0, [(1, STATE), (1, 1)])).then_inc(s_w, 16)
                    n += 2
                sp.dma_start(W2d[:], dram(w["d_w2"], 0, [(DIM, HALF), (HALF * DIM, 2), (1, DIM)])).then_inc(s_w, 16)
                n += 1
                for half in range(2):
                    p = slice(CHUNK * half, CHUNK * half + CHUNK)
                    for to, frm in ((b2d, "d_b2"), (Dc, "D_param"), (ldt, "log_dt")):
                        sp.dma_start(to[p, :].unsqueeze(2), dram(w[frm], 0, [(1, CHUNK), (CHUNK, NCHUNK), (1, 1)])).then_inc(s_w, 16)
                        n += 1
                sp.wait_ge(s_w, 16 * n)
                sp.sem_inc(s_c, 1)
                sp.wait_ge(norm.turned, norm.COPIES)
                for half in range(2):
                    for c in range(NCHUNK):
                        d = c * CHUNK
                        while d < (c + 1) * CHUNK:
                            kb, r = divmod(d, HALF)
                            k = min((c + 1) * CHUNK - d, HALF - r)
                            p0 = CHUNK * half + d - c * CHUNK
                            sp.dma_start(u[p0:p0 + k, c, :], xT[r:r + k, kb, LANES * half:LANES * half + LANES]).then_inc(s_u, 16)
                            d += k
                sp.wait_ge(s_e2, NB2 * groups)
                for i in range(3):
                    sp.dma_start(dram(abc, i * STATE * TOKENS, [(TOKENS, STATE), (1, TOKENS)]), ABC[32 * i:32 * i + STATE, :]).then_inc(s_abc, 16)
                sp.wait_ge(s_abc, 48)
                sp.wait_ge(s_u, 16 * 8)

            @block.gpsimd
            def _(pool):
                nc.gpsimd.memset(W2[:], 0.0).then_inc(s_z, 1)
                norm.constants(pool)
                norm.roots(pool)

            @block.vector
            def _(dve):
                norm.normalise(dve)
                dve.wait_ge(s_dt, 1)
                nc.vector.tensor_scalar(mdt[:], dt[:], -1.0, None, ALU.mult)
                dve.wait_ge(norm.ident_done, 2)
                for c in range(NCHUNK):
                    nc.vector.tensor_scalar(diag[:, c, :], ident[:], Dc[:, c:c + 1], None, ALU.mult).then_inc(s_dg, 1)

            def l1(ft):
                return (PARTS * ft, PARTS) if ft < 9 else (9 * PARTS + HALF * (ft - 9), HALF)

            @block.tensor
            def _(pe):
                pe.wait_ge(norm.ident_done, 2)
                norm.turn(pe)
                pe.wait_ge(norm.turned, norm.COPIES)
                pe.wait_ge(s_c, 1)

                def layer2(g):
                    half = g // (groups // 2)
                    pe.wait_ge(s_act, NL1 * (g + 1))
                    wait(pe, s_e2, NB2 * g)
                    for ft in range(9):
                        last = nc.tensor.matmul(ps[0:HALF, 4 * BANK:4 * BANK + GROUP], W2[:, ft, :], hid[g % 2][:, ft, :],
                                                start=(ft == 0), stop=(ft == 8))
                    last.then_inc(s_l2, 1)
                    p = slice(CHUNK * half, CHUNK * half + CHUNK)
                    for c in range(NCHUNK):
                        for kb in range(2):
                            last = nc.tensor.matmul(ps[p, (5 + c) * BANK:(5 + c) * BANK + GROUP], W2d[:, kb, CHUNK * c:CHUNK * c + CHUNK],
                                                    hid[g % 2][0:HALF, 9 + kb, :], start=(kb == 0), stop=(kb == 1))
                        last.then_inc(s_l2, 1)

                for g in range(groups):
                    for ft in range(NL1):
                        c0, rows_ = l1(ft)
                        n = NL1 * g + ft
                        wait(pe, s_act, n - 3)
                        for kb in range(2):
                            k = HALF + kb
                            last = nc.tensor.matmul(ps[0:rows_, (n % 4) * BANK:(n % 4) * BANK + GROUP], W1[0:k, kb, c0:c0 + rows_],
                                                    xT[0:k, kb, GROUP * g:GROUP * g + GROUP], start=(kb == 0), stop=(kb == 1))
                        last.then_inc(s_l1, 1)
                    if g >= 1:
                        layer2(g - 1)
                layer2(groups - 1)

            @block.scalar
            def _(act):
                norm.copy(act)
                act.wait_ge(s_c, 1)
                nc.scalar.activation(dt[:], ldt[:], ACT.Exp).then_inc(s_dt, 1)

                def evacuate2(g):
                    half = g // (groups // 2)
                    cols = slice(GROUP * g, GROUP * g + GROUP)
                    act.wait_ge(s_l2, 4 * g + 1)
                    for i in range(3):
                        p = slice(32 * i, 32 * i + STATE)
                        nc.scalar.activation(ABC[p, cols], ps[p, 4 * BANK:4 * BANK + GROUP], ACT.Abs if i == 0 else ACT.Identity,
                                             bias=b2[p, 0:1]).then_inc(s_e2, 1)
                    p = slice(CHUNK * half, CHUNK * half + CHUNK)
                    here = slice(GROUP * (g % (groups // 2)), GROUP * (g % (groups // 2) + 1))
                    for c in range(NCHUNK):
                        act.wait_ge(s_l2, 4 * g + 2 + c)
                        nc.scalar.activation(delta[p, c, here], ps[p, (5 + c) * BANK:(5 + c) * BANK + GROUP], ACT.Identity,
                                             bias=b2d[p, c:c + 1]).then_inc(s_e2, 1)

                for g in range(groups):
                    for ft in range(NL1):
                        _, rows_ = l1(ft)
                        n = NL1 * g + ft
                        act.wait_ge(s_l1, n + 1)
                        if g >= 2 and ft == 0:
                            act.wait_ge(s_l2, 4 * (g - 1))
                        nc.scalar.activation(hid[g % 2][0:rows_, ft, :], ps[0:rows_, (n % 4) * BANK:(n % 4) * BANK + GROUP],
                                             ACT.Silu).then_inc(s_act, 1)
                    if g >= 1:
                        evacuate2(g - 1)
                evacuate2(groups - 1)
                act.wait_ge(s_e2, NB2 * groups)
                nc.scalar.activation(delta[:].rearrange("p c t -> p (c t)"), delta[:].rearrange("p c t -> p (c t)"), ACT.Sigmoid)

        with ExitStack() as ctx2:
            s2 = Stage(nc, ctx2, name + "_scan")
            ps = s2.psum()
            bc = [s2.sbuf(f"bc{p}", [PARTS, 3, LANES]) for p in range(2)]
            gain = s2.sbuf("gain", [PARTS, NCHUNK, LANES])
            dA = [s2.sbuf(f"dA{p}", [PARTS, LANES]) for p in range(2)]
            wb = [s2.sbuf(f"wb{p}", [PARTS, LANES]) for p in range(2)]
            coef = [s2.sbuf(f"coef{p}", [PARTS, LANES]) for p in range(2)]
            inp = [s2.sbuf(f"inp{p}", [PARTS, LANES]) for p in range(2)]
            S = [s2.sbuf(f"S{p}", [PARTS, LANES]) for p in range(2)]
            prod = [s2.sbuf(f"prod{p}", [PARTS, LANES]) for p in range(2)]
            s_bc = [s2.sem(f"bc{p}") for p in range(2)]
            s_g, s_d0, s_da, s_w, s_wd, s_coef, s_inp, s_scan, s_prod, s_acc, s_ys, s_t, s_res, s_out, s_ld = (
                s2.sem(n) for n in ("g", "d0", "da", "w", "wd", "coef", "inp", "scan", "prod", "acc", "ys", "t", "res", "out", "ld"))
            yS = gain

            def pieces(c):
                at = c * LANES
                while at < (c + 1) * LANES:
                    to = min((c + 1) * LANES, (at // BANK + 1) * BANK)
                    yield at, to
                    at = to

            def schedule(eng, body, tail=0):
                for n in range(4):
                    body(n, n % 2)
                with eng.Fori(4, STATE, 2) as n:
                    body(n, 0)
                    body(n + 1, 1)

            block = ctx2.enter_context(nc.Block())

            @block.sync
            def _(sp):
                def body(n, p):
                    wait(sp, s_prod, 3 * (n - 1))
                    sp.sem_inc(s_ld, 1)
                    for i in range(3):
                        sp.dma_start(bc[p][:, i, :], dram(abc, (i * STATE + n) * TOKENS, [(LANES, 2), (0, CHUNK), (1, LANES)])).then_inc(s_bc[p], 16)

                schedule(sp, body)
                sp.wait_ge(s_res, 10)
                sp.dma_start(dram(h_out, 0, [(DIM, TILE), (TILE * DIM, NTILE), (1, DIM)]), rows[:]).then_inc(s_out, 16)
                sp.wait_ge(s_out, 16)

            def loaded(eng, n, p):
                eng.wait_ge(s_bc[p], 48 * (n - p + 2) // 2 if isinstance(n, int) else (n - p) * 24 + 48)

            @block.scalar
            def _(act):
                def body(n, p):
                    loaded(act, n, p)
                    for c in range(NCHUNK):
                        j = 3 * n + c
                        q = (3 * p + c) % 2
                        wait(act, s_inp, j - 1)
                        nc.scalar.activation(dA[q][:], bc[p][:, 0, :], ACT.Exp, scale=mdt[:, c:c + 1]).then_inc(s_da, 1)

                schedule(act, body)
                act.wait_ge(s_acc, 3 * STATE)
                for c in range(NCHUNK):
                    nc.scalar.copy(yS[:, c, :], ps[:, LANES * c:LANES * c + LANES]).then_inc(s_ys, 1)

            @block.gpsimd
            def _(pool):
                def prods(j, p, q):
                    pool.wait_ge(s_scan, j + 1)
                    wait(pool, s_acc, j - 1)
                    nc.gpsimd.tensor_tensor(prod[q][:], S[q][:], bc[p][:, 2, :], ALU.mult).then_inc(s_prod, 1)

                pool.wait_ge(s_g, 5)

                def body(n, p):
                    loaded(pool, n, p)
                    for c in range(NCHUNK):
                        j = 3 * n + c
                        q = (3 * p + c) % 2
                        if c < NCHUNK - 1:
                            wait(pool, s_inp, j - 1)
                            nc.gpsimd.tensor_tensor(wb[q][:], gain[:, c, :], bc[p][:, 1, :], ALU.mult).then_inc(s_w, 1)
                        if not isinstance(n, int) or j >= 1:
                            prods(j - 1, p if c else 1 - p, 1 - q)

                schedule(pool, body)
                prods(3 * STATE - 1, 1, (3 * STATE - 1) % 2)

            @block.vector
            def _(dve):
                nc.vector.tensor_scalar(gain[:], delta[:], -1.0, 1.0, ALU.mult, ALU.add).then_inc(s_g, 1)
                dve.wait_ge(s_g, 1)
                nc.vector.tensor_tensor(gain[:], gain[:], u[:], ALU.mult).then_inc(s_g, 1)
                dve.wait_ge(s_g, 2)
                for c in range(NCHUNK):
                    nc.vector.tensor_scalar(gain[:, c, :], gain[:, c, :], dt[:, c:c + 1], None, ALU.mult).then_inc(s_g, 1)
                nc.vector.memset(delta[:].rearrange("p c (b l) -> p (c b) l", l=SEQ)[:, :, 0:1], 0.0).then_inc(s_d0, 1)
                dve.wait_ge(s_d0, 1)

                def body(n, p):
                    for c in range(NCHUNK):
                        j = 3 * n + c
                        q = (3 * p + c) % 2
                        dve.wait_ge(s_da, j + 1)
                        wait(dve, s_scan, j - 1)
                        nc.vector.tensor_tensor(coef[q][:], delta[:, c, :], dA[q][:], ALU.mult).then_inc(s_coef, 1)
                        if c < NCHUNK - 1:
                            dve.wait_ge(s_w, (NCHUNK - 1) * n + c + 1)
                        else:
                            loaded(dve, n, p)
                            nc.vector.tensor_tensor(wb[q][:], gain[:, c, :], bc[p][:, 1, :], ALU.mult).then_inc(s_wd, 1)
                            dve.wait_ge(s_wd, n + 1)
                        nc.vector.tensor_tensor(inp[q][:], wb[q][:], dA[q][:], ALU.mult).then_inc(s_inp, 1)
                        dve.wait_ge(s_coef, j + 1)
                        dve.wait_ge(s_inp, j + 1)
                        wait(dve, s_prod, j - 1)
                        nc.vector.tensor_tensor_scan(S[q][:], coef[q][:], inp[q][:], 0.0, ALU.mult, ALU.add).then_inc(s_scan, 1)

                schedule(dve, body)
                for t in range(10):
                    dve.wait_ge(s_t, t + 1)
                    out = rows[:, t::10, :].rearrange("p h (c d) -> p c h d", c=NCHUNK)
                    nc.vector.tensor_tensor(out, ps[0:TILE, (t % 8) * BANK:(t % 8) * BANK + 384].rearrange("p (c h d) -> p c h d", c=NCHUNK, h=2),
                                            out, ALU.add).then_inc(s_res, 1)

            @block.tensor
            def _(pe):
                begun = set()
                for c in range(NCHUNK):
                    for a, b in pieces(c):
                        nc.tensor.matmul(ps[:, a:b], diag[:, c, :], u[:, c, a - LANES * c:b - LANES * c], start=(a // BANK not in begun),
                                         stop=True, skip_group_check=True)
                        begun.add(a // BANK)

                def body(n, p):
                    for c in range(NCHUNK):
                        j = 3 * n + c
                        q = (3 * p + c) % 2
                        pe.wait_ge(s_prod, j + 1)
                        for a, b in pieces(c):
                            last = nc.tensor.matmul(ps[:, a:b], ident[:], prod[q][:, a - LANES * c:b - LANES * c], start=False, stop=True,
                                                    skip_group_check=True)
                        last.then_inc(s_acc, 1)

                schedule(pe, body)
                pe.wait_ge(s_ys, 3)
                for t in range(10):
                    wait(pe, s_res, t - 7)
                    for c in range(NCHUNK):
                        last = nc.tensor.transpose(ps[0:TILE, (t % 8) * BANK + PARTS * c:(t % 8) * BANK + PARTS * c + PARTS],
                                                   yS[:, c, TILE * t:TILE * t + TILE], ident[:])
                    last.then_inc(s_t, 1)


EXPERTS = 8


def experts(nc, name, a_in, base, h_out, xs, ys, w, gated):
    slots = 1 if gated else 2
    ntiles = (slots * TOKENS + PARTS - 1) // PARTS + EXPERTS - 1
    ntiles += ntiles % 2
    hidden = 469 if gated else 768
    fts = [(c, min(PARTS, hidden - c)) for c in range(0, hidden, PARTS)]
    nft = len(fts)
    wide = 2 * hidden if gated else hidden
    cut = hidden if gated else hidden // 2
    with ExitStack() as ctx:
        st = Stage(nc, ctx, name)
        rows = st.sbuf("rows", [TILE, NTILE, DIM])
        pos = [st.sbuf(f"pos{k}", [TILE, NTILE], U32) for k in range(slots)]
        score = [st.sbuf(f"score{k}", [TILE, NTILE]) for k in range(slots)]
        texp = st.sbuf("texp", [1, ntiles], I32)
        ident = st.sbuf("ident", [PARTS, PARTS])
        W1 = st.sbuf("W1", [HALF + 1, 2, EXPERTS, wide])
        W2 = st.sbuf("W2", [PARTS, nft, EXPERTS, DIM])
        B2 = None if gated else st.sbuf("B2", [PARTS, EXPERTS, DIM])

        with ExitStack() as ctx2:
            s2 = Stage(nc, ctx2, name + "_route")
            xT = s2.sbuf("xT", [HALF + 1, 2, TOKENS])
            xn = s2.sbuf("xn", [TILE, NTILE, DIM])
            ps = s2.psum()
            norm = NormedColumns(nc, s2, ps, a_in, rows, xT, ident, xn, None if gated else (w["lng"], w["lnb"]))
            zeros = s2.sbuf("zeros", [PARTS, 4 * DIM])
            graw = s2.sbuf("graw", [EXPERTS, DIM + 1])
            GT = s2.sbuf("GT", [HALF + 1, 2, EXPERTS])
            L = s2.sbuf("L", [TILE, NTILE, EXPERTS])
            best = [s2.sbuf(f"best{k}", [TILE, NTILE]) for k in range(slots)]
            OH = [s2.sbuf(f"OH{k}", [TILE, NTILE, EXPERTS]) for k in range(slots)]
            both = s2.sbuf("both", [TILE, NTILE, EXPERTS])
            key = s2.sbuf("key", [TILE, NTILE, EXPERTS])
            top = s2.sbuf("top", [TILE, NTILE])
            order_i, order = s2.sbuf("order_i", [TILE, EXPERTS], I32), s2.sbuf("order", [TILE, EXPERTS])
            NTH = TOKENS // PARTS + 1
            thr_i, thr = s2.sbuf("thr_i", [TILE, NTH], I32), s2.sbuf("thr", [TILE, NTH])
            tn_i, tn = s2.sbuf("tn_i", [1, ntiles], I32), s2.sbuf("tn", [1, ntiles])
            upper = s2.sbuf("upper", [TILE, TILE])
            ones = s2.sbuf("ones", [TILE, TILE])
            chain0 = s2.sbuf("chain0", [TILE, EXPERTS, NTILE])
            tot = s2.sbuf("tot", [TILE, EXPERTS, NTILE])
            incl = s2.sbuf("incl", [TILE, EXPERTS, NTILE])
            over = s2.sbuf("over", [TILE, EXPERTS, NTH])
            nt, ntin = s2.sbuf("nt", [TILE, EXPERTS]), s2.sbuf("ntin", [TILE, EXPERTS])
            start = s2.sbuf("start", [TILE, EXPERTS])
            place = s2.sbuf("place", [TILE, NTILE, EXPERTS])
            pf = s2.sbuf("pf", [TILE, NTILE])
            tge = s2.sbuf("tge", [1, ntiles, EXPERTS])
            te = s2.sbuf("te", [1, ntiles])
            s_g, s_fill, s_zero, s_gt, s_gts, s_lg, s_cst, s_v, s_oh, s_rank, s_pos, s_exp, s_sc, s_up = (
                s2.sem(n) for n in ("g", "fill", "zero", "gt", "gts", "lg", "cst", "v", "oh", "rank", "pos", "exp", "sc", "up"))
            parts1 = 2 if gated else 1
            raw1 = [s2.sbuf(f"raw1{p}", [PARTS, parts1, nft, DIM]) for p in range(2)]
            raw2 = [s2.sbuf(f"raw2{p}", [HALF, 2, hidden]) for p in range(2)]
            s_in = [s2.sem(f"in{p}") for p in range(2)]
            s_b, s_t, s_e, s_gate = s2.sem("b"), s2.sem("t"), s2.sem("e"), s2.sem("gate")
            whole = hidden // PARTS
            left = hidden - whole * PARTS
            jobs = []
            for part in range(parts1):
                for kb in range(2):
                    for f0 in range(0, nft, 4):
                        jobs.append((1, part, kb, fts[f0:f0 + 4]))
            for f0, (c0, k) in enumerate(fts):
                jobs.append((2, f0, 0, [(c0, k)]))
            njobs = len(jobs)
            nbanks = njobs // 2
            ndma = (parts1 * (2 if left else 1)) + 1

            def first_experts(body):
                body(0, 0)
                body(1, 1)

            def other_experts(eng, body, between=None):
                body(2, 0)
                if between:
                    between()
                body(3, 1)
                with eng.Fori(4, EXPERTS - 1, 2) as e:
                    body(e, 0)
                    body(e + 1, 1)

            block = ctx2.enter_context(nc.Block())

            @block.sync
            def _(sp):
                norm.load(sp)
                with nc.allow_non_contiguous_dma(reason="eight biases"):
                    sp.dma_start(graw[:, 0:DIM], w["gate_w"]).then_inc(s_g, 16)
                    sp.dma_start(graw[:, DIM:], dram(w["gate_b"], 0, [(1, EXPERTS), (1, 1)])).then_inc(s_g, 16)
                if not gated:
                    sp.dma_start(W1[HALF:HALF + 1, 1, :, :].rearrange("p e c -> p (e c)"), dram(w["b1"], 0, [(EXPERTS * hidden, 1), (1, EXPERTS * hidden)])).then_inc(s_b, 16)
                    sp.dma_start(B2[:].rearrange("p e c -> p (e c)"), dram(w["b2"], 0, [(0, PARTS), (1, EXPERTS * DIM)])).then_inc(s_b, 16)

                def body(e, p):
                    wait(sp, s_t, njobs * (e - 1))
                    sp.sem_inc(s_gate, 1)
                    for part in range(parts1):
                        frm = w["w1"][part]
                        sp.dma_start(raw1[p][:, part, 0:whole, :], dram(frm, e * (hidden * DIM), [(DIM, PARTS), (PARTS * DIM, whole), (1, DIM)])).then_inc(s_in[p], 16)
                        if left:
                            sp.dma_start(raw1[p][0:left, part, whole, :], dram(frm, e * (hidden * DIM) + whole * PARTS * DIM, [(DIM, left), (1, DIM)])).then_inc(s_in[p], 16)
                    sp.dma_start(raw2[p][:], dram(w["w2"], e * (hidden * DIM), [(hidden, HALF), (HALF * hidden, 2), (1, hidden)])).then_inc(s_in[p], 16)

                first_experts(body)
                sp.wait_ge(s_zero, 1)
                for n in range(0, ntiles, 4):
                    sp.dma_start(dram(xs, n * PARTS * DIM, [(4 * DIM, PARTS), (1, 4 * DIM)]), zeros[:]).then_inc(s_fill, 16)
                other_experts(sp, body)
                if not gated:
                    sp.wait_ge(s_b, 32)
                sp.wait_ge(s_fill, 16 * (ntiles // 4))

            @block.gpsimd
            def _(pool):
                norm.constants(pool)
                nc.gpsimd.iota(order_i[:], pattern=[[-1, EXPERTS]], base=EXPERTS, channel_multiplier=0)
                nc.gpsimd.iota(thr_i[:], pattern=[[PARTS, NTH]], base=0, channel_multiplier=0)
                nc.gpsimd.iota(tn_i[:], pattern=[[1, ntiles]], base=0, channel_multiplier=0).then_inc(s_cst, 1)
                pool.wait_ge(s_cst, 1)
                nc.gpsimd.memset(upper[:], 1.0).then_inc(s_up, 1)
                nc.gpsimd.memset(ones[:], 1.0)
                pool.wait_ge(s_up, 1)
                nc.gpsimd.affine_select(out=upper[:], in_=upper[:], compare_op=ALU.is_gt, fill=0.0, base=0,
                                        pattern=[[1, TILE]], channel_multiplier=-1).then_inc(s_up, 1)
                norm.roots(pool)
                pool.wait_ge(s_fill, 16 * (ntiles // 4))
                for k in range(slots):
                    pool.wait_ge(s_pos, k + 1)
                    for i in range(NTILE):
                        nc.gpsimd.indirect_dma_start(out=xs, out_offset=bass.IndirectOffsetOnAxis(ap=pos[k][:, i:i + 1], axis=0),
                                                     in_=xn[:, i, :], in_offset=None).then_inc(s_sc, 16)
                pool.wait_ge(s_sc, 16 * NTILE * slots)

            @block.tensor
            def _(pe):
                def body(e, p):
                    pe.wait_ge(s_in[p], 16 * ndma * (e - p + 2) // 2 if isinstance(e, int) else (e - p) * (8 * ndma) + 16 * ndma)
                    for n, (kind, a, kb, ts) in enumerate(jobs):
                        wait(pe, s_e, njobs * e + n - (nbanks - 1))
                        b = (3 + n % nbanks) * BANK
                        if kind == 1:
                            for f, (c0, k) in enumerate(ts):
                                last = nc.tensor.transpose(ps[0:HALF, b + PARTS * f:b + PARTS * f + k],
                                                           raw1[p][0:k, a, c0 // PARTS, HALF * kb:HALF * kb + HALF], ident[0:k, 0:k])
                        else:
                            c0, k = ts[0]
                            for h in range(2):
                                last = nc.tensor.transpose(ps[0:k, b + HALF * h:b + HALF * h + HALF], raw2[p][:, h, c0:c0 + k], ident[0:HALF, 0:HALF])
                        last.then_inc(s_t, 1)

                pe.wait_ge(norm.ident_done, 2)
                first_experts(body)
                norm.turn(pe)
                pe.wait_ge(norm.turned, norm.COPIES)
                pe.wait_ge(s_g, 32)
                for kb in range(2):
                    last = nc.tensor.transpose(ps[0:HALF + kb, kb * EXPERTS:(kb + 1) * EXPERTS], graw[:, HALF * kb:HALF * kb + HALF + kb],
                                               ident[0:EXPERTS, 0:EXPERTS])
                last.then_inc(s_gt, 1)
                pe.wait_ge(s_gts, 1)
                for i in range(NTILE):
                    for kb in range(2):
                        last = nc.tensor.matmul(ps[0:TILE, 2 * EXPERTS + EXPERTS * i:2 * EXPERTS + EXPERTS * i + EXPERTS],
                                                xT[0:HALF + kb, kb, TILE * i:TILE * i + TILE], GT[0:HALF + kb, kb, :], start=(kb == 0), stop=(kb == 1))
                last.then_inc(s_lg, 1)

                def rank():
                    pe.wait_ge(s_oh, 1)
                    pe.wait_ge(s_up, 2)
                    flat = both[:].rearrange("p t e -> p (t e)")
                    nc.tensor.matmul(ps[0:TILE, BANK:BANK + NTILE * EXPERTS], upper[:], flat, start=True, stop=True)
                    nc.tensor.matmul(ps[0:TILE, BANK + 256:BANK + 256 + NTILE * EXPERTS], ones[:], flat, start=True, stop=True).then_inc(s_rank, 1)

                other_experts(pe, body, rank)

            @block.vector
            def _(dve):
                count = [0]

                def link(ins):
                    count[0] += 1
                    ins.then_inc(s_v, 1)
                    dve.wait_ge(s_v, count[0])

                nc.vector.memset(zeros[:], 0.0).then_inc(s_zero, 1)
                norm.normalise(dve)
                nc.vector.memset(chain0[:], 1.0)
                link(nc.vector.memset(start[:], 1.0))
                link(nc.vector.memset(chain0[:, :, 0:1], 0.0))
                dve.wait_ge(s_cst, 1)
                nc.vector.tensor_copy(order[:], order_i[:])
                nc.vector.tensor_copy(thr[:], thr_i[:])
                link(nc.vector.tensor_copy(tn[:], tn_i[:]))
                dve.wait_ge(s_gt, 1)
                nc.vector.tensor_copy(GT[0:HALF, 0, :], ps[0:HALF, 0:EXPERTS])
                nc.vector.tensor_copy(GT[:, 1, :], ps[0:HALF + 1, EXPERTS:2 * EXPERTS]).then_inc(s_gts, 1)
                dve.wait_ge(s_lg, 1)
                link(nc.vector.tensor_copy(L[:].rearrange("p t e -> p (t e)"), ps[0:TILE, 2 * EXPERTS:2 * EXPERTS + NTILE * EXPERTS]))
                for k in range(slots):
                    link(nc.vector.reduce_max(best[k][:], L[:], axis=AX_X))
                    link(nc.vector.tensor_tensor(key[:], L[:], spread(best[k][:], 2, EXPERTS), ALU.is_equal))
                    link(nc.vector.tensor_tensor(key[:], key[:], spread(order[:], 1, NTILE), ALU.mult))
                    link(nc.vector.reduce_max(top[:], key[:], axis=AX_X))
                    link(nc.vector.tensor_tensor(OH[k][:], key[:], spread(top[:], 2, EXPERTS), ALU.is_equal))
                    if k + 1 < slots:
                        link(nc.vector.scalar_tensor_tensor(L[:].rearrange("p t e -> p (t e)"), OH[k][:].rearrange("p t e -> p (t e)"), -3.0e38,
                                                            L[:].rearrange("p t e -> p (t e)"), ALU.mult, ALU.add))
                if slots == 2:
                    nc.vector.tensor_tensor(both[:], OH[0][:], OH[1][:], ALU.add).then_inc(s_oh, 1)
                    link(nc.vector.tensor_tensor(score[1][:], best[1][:], best[0][:], ALU.subtract))
                else:
                    nc.vector.tensor_copy(both[:], OH[0][:]).then_inc(s_oh, 1)
                dve.wait_ge(s_rank, 1)
                link(nc.vector.tensor_copy(tot[:].rearrange("p e t -> p t e"), ps[0:TILE, BANK + 256:BANK + 256 + NTILE * EXPERTS].rearrange("p (t e) -> p t e", e=EXPERTS)))
                link(nc.vector.tensor_tensor_scan(incl[:].rearrange("p e t -> p (e t)"), chain0[:].rearrange("p e t -> p (e t)"),
                                                  tot[:].rearrange("p e t -> p (e t)"), 0.0, ALU.mult, ALU.add))
                link(nc.vector.tensor_tensor(over[:], spread(incl[:, :, NTILE - 1], 2, NTH), spread(thr[:], 1, EXPERTS), ALU.is_gt))
                link(nc.vector.reduce_sum(nt[:], over[:], axis=AX_X))
                link(nc.vector.tensor_tensor_scan(ntin[:], start[:], nt[:], 0.0, ALU.mult, ALU.add))
                link(nc.vector.tensor_tensor(start[:], ntin[:], nt[:], ALU.subtract))
                link(nc.vector.tensor_scalar(start[:], start[:], float(PARTS), None, ALU.mult))
                link(nc.vector.tensor_tensor(incl[:], incl[:], tot[:], ALU.subtract))
                link(nc.vector.tensor_tensor(place[:], spread(start[:], 1, NTILE), incl[:].rearrange("p e t -> p t e"), ALU.add))
                link(nc.vector.tensor_tensor(place[:], place[:], ps[0:TILE, BANK:BANK + NTILE * EXPERTS].rearrange("p (t e) -> p t e", e=EXPERTS), ALU.add))
                for k in range(slots):
                    link(nc.vector.tensor_tensor(key[:], place[:], OH[k][:], ALU.mult))
                    link(nc.vector.reduce_sum(pf[:], key[:], axis=AX_X))
                    nc.vector.tensor_copy(pos[k][:], pf[:]).then_inc(s_pos, 1)
                    dve.wait_ge(s_pos, k + 1)
                link(nc.vector.tensor_tensor(tge[:], spread(tn[:], 2, EXPERTS), spread(ntin[0:1, :], 1, ntiles), ALU.is_ge))
                link(nc.vector.reduce_sum(te[:], tge[:], axis=AX_X))
                link(nc.vector.tensor_scalar(te[:], te[:], float(EXPERTS - 1), None, ALU.min))
                nc.vector.tensor_copy(texp[:], te[:])
                if slots == 2:
                    dve.wait_ge(s_exp, 1)
                    link(nc.vector.tensor_scalar(score[0][:], score[1][:], 1.0, None, ALU.add))
                    link(nc.vector.reciprocal(score[0][:], score[0][:]))
                    link(nc.vector.tensor_tensor(score[1][:], score[1][:], score[0][:], ALU.mult))

            @block.scalar
            def _(act):
                def body(e, p):
                    for n, (kind, a, kb, ts) in enumerate(jobs):
                        act.wait_ge(s_t, njobs * e + n + 1)
                        b = (3 + n % nbanks) * BANK
                        if kind == 1:
                            c0 = a * hidden + ts[0][0]
                            k = sum(x[1] for x in ts)
                            to = W1[0:HALF, kb, bass.ds(e, 1), c0:c0 + k].rearrange("p a c -> p (a c)")
                            nc.scalar.copy(to, ps[0:HALF, b:b + k]).then_inc(s_e, 1)
                        else:
                            k = ts[0][1]
                            to = W2[0:k, a, bass.ds(e, 1), :].rearrange("p a c -> p (a c)")
                            nc.scalar.copy(to, ps[0:k, b:b + DIM]).then_inc(s_e, 1)

                first_experts(body)
                norm.copy(act)
                other_experts(act, body)
                if slots == 2:
                    act.wait_ge(s_rank, 1)
                    act.wait_ge(s_oh, 1)
                    act.wait_ge(s_pos, 1)
                    nc.scalar.activation(score[1][:], score[1][:], ACT.Exp).then_inc(s_exp, 1)

        with ExitStack() as ctx2:
            s2 = Stage(nc, ctx2, name + "_tiles")
            ps = s2.psum()
            X = [s2.sbuf(f"X{p}", [PARTS, DIM]) for p in range(2)]
            XT = s2.sbuf("XT", [HALF + 1, 2, PARTS])
            G = s2.sbuf("G", [PARTS, hidden])
            act_out = s2.sbuf("act_out", [PARTS, hidden]) if gated else G
            GT = s2.sbuf("GT", [PARTS, nft, PARTS])
            Y = [s2.sbuf(f"Y{p}", [PARTS, DIM]) for p in range(2)]
            gb = s2.sbuf("gb", [HALF, 2, 2])
            s_in = [s2.sem(f"in{p}") for p in range(2)]
            s_out = [s2.sem(f"out{p}") for p in range(2)]
            s_gb, s_xt, s_xts, s_l1, s_g1, s_g2, s_gt, s_gts, s_l2, s_y, s_gate = (
                s2.sem(n) for n in ("gb", "xt", "xts", "l1", "g1", "g2", "gt", "gts", "l2", "y", "gate"))
            s_g = s_g2 if gated else s_g1
            gper = 1 if gated else 2

            def live(i):
                return 0 <= i < ntiles if isinstance(i, int) else True

            def schedule(eng, body):
                for t in range(4):
                    body(t, t % 2)
                with eng.Fori(4, ntiles - 1, 2) as t:
                    body(t, 0)
                    body(t + 1, 1)
                body(ntiles, 0)
                body(ntiles + 1, 1)

            def paired(each, i, p):
                return each * (i - p + 2) // 2 if isinstance(i, int) else (i - p) * (each // 2) + each

            block = ctx2.enter_context(nc.Block())

            @block.sync
            def _(sp):
                if not gated:
                    with nc.allow_non_contiguous_dma(reason="columns of the norm's gain and bias"):
                        for n, m in enumerate(("lng", "lnb")):
                            for kb in range(2):
                                sp.dma_start(gb[:, n, kb:kb + 1], dram(w[m], HALF * kb, [(1, HALF), (1, 1)])).then_inc(s_gb, 16)

                def body(t, p):
                    if live(t):
                        wait(sp, s_xt, t - 1)
                        sp.sem_inc(s_gate, 1)
                        sp.dma_start(X[p][:], dram(xs, t * (PARTS * DIM), [(DIM, PARTS), (1, DIM)])).then_inc(s_in[p], 16)
                    if live(t - 2):
                        sp.wait_ge(s_y, t - 1)
                        sp.sem_inc(s_gate, 1)
                        sp.dma_start(dram(ys, (t - 2) * (PARTS * DIM), [(DIM, PARTS), (1, DIM)]), Y[p][:]).then_inc(s_out[p], 16)

                schedule(sp, body)
                for p in range(2):
                    sp.wait_ge(s_out[p], 16 * ntiles // 2)

            @block.tensor
            def _(pe):
                def body(t, p):
                    m = t - 1
                    if live(t):
                        pe.wait_ge(s_in[p], paired(16, t, p))
                        wait(pe, s_xts, t)
                        for kb in range(2):
                            last = nc.tensor.transpose(ps[0:HALF, PARTS * kb:PARTS * kb + PARTS], X[p][:, HALF * kb:HALF * kb + HALF], ident[:])
                        last.then_inc(s_xt, 1)
                    if live(m):
                        pe.wait_ge(s_g, gper * t)
                        wait(pe, s_gts, 2 * m)
                        for f, (c0, k) in enumerate(fts):
                            last = nc.tensor.transpose(ps[0:k, BANK + PARTS * f:BANK + PARTS * f + PARTS], G[:, c0:c0 + k], ident[:])
                        last.then_inc(s_gt, 1)
                    if live(t):
                        e = pe.value_load(texp[0:1, t:t + 1] if isinstance(t, int) else texp[0:1, bass.ds(t, 1)], min_val=0, max_val=EXPERTS - 1)
                        pe.wait_ge(s_xts, t + 1)
                        wait(pe, s_g1, 2 // (1 if not gated else 2) * t)
                        if gated:
                            wait(pe, s_g2, t)
                        for c in range(2):
                            for kb in range(2):
                                k = HALF if kb == 0 or gated else HALF + 1
                                last = nc.tensor.matmul(ps[:, (3 + c) * BANK:(3 + c) * BANK + cut], XT[0:k, kb, :],
                                                        W1[0:k, kb, bass.ds(e, 1), cut * c:cut * c + cut].rearrange("p a c -> p (a c)"),
                                                        start=(kb == 0), stop=(kb == 1))
                            last.then_inc(s_l1, 1)
                    if live(m):
                        e = pe.value_load(texp[0:1, m:m + 1] if isinstance(m, int) else texp[0:1, bass.ds(m, 1)], min_val=0, max_val=EXPERTS - 1)
                        pe.wait_ge(s_gts, 2 * t)
                        wait(pe, s_y, m)
                        out = ps[:, 5 * BANK:5 * BANK + DIM]
                        for f, (c0, k) in enumerate(fts):
                            last = nc.tensor.matmul(out, GT[0:k, f, :], W2[0:k, f, bass.ds(e, 1), :].rearrange("p a c -> p (a c)"),
                                                    start=(f == 0), stop=(f == nft - 1))
                        last.then_inc(s_l2, 1)

                schedule(pe, body)

            @block.scalar
            def _(act):
                if not gated:
                    act.wait_ge(s_gb, 64)

                def body(t, p):
                    m = t - 1
                    if live(m):
                        act.wait_ge(s_gt, t)
                        wait(act, s_l2, m)
                        if nft > 4:
                            nc.scalar.copy(GT[:, 4:, :].rearrange("p f c -> p (f c)"), ps[:, 2 * BANK:2 * BANK + PARTS * (nft - 4)]).then_inc(s_gts, 1)
                    if live(t):
                        for c in range(2 if not gated else 1):
                            act.wait_ge(s_l1, 2 * t + c + 1)
                            if c == 0:
                                wait(act, s_gt if not gated else s_g2, t)
                            nc.scalar.activation(act_out[:, cut * c:cut * c + cut], ps[:, (3 + c) * BANK:(3 + c) * BANK + cut],
                                                 ACT.Silu if gated else ACT.Gelu).then_inc(s_g1, 1)

                schedule(act, body)

            @block.vector
            def _(dve):
                if not gated:
                    nc.vector.memset(XT[HALF:HALF + 1, :, :], 1.0)
                    dve.wait_ge(s_gb, 64)

                def body(t, p):
                    m, n = t - 1, t - 2
                    if live(n) and not gated:
                        e = dve.value_load(texp[0:1, n:n + 1] if isinstance(n, int) else texp[0:1, bass.ds(n, 1)], min_val=0, max_val=EXPERTS - 1)
                    if live(t):
                        dve.wait_ge(s_xt, t + 1)
                        wait(dve, s_l1, 2 * t)
                        for kb in range(2):
                            got = ps[0:HALF, PARTS * kb:PARTS * kb + PARTS]
                            if gated:
                                last = nc.vector.tensor_copy(XT[0:HALF, kb, :], got)
                            else:
                                last = nc.vector.tensor_scalar(XT[0:HALF, kb, :], got, gb[:, 0, kb:kb + 1], gb[:, 1, kb:kb + 1], ALU.mult, ALU.add)
                        last.then_inc(s_xts, 1)
                    if live(m):
                        dve.wait_ge(s_gt, t)
                        wait(dve, s_l2, m)
                        if gated:
                            nc.vector.tensor_copy(GT[:, 0:3, :].rearrange("p f c -> p (f c)"), ps[:, BANK:BANK + 3 * PARTS]).then_inc(s_gts, 1)
                            k = fts[3][1]
                            nc.vector.tensor_copy(GT[0:k, 3, :], ps[0:k, BANK + 3 * PARTS:BANK + 4 * PARTS]).then_inc(s_gts, 1)
                        else:
                            nc.vector.tensor_copy(GT[:, 0:4, :].rearrange("p f c -> p (f c)"), ps[:, BANK:BANK + 4 * PARTS]).then_inc(s_gts, 1)
                    if live(n):
                        dve.wait_ge(s_l2, n + 1)
                        if not isinstance(n, int) or n >= 2:
                            dve.wait_ge(s_out[p], paired(16, n - 2, p))
                        y = ps[:, 5 * BANK:5 * BANK + DIM]
                        if gated:
                            nc.vector.tensor_copy(Y[p][:], y).then_inc(s_y, 1)
                        else:
                            nc.vector.tensor_tensor(Y[p][:], y, B2[:, bass.ds(e, 1), :].rearrange("p a c -> p (a c)"), ALU.add).then_inc(s_y, 1)
                    if live(t) and gated:
                        dve.wait_ge(s_l1, 2 * t + 2)
                        dve.wait_ge(s_g1, t + 1)
                        wait(dve, s_gt, t)
                        nc.vector.tensor_tensor(G[:], act_out[:], ps[:, 4 * BANK:4 * BANK + cut], ALU.mult).then_inc(s_g2, 1)

                schedule(dve, body)

        with ExitStack() as ctx2:
            s2 = Stage(nc, ctx2, name + "_sum")
            more = s2.sbuf("more", [TILE, NTILE, DIM]) if base is not None else None
            Yg = [s2.sbuf(f"Y{k}", [TILE, NTILE, DIM]) for k in range(slots)]
            s_ga = [[s2.sem(f"ga{k}{i}") for i in range(4)] for k in range(slots)]
            s_m, s_v, s_out = s2.sem("m"), s2.sem("v"), s2.sem("out")
            per = NTILE // 4
            block = ctx2.enter_context(nc.Block())

            @block.sync
            def _(sp):
                if base is not None:
                    sp.dma_start(more[:], dram(base, 0, [(DIM, TILE), (TILE * DIM, NTILE), (1, DIM)])).then_inc(s_m, 16)
                steps = slots + (base is not None)
                for q in range(4):
                    sp.wait_ge(s_v, steps * per * (q + 1))
                    sp.dma_start(dram(h_out, q * per * TILE * DIM, [(DIM, TILE), (TILE * DIM, per), (1, DIM)]), rows[:, per * q:per * q + per, :]).then_inc(s_out, 16)
                sp.wait_ge(s_out, 64)

            @block.gpsimd
            def _(pool):
                for i in range(NTILE):
                    for k in range(slots):
                        nc.gpsimd.indirect_dma_start(out=Yg[k][:, i, :], out_offset=None, in_=dram(ys, 0, [(DIM, ntiles * PARTS), (1, DIM)]),
                                                     in_offset=bass.IndirectOffsetOnAxis(ap=pos[k][:, i:i + 1], axis=0)).then_inc(s_ga[k][i // per], 16)

            @block.vector
            def _(dve):
                n = 0
                for q in range(4):
                    for k in range(slots):
                        dve.wait_ge(s_ga[k][q], 16 * per)
                    if base is not None and q == 0:
                        dve.wait_ge(s_m, 16)
                    for i in range(per * q, per * q + per):
                        if base is not None:
                            nc.vector.tensor_tensor(rows[:, i, :], rows[:, i, :], more[:, i, :], ALU.add).then_inc(s_v, 1)
                            n += 1
                            dve.wait_ge(s_v, n)
                        for k in range(slots):
                            if slots == 1:
                                ins = nc.vector.tensor_tensor(rows[:, i, :], rows[:, i, :], Yg[k][:, i, :], ALU.add)
                            else:
                                ins = nc.vector.scalar_tensor_tensor(rows[:, i, :], Yg[k][:, i, :], score[k][:, i:i + 1], rows[:, i, :], ALU.mult, ALU.add)
                            ins.then_inc(s_v, 1)
                            n += 1
                            dve.wait_ge(s_v, n)



def tower(nc, a, out):
    def scratch(name, shape):
        return nc.dram_tensor(name, shape, F32, kind="Internal").ap()

    def under(prefix, names):
        return {n: a[prefix + n] for n in names}

    xpad = scratch("xpad", [IMAGES, CHANNELS, PAD_ROWS, PAD_COLS])
    t1 = scratch("t1", [IMAGES, 33, 33, EMB])
    t2 = scratch("t2", [IMAGES, 17, 17, EMB])
    h0, h1, ffn_x, h2, h3 = (scratch(n, [TOKENS, DIM]) for n in ("h0", "h1", "ffn_x", "h2", "h3"))
    abc = scratch("abc", [48, TOKENS])
    xs = scratch("xs", [5120, DIM])
    ys = scratch("ys", [5120, DIM])

    performer_names = ("n1g", "n1b", "kqvw", "kqvb", "projw", "projb", "n2g", "n2b", "w1", "b1", "w2", "b2", "w")
    ssm_names = [m + s for m in "ABCd" for s in ("_w1", "_b1", "_w2", "_b2")] + ["D_param", "log_dt"]
    first = {"w": {c: (a["L0_attn_" + c.upper() + "W_w"], 0) for c in "qkvo"}, "b": {c: a["L0_attn_" + c.upper() + "W_b"] for c in "qkvo"}}
    second = {"w": {c: (a["L0_ffn_qkv_w"], DIM * i) for i, c in enumerate("qkv")}, "b": {"o": a["L0_ffn_proj_b"]},
              "lng": a["L0_ffn_ln1_g"], "lnb": a["L0_ffn_ln1_b"]}
    second["w"]["o"] = (a["L0_ffn_proj_w"], 0)
    moe = {"gate_w": a["L0_ffn_gate_w"], "gate_b": a["L0_ffn_gate_b"], "w1": [a["L0_ffn_w1"]], "b1": a["L0_ffn_b1"],
           "w2": a["L0_ffn_w2"], "b2": a["L0_ffn_b2"], "lng": a["L0_ffn_ln2_g"], "lnb": a["L0_ffn_ln2_b"]}
    glu = {"gate_w": a["L1_ffn_Wg"], "gate_b": a["L1_ffn_bg"], "w1": [a["L1_ffn_W1"], a["L1_ffn_W2"]], "w2": a["L1_ffn_W3"]}

    with nc.cleanup_on_exit():
        pad_image(nc, a["x"], xpad)
        performer(nc, "a1", xpad, t1, under("L0_tok_a1_", performer_names), True)
    with nc.cleanup_on_exit():
        performer(nc, "a2", t1, t2, under("L0_tok_a2_", performer_names), False)
    with nc.cleanup_on_exit():
        project(nc, t2, h0, a["L0_tok_proj_w"], a["L0_tok_proj_b"], a["cls_tok"])
    with nc.cleanup_on_exit():
        attention(nc, "at", h0, h1, first, False)
    with nc.cleanup_on_exit():
        attention(nc, "fa", h1, ffn_x, second, True)
    with nc.cleanup_on_exit():
        experts(nc, "moe", ffn_x, h1, h2, xs, ys, moe, False)
    with nc.cleanup_on_exit():
        state_space(nc, "ssm", h2, h3, abc, under("L1_attn_", ssm_names))
    with nc.cleanup_on_exit():
        experts(nc, "glu", h3, None, out, xs, ys, glu, True)



def kernel(**inputs):
    import numpy as np
    from concourse import bacc
    from concourse.bass_utils import run_bass_kernel_spmd

    nc = bacc.Bacc("TRN2", target_bir_lowering=False, num_devices=1)
    arrays = {"in_" + n: np.ascontiguousarray(v) for n, v in inputs.items()}
    a = {n: nc.dram_tensor("in_" + n, v.shape, F32, kind="ExternalInput").ap() for n, v in inputs.items()}
    out = nc.dram_tensor("out", (IMAGES, TOKENS // IMAGES, DIM), F32, kind="ExternalOutput").ap()
    tower(nc, a, dram(out, 0, [(DIM, TOKENS), (1, DIM)]))
    return run_bass_kernel_spmd(nc, [arrays], core_ids=[0]).results[0]["out"]
```

```python
from contextlib import ExitStack

import concourse.bass as bass
from concourse import mybir
from concourse.alu_op_type import AluOpType as ALU

ACT = mybir.ActivationFunctionType
F32 = mybir.dt.float32
I32, U32 = mybir.dt.int32, mybir.dt.uint32
AX_X = mybir.AxisListType.X
PARTS = 128
BANK = 512

IMAGES, CHANNELS, SIDE = 32, 3, 128
EMB, FEATS = 64, 32
EPS = 1e-5


def dram(ap, offset, dims):
    return bass.AP(ap.tensor, offset, [list(d) for d in dims])


def spread(ap, axis, n):
    shape = list(ap.shape)
    return ap.unsqueeze(axis).broadcast_to(shape[:axis] + [n] + shape[axis:])


def wait(eng, sem, n):
    if not isinstance(n, int) or n > 0:
        eng.wait_ge(sem, n)


class Stage:

    def __init__(self, nc, ctx, name):
        self.nc, self.ctx, self.name = nc, ctx, name

    def sbuf(self, name, shape, dtype=F32):
        return self.ctx.enter_context(self.nc.sbuf_tensor(f"{self.name}_{name}", shape, dtype))

    def psum(self):
        return self.ctx.enter_context(self.nc.psum_tensor(f"{self.name}_psum", [PARTS, 8 * BANK], F32))

    def sem(self, name):
        return self.nc.alloc_semaphore(name=f"{self.name}_{name}")


def make_identity(nc, pool, ident, done):
    nc.gpsimd.memset(ident[:], 0.0).then_inc(done, 1)
    pool.wait_ge(done, 1)
    nc.gpsimd.affine_select(out=ident[:], in_=ident[:], compare_op=ALU.not_equal, fill=1.0, base=0,
                            pattern=[[-1, PARTS]], channel_multiplier=1).then_inc(done, 1)


PAD_ROWS, PAD_COLS = 132, 132


class PaddedImage:

    def __init__(self, nc, st, x, xpad):
        self.nc, self.x, self.xpad = nc, x, xpad
        self.zeros = st.sbuf("pad_zeros", [PARTS, PAD_COLS * 2])
        self.zeroed, self.edged, self.copied = st.sem("pad_zeroed"), st.sem("pad_edged"), st.sem("pad_copied")
        self.planes = IMAGES * CHANNELS
        self.plane = PAD_ROWS * PAD_COLS

    def zero(self, dve):
        self.nc.vector.memset(self.zeros[:], 0.0).then_inc(self.zeroed, 1)

    def inside(self, eng, sent):
        parts = 4
        step = self.planes // parts
        for n in range(parts):
            if n == 2:
                eng.wait_ge(sent, 1)
            eng.dma_start(dram(self.xpad, n * step * self.plane + 2 * PAD_COLS + 2, [(self.plane, step), (PAD_COLS, SIDE), (1, SIDE)]),
                          dram(self.x, n * step * SIDE * SIDE, [(SIDE * SIDE, step), (SIDE, SIDE), (1, SIDE)])).then_inc(self.copied, 16)

    def edges(self, eng):
        planes, plane = self.planes, self.plane
        eng.wait_ge(self.zeroed, 1)
        eng.dma_start(dram(self.xpad, 0, [(plane, planes), (1, 2 * PAD_COLS)]), self.zeros[0:planes, :]).then_inc(self.edged, 16)
        eng.dma_start(dram(self.xpad, 130 * PAD_COLS, [(plane, planes), (1, 2 * PAD_COLS)]), self.zeros[0:planes, :]).then_inc(self.edged, 16)
        for c in (0, 130):
            eng.dma_start(dram(self.xpad, 2 * PAD_COLS + c, [(plane, planes), (PAD_COLS, SIDE), (1, 2)]),
                          self.zeros[0:planes, 0:2 * SIDE].rearrange("p (a b) -> p a b", b=2)).then_inc(self.edged, 16)

    def arrived(self, eng):
        eng.wait_ge(self.copied, 16 * 4)
        eng.wait_ge(self.edged, 16 * 4)



def performer(nc, name, src, dst, w, first, image=None):
    quads = 2 if first else 1
    tiles = 4 * quads
    steps = IMAGES if first else IMAGES // 2
    own = 1 if first else 2
    dim = 147 if first else 576
    width = 126 if first else 577
    ktiles = [(0, 126)] if first else [(0, 128), (128, 128), (256, 128), (384, 128), (512, 65)]
    rem = dim - 126
    taps = 9
    early = 1 if first else 2
    COLS = 256

    with ExitStack() as ctx:
        st = Stage(nc, ctx, name)
        ps = st.psum()
        ident = st.sbuf("ident", [PARTS, PARTS])
        W = st.sbuf("W", [PARTS, len(ktiles), COLS])
        Wrem = st.sbuf("Wrem", [PARTS, 4, COLS]) if first else None
        projw1 = st.sbuf("projw1", [EMB + 1, EMB + 1])
        w1 = st.sbuf("w1", [PARTS, PARTS])
        w2 = st.sbuf("w2", [PARTS, PARTS])
        b1 = st.sbuf("b1", [PARTS, 1])
        b2 = st.sbuf("b2", [PARTS, EMB])
        projb = st.sbuf("projb", [PARTS, EMB])
        mask = st.sbuf("mask", [PARTS, 4])
        mhalf = st.sbuf("mhalf", [PARTS, 8])
        epst = st.sbuf("eps", [PARTS, 8])
        X = [st.sbuf(f"X{p}", [PARTS, 21, 35] if first else [PARTS, 4, dim]) for p in range(2)]
        names = ("x_in0", "x_in1", "out0", "out1", "border", "stat", "aggr", "eps1", "rstd1", "norm", "trans", "tback", "rem", "kq", "sq", "v", "xd", "z", "exp",
                 "kv", "kvs", "qt", "rq", "kp", "bd", "num", "den", "rden", "ymul", "y", "vp", "yb", "stat2", "aggr2",
                 "eps2", "rstd2", "norm2", "yt", "yts", "m1", "gelu", "m2", "fin", "ones", "zero", "tail", "load", "gate")
        s = {n: st.sem(n) for n in names}

        def load(sp, i, p):
            wait(sp, s["norm"], i - 1)
            if first:
                sp.sem_inc(s["load"], 1)
                wait(sp, s["tail"], 2 * (i - 1))
            sp.sem_inc(s["load"], 1)
            if first:
                for ob in range(4):
                    for c in range(CHANNELS):
                        sp.dma_start(X[p][32 * ob:32 * ob + 32, 7 * c:7 * c + 7, :],
                                     dram(src, (i * CHANNELS + c) * (PAD_ROWS * PAD_COLS) + 32 * ob,
                                          [(4 * PAD_COLS, 32), (PAD_COLS, 7), (1, 35)])).then_inc(s["x_in%d" % p], 16)
            else:
                for im in range(2):
                    for tl in range(2):
                        for ky in range(3):
                            sp.dma_start(X[p][:, 2 * im + tl, 192 * ky:192 * ky + 192],
                                         dram(src, (2 * i + im) * (33 * 33 * EMB) + (16 * tl + ky) * 33 * EMB,
                                              [(2 * 33 * EMB, 8), (2 * EMB, 16), (1, 3 * EMB)])).then_inc(s["x_in%d" % p], 16)

        with ExitStack() as ctx2:
            s2 = Stage(nc, ctx2, name + "_prep")
            s_w, s_id, s_bias, s_gain, s_kq, s_kqs, s_feat, s_featdone, s_rem, s_ready = (
                s2.sem(n) for n in ("w", "id", "bias", "gain", "kq", "kqs", "feat", "featdone", "rem", "ready"))
            s_bd, s_small, s_zero, s_mv = s2.sem("bd"), s2.sem("small"), s2.sem("zero"), s2.sem("mv")
            s_sent = s2.sem("sent")
            gcol = s2.sbuf("gcol", [PARTS, 6])
            bcol = s2.sbuf("bcol", [PARTS, 6])
            Wr = s2.sbuf("Wr", [PARTS, 1, COLS])
            kqvb = s2.sbuf("kqvb", [1, 3 * EMB])
            brow = s2.sbuf("brow", [1, 3 * EMB])
            wr2 = s2.sbuf("wr2", [FEATS, 2 * EMB])
            WB = s2.sbuf("WB", [PARTS, 2 * FEATS])
            WT = s2.sbuf("WT", [PARTS, PARTS])
            g2 = s2.sbuf("g2", [PARTS, 1])
            n2b = s2.sbuf("n2b", [PARTS, 1])
            b1r = s2.sbuf("b1r", [PARTS, 1])
            if first:
                parts_of = [(126, 126, W[:, 0, :]), (rem, rem + 1, Wr[:, 0, :])]
            else:
                parts_of = [(128, 128, W[:, k, :]) for k in range(4)] + [(64, 65, W[:, 4, :])]
            nk = len(parts_of)
            pad = PaddedImage(nc, s2, image, src) if first else None
            block = ctx2.enter_context(nc.Block())

            @block.sync
            def _(sp):
                n = 0
                ctx2.enter_context(nc.allow_non_contiguous_dma(reason="columns of a few hundred gains and biases"))
                sp.wait_ge(s_zero, 4)
                for k, (rows, _, place) in enumerate(parts_of):
                    if first:
                        sp.dma_start(place[0:rows, 0:3 * EMB], w["kqvw"][126 * k:126 * k + rows, :]).then_inc(s_w, 16)
                        sp.dma_start(gcol[0:rows, k:k + 1], dram(w["n1g"], 126 * k, [(1, rows), (1, 1)])).then_inc(s_w, 16)
                        sp.dma_start(bcol[0:rows, k:k + 1], dram(w["n1b"], 126 * k, [(1, rows), (1, 1)])).then_inc(s_w, 16)
                        n += 3
                if not first:
                    for odd in range(2):
                        p0, count = EMB * odd, taps // 2 + 1 - odd
                        sp.dma_start(W[p0:p0 + EMB, 0:count, 0:3 * EMB],
                                     dram(w["kqvw"], odd * 3 * EMB, [(taps * 3 * EMB, EMB), (2 * 3 * EMB, count), (1, 3 * EMB)])).then_inc(s_w, 16)
                        sp.dma_start(gcol[p0:p0 + EMB, 0:count].unsqueeze(2), dram(w["n1g"], odd, [(taps, EMB), (2, count), (1, 1)])).then_inc(s_w, 16)
                        sp.dma_start(bcol[p0:p0 + EMB, 0:count].unsqueeze(2), dram(w["n1b"], odd, [(taps, EMB), (2, count), (1, 1)])).then_inc(s_w, 16)
                        n += 3
                sp.dma_start(kqvb[0:1, :], dram(w["kqvb"], 0, [(1, 1), (1, 3 * EMB)])).then_inc(s_w, 16)
                for half in range(2):
                    p0 = EMB * half
                    sp.dma_start(w1[p0:p0 + EMB, p0:p0 + EMB], w["w1"]).then_inc(s_w, 16)
                    sp.dma_start(w2[p0:p0 + EMB, p0:p0 + EMB], w["w2"]).then_inc(s_w, 16)
                sp.dma_start(wr2[:].rearrange("p (a b) -> p a b", a=2), dram(w["w"], 0, [(EMB, FEATS), (0, 2), (1, EMB)])).then_inc(s_w, 16)
                for to, frm in ((g2, "n2g"), (n2b, "n2b"), (b1r, "b1")):
                    sp.dma_start(to[:], dram(w[frm], 0, [(0, 2), (1, EMB), (1, 1)])).then_inc(s_w, 16)
                sp.dma_start(projw1[0:EMB, 0:EMB], w["projw"]).then_inc(s_w, 16)
                sp.dma_start(b2[:], dram(w["b2"], 0, [(0, PARTS), (1, EMB)])).then_inc(s_w, 16)
                sp.dma_start(projb[:], dram(w["projb"], 0, [(0, PARTS), (1, EMB)])).then_inc(s_w, 16)
                n += 1 + 4 + 4 + 3
                sp.sem_inc(s_sent, 1)
                sp.wait_ge(s_w, 16 * n)
                sp.sem_inc(s_ready, 1)
                if first:
                    sp.wait_ge(s_gain, nk + 1)
                    sp.dma_start(Wr[rem:rem + 1, 0, 0:3 * EMB], brow[0:1, :]).then_inc(s_bd, 16)
                    sp.wait_ge(s_featdone, nk)
                    for q in range(4):
                        sp.dma_start(Wrem[32 * q:32 * q + rem + 1, q, :], Wr[0:rem + 1, 0, :]).then_inc(s_rem, 16)
                    sp.wait_ge(s_rem, 64)

            @block.scalar
            def _(act):
                if first:
                    pad.inside(act, s_sent)
                    pad.edges(act)
                    pad.arrived(act)
                act.wait_ge(s_ready, 1)
                for i in range(early):
                    load(act, i, i)

            @block.gpsimd
            def _(pool):
                make_identity(nc, pool, ident, s_id)

            @block.vector
            def _(dve):
                if first:
                    pad.zero(dve)
                nc.vector.memset(w1[:], 0.0).then_inc(s_zero, 1)
                nc.vector.memset(w2[:], 0.0).then_inc(s_zero, 1)
                nc.vector.memset(projw1[:], 0.0).then_inc(s_zero, 1)
                nc.vector.memset(Wr[:], 0.0).then_inc(s_zero, 1)
                nc.vector.memset(WB[:], 0.0).then_inc(s_mv, 1)
                if first:
                    nc.vector.memset(Wrem[:], 0.0).then_inc(s_mv, 1)
                nc.vector.memset(mask[:], 0.0).then_inc(s_small, 1)
                nc.vector.memset(mhalf[:], -0.5)
                nc.vector.memset(epst[:], EPS)
                dve.wait_ge(s_small, 1)
                for q in range(4):
                    nc.vector.memset(mask[32 * q:32 * q + 32, q:q + 1], 1.0)
                dve.wait_ge(s_ready, 1)
                nc.vector.memset(projw1[EMB:EMB + 1, EMB:EMB + 1], 1.0)
                dve.wait_ge(s_bias, 1)
                nc.vector.tensor_tensor(brow[0:1, :], ps[0:1, 0:3 * EMB], kqvb[0:1, :], ALU.add).then_inc(s_gain, 1)
                for k, (rows, _, place) in enumerate(parts_of):
                    nc.vector.tensor_scalar(place[0:rows, 0:3 * EMB], place[0:rows, 0:3 * EMB], gcol[0:rows, k:k + 1],
                                            None, ALU.mult).then_inc(s_gain, 1)
                if not first:
                    dve.wait_ge(s_gain, 1)
                    nc.vector.tensor_copy(W[EMB:EMB + 1, 4, 0:3 * EMB], brow[0:1, :]).then_inc(s_bd, 16)
                dve.wait_ge(s_kq, 1)
                dve.wait_ge(s_mv, 1)
                nc.vector.tensor_copy(WB[0:EMB, 0:FEATS], ps[0:EMB, BANK:BANK + FEATS])
                nc.vector.tensor_copy(WB[EMB:, FEATS:], ps[EMB:, BANK:BANK + FEATS]).then_inc(s_kqs, 1)
                for k, (_, rows, place) in enumerate(parts_of):
                    dve.wait_ge(s_kq, k + 2)
                    nc.vector.tensor_copy(WT[:, 0:rows], ps[:, 2 * BANK:2 * BANK + rows]).then_inc(s_kqs, 1)
                    dve.wait_ge(s_feat, k + 1)
                    nc.vector.tensor_copy(place[0:rows, 3 * EMB:COLS], ps[0:rows, 3 * BANK:3 * BANK + 2 * FEATS]).then_inc(s_featdone, 1)
                dve.wait_ge(s_bias, 2)
                nc.vector.tensor_tensor(b1[:], ps[:, 4 * BANK:4 * BANK + 1], b1r[:], ALU.add)
                nc.vector.tensor_scalar(w1[:], w1[:], g2[:, 0:1], None, ALU.mult)

            @block.tensor
            def _(pe):
                pe.wait_ge(s_ready, 1)
                for k, (rows, _, place) in enumerate(parts_of):
                    last = nc.tensor.matmul(ps[0:1, 0:3 * EMB], bcol[0:rows, k:k + 1], place[0:rows, 0:3 * EMB],
                                            start=(k == 0), stop=(k == nk - 1))
                last.then_inc(s_bias, 1)
                nc.tensor.matmul(ps[:, 4 * BANK:4 * BANK + 1], w1[:], n2b[:, 0:1], start=True, stop=True).then_inc(s_bias, 1)
                pe.wait_ge(s_id, 2)
                nc.tensor.transpose(ps[:, BANK:BANK + FEATS], wr2[:], ident[0:FEATS, 0:FEATS]).then_inc(s_kq, 1)
                pe.wait_ge(s_bd, 16)
                pe.wait_ge(s_gain, nk + 1)
                for k, (_, rows, place) in enumerate(parts_of):
                    wait(pe, s_kqs, k + 1)
                    nc.tensor.transpose(ps[:, 2 * BANK:2 * BANK + rows], place[0:rows, 0:2 * EMB], ident[0:rows, 0:rows]).then_inc(s_kq, 1)
                    pe.wait_ge(s_kqs, k + 2)
                    wait(pe, s_featdone, k)
                    nc.tensor.matmul(ps[0:rows, 3 * BANK:3 * BANK + 2 * FEATS], WT[:, 0:rows], WB[:], start=True, stop=True).then_inc(s_feat, 1)

        hN = st.sbuf("hN", [PARTS, tiles, width])
        hR = st.sbuf("hR", [PARTS, tiles, 32]) if first else None
        stats = st.sbuf("stats", [PARTS, tiles, 1 if first else 2, 6])
        mv = st.sbuf("mv", [PARTS, tiles, 2])
        rstd = st.sbuf("rstd", [PARTS, tiles])
        nkt = 1 if first else 5
        hT = st.sbuf("hT", [PARTS, quads if first else nkt, BANK])
        RQ = st.sbuf("RQ", [PARTS, BANK])
        sq = st.sbuf("sq", [PARTS, tiles, 2, EMB])
        xd = st.sbuf("xd", [PARTS, tiles, 2])
        v1 = st.sbuf("v1", [PARTS, tiles, EMB + 1])
        z = st.sbuf("z", [PARTS, 2, tiles, FEATS])
        kpq = st.sbuf("kpq", [PARTS, 2, tiles, FEATS])
        kvT = st.sbuf("kvT", [EMB + 1, 4, FEATS])
        BD = st.sbuf("BD", [PARTS, 4, EMB + 1])
        den = st.sbuf("den", [PARTS, tiles])
        rden = st.sbuf("rden", [PARTS, tiles])
        vp = st.sbuf("vp", [PARTS, tiles, EMB])
        y = st.sbuf("y", [PARTS, tiles, EMB])
        yb = st.sbuf("yb", [PARTS, tiles, EMB])
        stats2 = st.sbuf("stats2", [PARTS, tiles, 6])
        mv2 = st.sbuf("mv2", [PARTS, tiles, 2])
        rstd2 = st.sbuf("rstd2", [PARTS, tiles])
        yn = st.sbuf("yn", [PARTS, tiles, EMB])
        yT = st.sbuf("yT", [PARTS, tiles // 2, PARTS])
        G = st.sbuf("G", [PARTS, tiles // 2, PARTS])
        O = [st.sbuf(f"O{p}", [PARTS, tiles, EMB]) for p in range(2)]
        BDz = st.sbuf("BDz", [IMAGES, 33 * EMB])
        half = tiles // 2 * PARTS

        nq = quads if first else 1
        nt = quads if first else nkt
        out_dmas = 4 if first else 4
        in_dmas = 12 if first else 12

        def bank(b, n=BANK):
            return ps[:, b * BANK:b * BANK + n]

        TB = (0, 1) if first else (4, 5, 0, 4, 5)
        KQ = [ps[:, (2 + 2 * q) * BANK:(4 + 2 * q) * BANK].rearrange("p (t c) -> p t c", c=COLS) for q in range(quads)]
        KV, KP = ps[0:EMB + 1, 6 * BANK:6 * BANK + own * FEATS], ps[:, 6 * BANK + 64:6 * BANK + 64 + EMB + 1]
        NUM = [ps[:, 6 * BANK + 192:6 * BANK + 192 + 4 * (EMB + 1)].rearrange("p (t c) -> p t c", c=EMB + 1),
               ps[:, 7 * BANK:7 * BANK + 4 * (EMB + 1)].rearrange("p (t c) -> p t c", c=EMB + 1)]

        def window(p, j, n=21):
            return X[p][:, 0:n, 4 * j:4 * j + 7] if first else X[p][:, j, :]

        def twice(each, i, p):
            return each * (i - p + 2) // 2 if isinstance(i, int) else (i - p) * (each // 2) + each

        def live(i):
            return 0 <= i < steps if isinstance(i, int) else True

        def schedule(eng, body):
            for t in range(6):
                body(t, t % 2)
            with eng.Fori(6, steps, 2) as t:
                body(t, 0)
                body(t + 1, 1)
            for t in range(steps, steps + 4):
                body(t, t % 2)

        block = ctx.enter_context(nc.Block())

        @block.sync
        def _(sp):
            rows = 33 if first else 17
            pic = rows * rows * EMB

            def border():
                sp.wait_ge(s["zero"], 1)
                sp.dma_start(dram(dst, 0, [(pic, IMAGES), (1, rows * EMB)]),
                             BDz[0:IMAGES, 0:rows * EMB]).then_inc(s["border"], 16)
                sp.dma_start(dram(dst, rows * EMB, [(pic, IMAGES), (rows * EMB, rows - 1), (1, EMB)]),
                             BDz[0:IMAGES, 0:(rows - 1) * EMB].rearrange("p (a b) -> p a b", b=EMB)).then_inc(s["border"], 16)

            def store(i, p):
                sp.wait_ge(s["fin"], i + 1)
                sp.sem_inc(s["load"], 1)
                if first:
                    for ob in range(4):
                        sp.dma_start(dram(dst, i * pic + (33 + 1 + 8 * ob) * EMB, [(33 * EMB, 32), (1, 8 * EMB)]),
                                     O[p][32 * ob:32 * ob + 32, :, :]).then_inc(s["out%d" % p], 16)
                else:
                    for im in range(2):
                        for tl in range(2):
                            sp.dma_start(dram(dst, (2 * i + im) * pic + (17 * (1 + 8 * tl) + 1) * EMB,
                                              [(17 * EMB, 8), (EMB, 16), (1, EMB)]), O[p][:, 2 * im + tl, :]).then_inc(s["out%d" % p], 16)

            def body(t, p):
                if live(t) and not (isinstance(t, int) and t < early):
                    load(sp, t, p)
                if isinstance(t, int) and t == 1:
                    border()
                if live(t - 4):
                    store(t - 4, p)

            schedule(sp, body)
            sp.wait_ge(s["border"], 32)
            for p in range(2):
                sp.wait_ge(s["out%d" % p], 16 * out_dmas * steps // 2)

        @block.gpsimd
        def _(pool):
            if first:
                nc.gpsimd.memset(hR[:, :, rem + 1:], 0.0)
                nc.gpsimd.memset(hR[:, :, rem:rem + 1], 1.0)
            else:
                nc.gpsimd.memset(hN[:, :, dim:dim + 1], 1.0)
            nc.gpsimd.memset(v1[:, :, EMB:EMB + 1], 1.0).then_inc(s["ones"], 1)
            nc.gpsimd.memset(BDz[:], 0.0).then_inc(s["zero"], 1)

            def inverse_root(i, aggr, eps, done, mvt, out):
                pool.wait_ge(s[aggr], tiles * (i + 1))
                nc.gpsimd.tensor_tensor(out[:], mvt[:, :, 1], epst[:, 0:tiles], ALU.add).then_inc(s[eps], 1)
                pool.wait_ge(s[eps], i + 1)
                nc.gpsimd.tensor_tensor(out[:], out[:], mhalf[:, 0:tiles], ALU.pow).then_inc(s[done], 1)

            def body(t, p):
                l = t - 3
                if live(t - 2):
                    pool.wait_ge(s["v"], quads * (t - 1))
                    wait(pool, s["y"], t - 2)
                    nc.gpsimd.tensor_tensor(vp[:], v1[:, :, 0:EMB], spread(projb[:], 1, tiles), ALU.add).then_inc(s["vp"], 1)
                if live(l):
                    inverse_root(l, "aggr2", "eps2", "rstd2", mv2, rstd2)
                    pool.wait_ge(s["y"], l + 1)
                    wait(pool, s["fin"], l)
                    nc.gpsimd.tensor_tensor(yb[:], y[:], spread(b2[:], 1, tiles), ALU.add).then_inc(s["yb"], 1)
                if live(t):
                    inverse_root(t, "aggr", "eps1", "rstd1", mv, rstd)
                    if first:
                        tail = bass.AP(X[p][:].tensor, 18 * 35, [list(X[p][:].ap[0]), [4, tiles], [35, 3], [1, 7]])
                        out = hR[:, :, 0:rem].rearrange("p t (a b) -> p t a b", b=7)
                        wait(pool, s["trans"], 3 * t)
                        nc.gpsimd.tensor_tensor(out, tail, spread(spread(mv[:, :, 0], 2, 3), 3, 7), ALU.subtract).then_inc(s["tail"], 1)
                        pool.wait_ge(s["tail"], 2 * t + 1)
                        nc.gpsimd.tensor_tensor(hR[:, :, 0:rem], hR[:, :, 0:rem], spread(rstd[:], 2, rem), ALU.mult).then_inc(s["tail"], 1)

            schedule(pool, body)

        @block.vector
        def _(dve):
            def statistics(i, p):
                if first:
                    wait(dve, s["tail"], 2 * i)
                dve.wait_ge(s["x_in%d" % p], twice(16 * in_dmas, i, p))
                for j in range(tiles):
                    if first:
                        nc.vector.bn_stats(stats[:, j, 0, :], window(p, j)).then_inc(s["stat"], 1)
                    else:
                        for h in range(2):
                            last = nc.vector.bn_stats(stats[:, j, h, :], X[p][:, j, 288 * h:288 * h + 288])
                        last.then_inc(s["stat"], 1)

            def aggregate(i):
                for j in range(tiles):
                    nc.vector.bn_aggr(mv[:, j, :], stats[:, j, :, :].rearrange("p a b -> p (a b)")).then_inc(s["aggr"], 1)

            def normalise(i, p):
                dve.wait_ge(s["rstd1"], i + 1)
                wait(dve, s["trans"], (nt + (1 if first else 0)) * i)
                for j in range(tiles):
                    out = hN[:, j, :].rearrange("p (a b) -> p a b", b=7) if first else hN[:, j, 0:dim]
                    last = nc.vector.tensor_scalar(out, window(p, j, 18), mv[:, j, 0:1], rstd[:, j:j + 1], ALU.subtract, ALU.mult)
                last.then_inc(s["norm"], 1)

            def exponent(i, q):
                tl = slice(4 * q, 4 * q + 4)
                dve.wait_ge(s["sq"], quads * i + q + 1)
                nc.vector.reduce_sum(xd[:, tl, :], sq[:, tl, :, :], axis=AX_X).then_inc(s["xd"], 1)
                dve.wait_ge(s["xd"], quads * i + q + 1)
                wait(dve, s["exp"], i)
                dve.wait_ge(s["v"], quads * i + q + 1)
                nc.vector.tensor_tensor(z[:, :, tl, :].rearrange("p a t f -> p t a f"), KQ[q][:, :, 3 * EMB:COLS].rearrange("p t (a f) -> p t a f", a=2),
                                        spread(xd[:, tl, :], 3, FEATS), ALU.subtract).then_inc(s["z"], 1)

            def block_diagonal(i):
                dve.wait_ge(s["kp"], i + 1)
                wait(dve, s["num"], quads * i)
                nc.vector.tensor_tensor(BD[:], spread(KP, 1, 4), spread(mask[:], 2, EMB + 1), ALU.mult).then_inc(s["bd"], 1)

            def attend(i):
                for q in range(quads):
                    dve.wait_ge(s["num"], quads * i + q + 1)
                    nc.vector.tensor_scalar(den[:, 4 * q:4 * q + 4], NUM[q][:, :, EMB], 1e-8 * FEATS, None, ALU.add).then_inc(s["den"], 1)
                dve.wait_ge(s["den"], quads * (i + 1))
                nc.vector.reciprocal(rden[:], den[:]).then_inc(s["rden"], 1)
                dve.wait_ge(s["rden"], i + 1)
                wait(dve, s["yb"], i)
                for q in range(quads):
                    nc.vector.tensor_tensor(y[:, 4 * q:4 * q + 4, :], NUM[q][:, :, 0:EMB],
                                            spread(rden[:, 4 * q:4 * q + 4], 2, EMB), ALU.mult).then_inc(s["ymul"], 1)
                dve.wait_ge(s["ymul"], quads * (i + 1))
                dve.wait_ge(s["vp"], i + 1)
                nc.vector.tensor_tensor(y[:], y[:], vp[:], ALU.add).then_inc(s["y"], 1)
                dve.wait_ge(s["y"], i + 1)
                for j in range(tiles):
                    nc.vector.bn_stats(stats2[:, j, :], y[:, j, :]).then_inc(s["stat2"], 1)

            def aggregate2(i):
                for j in range(tiles):
                    nc.vector.bn_aggr(mv2[:, j, :], stats2[:, j, :]).then_inc(s["aggr2"], 1)

            def normalise2(i):
                dve.wait_ge(s["rstd2"], i + 1)
                wait(dve, s["yt"], i)
                for j in range(tiles):
                    last = nc.vector.tensor_scalar(yn[:, j, :], y[:, j, :], mv2[:, j, 0:1], rstd2[:, j:j + 1], ALU.subtract, ALU.mult)
                last.then_inc(s["norm2"], 1)

            def finish(i, p):
                dve.wait_ge(s["m2"], i + 1)
                dve.wait_ge(s["yb"], i + 1)
                wait(dve, s["out%d" % p], twice(16 * out_dmas, i - 2, p))
                nc.vector.tensor_tensor(O[p][:].rearrange("p t e -> p (t e)"), bank(1, half), yb[:].rearrange("p t e -> p (t e)"),
                                        ALU.add).then_inc(s["fin"], 1)

            def body(t, p):
                l = t - 3
                if live(t - 2):
                    exponent(t - 2, quads - 1)
                if live(t - 4):
                    finish(t - 4, p)
                if live(l):
                    attend(l)
                    dve.wait_ge(s["stat2"], tiles * (l + 1))
                    dve.sem_inc(s["gate"], 1)
                    aggregate2(l)
                if live(t):
                    statistics(t, p)
                if live(t):
                    dve.wait_ge(s["stat"], tiles * (t + 1))
                    dve.sem_inc(s["gate"], 1)
                    aggregate(t)
                if live(l):
                    normalise2(l)
                if live(t - 1) and quads == 2:
                    exponent(t - 1, 0)
                if live(t - 2):
                    block_diagonal(t - 2)
                if live(t):
                    normalise(t, p)

            schedule(dve, body)

        @block.scalar
        def _(act):
            def body(t, p):
                m, k, l = t - 1, t - 2, t - 3
                if live(m):
                    for q in range(nt):
                        rows = ktiles[0][1] if first else ktiles[q][1]
                        if first and q == 1:
                            act.wait_ge(s["trans"], 3 * m + 2)
                            nc.scalar.copy(RQ[:, 0:256], bank(3)[:, 0:256]).then_inc(s["rem"], 1)
                        act.wait_ge(s["trans"], 3 * m + (1, 3)[q] if first else nt * m + q + 1)
                        nc.scalar.copy(hT[0:rows, q, :], ps[0:rows, TB[q] * BANK:(TB[q] + 1) * BANK]).then_inc(s["tback"], 1)
                if live(k):
                    act.wait_ge(s["z"], quads * (k + 1))
                    wait(act, s["qt"], k)
                    nc.scalar.activation(kpq[:].rearrange("p a t f -> p (a t f)"), z[:].rearrange("p a t f -> p (a t f)"), ACT.Exp).then_inc(s["exp"], 1)

                def squares(q):
                    tl = slice(4 * q, 4 * q + 4)
                    act.wait_ge(s["kq"], quads * m + q + 1)
                    wait(act, s["xd"], quads * m)
                    nc.scalar.activation(sq[:, tl, :, :].rearrange("p t a e -> p t (a e)"), KQ[q][:, :, 0:2 * EMB], ACT.Square,
                                         scale=0.5 ** 0.5).then_inc(s["sq"], 1)
                    wait(act, s["kv"], m)
                    wait(act, s["vp"], m)
                    if isinstance(m, int) and m == 0:
                        act.wait_ge(s["ones"], 1)
                    nc.scalar.copy(v1[:, tl, 0:EMB], KQ[q][:, :, 2 * EMB:3 * EMB]).then_inc(s["v"], 1)

                if live(m) and quads == 2:
                    squares(0)
                if live(k):
                    act.wait_ge(s["kv"], k + 1)
                    kv = KV.rearrange("p (i f) -> p i f", f=FEATS)
                    nc.scalar.copy(kvT[:].rearrange("p (i r) f -> p i r f", i=own), spread(kv, 2, 4 // own)).then_inc(s["kvs"], 1)
                if live(k):
                    act.wait_ge(s["qt"], k + 1)
                    nc.scalar.copy(RQ[:, 256:256 + PARTS * quads], bank(7)[:, 256:256 + PARTS * quads]).then_inc(s["rq"], 1)
                if live(l):
                    act.wait_ge(s["yt"], l + 1)
                    nc.scalar.copy(yT[:].rearrange("p t c -> p (t c)"), bank(7, half)).then_inc(s["yts"], 1)
                if live(l):
                    act.wait_ge(s["m1"], l + 1)
                    nc.scalar.activation(G[:].rearrange("p t c -> p (t c)"), bank(0, half), ACT.Gelu, bias=b1[:, 0:1]).then_inc(s["gelu"], 1)
                if live(m):
                    squares(quads - 1)

            schedule(act, body)

        @block.tensor
        def _(pe):
            def main_transposes(m):
                pe.wait_ge(s["norm"], m + 1)
                if isinstance(m, int) and m == 0:
                    pe.wait_ge(s["ones"], 1)
                for q in range(nt):
                    c0, rows = ktiles[0] if first else ktiles[q]
                    if TB[q] == 0:
                        wait(pe, s["gelu"], m - 2)
                    if q == 0:
                        wait(pe, s["tback"], nt * m)
                    if q == 1 and first:
                        pe.wait_ge(s["tail"], 2 * (m + 1))
                        if not isinstance(m, int) or m >= 1:
                            pe.wait_ge(s["z"], 2 * m - 1)
                            pe.wait_ge(s["v"], 2 * m - 1)
                        for h in range(quads):
                            last = nc.tensor.transpose(bank(3)[:, PARTS * h:PARTS * h + PARTS],
                                                       hR[:, 4 * h:4 * h + 4, :].rearrange("p t c -> p (t c)"), ident[:])
                        last.then_inc(s["trans"], 1)
                    if TB[q] == 1:
                        wait(pe, s["fin"], m - 2)
                    if q >= 3:
                        pe.wait_ge(s["tback"], nt * m + q - 2)
                    for j in range(4):
                        tile = 4 * q + j if first else j
                        last = nc.tensor.transpose(ps[0:rows, TB[q] * BANK + PARTS * j:TB[q] * BANK + PARTS * j + PARTS],
                                                   hN[:, tile, c0:c0 + rows], ident[:])
                    last.then_inc(s["trans"], 1)

            cuts = [[(0, 0), (0, 1), (0, 2), (0, 3)], [(1, 0), (1, 1)], [(1, 2)], [(1, 3)]] if quads == 2 else \
                   [[(0, 0)], [(0, 1)], [(0, 2)], [(0, 3)]]

            def matmuls(m, cut):
                for q, j in cuts[cut]:
                    if j == 0:
                        pe.wait_ge(s["tback"], nt * m + (q + 1 if first else nt))
                        if first:
                            pe.wait_ge(s["rem"], m + 1)
                        wait(pe, s["z"], quads * (m - 1) + q + 1 if not isinstance(m, int) or m >= 1 else 0)
                        wait(pe, s["v"], quads * (m - 1) + q + 1 if not isinstance(m, int) or m >= 1 else 0)
                    out = KQ[q][:, j, :]
                    cols = slice(PARTS * j, PARTS * j + PARTS)
                    if first:
                        nc.tensor.matmul(out, hT[0:126, q, cols], W[0:126, 0, :], start=True, stop=False)
                        last = nc.tensor.matmul(out, RQ[:, PARTS * q:PARTS * q + PARTS], Wrem[:, j, :], start=False, stop=True)
                    else:
                        for kt in range(nkt):
                            rows = ktiles[kt][1]
                            last = nc.tensor.matmul(out, hT[0:rows, kt, cols], W[0:rows, kt, :], start=(kt == 0), stop=(kt == nkt - 1))
                    if j == 3:
                        last.then_inc(s["kq"], 1)

            def body(t, p):
                m, k, l = t - 1, t - 2, t - 3
                if live(m):
                    main_transposes(m)
                    matmuls(m, 0)
                if live(k):
                    pe.wait_ge(s["exp"], k + 1)
                    wait(pe, s["ymul"], quads * (k - 1) + 1 if not isinstance(k, int) or k >= 1 else 0)
                    per = tiles // own
                    for im in range(own):
                        for j in range(per):
                            tile = per * im + j
                            last = nc.tensor.matmul(KV[:, FEATS * im:FEATS * im + FEATS], v1[:, tile, :], kpq[:, 0, tile, :],
                                                    start=(j == 0), stop=(j == per - 1))
                    last.then_inc(s["kv"], 1)
                if live(k):
                    wait(pe, s["ymul"], quads * (l + 1))
                    for q in range(quads):
                        last = nc.tensor.transpose(bank(7)[:, 256 + PARTS * q:256 + PARTS * q + PARTS],
                                                   kpq[:, 1, 4 * q:4 * q + 4, :].rearrange("p t f -> p (t f)"), ident[:])
                    last.then_inc(s["qt"], 1)
                if live(m):
                    matmuls(m, 1)
                if live(k):
                    pe.wait_ge(s["kvs"], k + 1)
                    nc.tensor.matmul(KP, kvT[:].rearrange("p r f -> p (r f)"), projw1[:], start=True, stop=True).then_inc(s["kp"], 1)
                if live(l):
                    pe.wait_ge(s["norm2"], l + 1)
                    if live(k):
                        pe.wait_ge(s["rq"], k + 1)
                    else:
                        wait(pe, s["ymul"], quads * (l + 1))
                    for j in range(tiles // 2):
                        last = nc.tensor.transpose(bank(7)[:, PARTS * j:PARTS * j + PARTS],
                                                   yn[:, 2 * j:2 * j + 2, :].rearrange("p t e -> p (t e)"), ident[:])
                    last.then_inc(s["yt"], 1)
                if live(m):
                    matmuls(m, 2)
                if live(l):
                    pe.wait_ge(s["yts"], l + 1)
                    if live(m):
                        pe.wait_ge(s["tback"], nt * (m + 1))
                    nc.tensor.matmul(bank(0, half), w1[:], yT[:].rearrange("p t c -> p (t c)"), start=True, stop=True).then_inc(s["m1"], 1)
                if live(m):
                    matmuls(m, 3)
                if live(k):
                    pe.wait_ge(s["bd"], k + 1)
                    pe.wait_ge(s["rq"], k + 1)
                    for q in range(quads):
                        last = nc.tensor.matmul(NUM[q].rearrange("p t c -> p (t c)"), RQ[:, 256 + PARTS * q:256 + PARTS * q + PARTS],
                                                BD[:].rearrange("p t c -> p (t c)"), start=True, stop=True)
                        last.then_inc(s["num"], 1)
                if live(l):
                    pe.wait_ge(s["gelu"], l + 1)
                    wait(pe, s["fin"], l)
                    for j in range(tiles // 2):
                        last = nc.tensor.matmul(bank(1)[:, PARTS * j:PARTS * j + PARTS], G[:, j, :], w2[:], start=True, stop=True)
                    last.then_inc(s["m2"], 1)

            schedule(pe, body)


DIM, SEQ, HALF = 192, 65, 96
TOKENS = IMAGES * SEQ
TILE, NTILE = 104, 20


def project(nc, src, dst, w, b, cls):
    steps, dim, taps = IMAGES // 2, 576, 9
    ktiles = [(128 * k, 128) for k in range(4)] + [(512, 65)]
    with ExitStack() as ctx:
        st = Stage(nc, ctx, "proj")
        ps = st.psum()
        ident = st.sbuf("ident", [PARTS, PARTS])
        W = st.sbuf("W", [PARTS, 5, DIM])
        DEPTH = 4
        X = [st.sbuf(f"X{p}", [PARTS, dim + 1]) for p in range(DEPTH)]
        XT = st.sbuf("XT", [PARTS, 5, PARTS])
        O = [st.sbuf(f"O{p}", [PARTS, DIM]) for p in range(2)]
        s_w, s_id, s_ones, s_cls = st.sem("w"), st.sem("id"), st.sem("ones"), st.sem("cls")
        s_in = [st.sem(f"in{p}") for p in range(DEPTH)]
        s_out = [st.sem(f"out{p}") for p in range(2)]
        s_t, s_ts, s_t5, s_mm, s_o = st.sem("t"), st.sem("ts"), st.sem("t5"), st.sem("mm"), st.sem("o")
        block = ctx.enter_context(nc.Block())

        @block.sync
        def _(sp):
            sp.dma_start(dram(dst, 0, [(SEQ * DIM, IMAGES), (1, DIM)]), dram(cls, 0, [(0, IMAGES), (1, DIM)])).then_inc(s_cls, 16)
            for odd in range(2):
                p0, count = EMB * odd, taps // 2 + 1 - odd
                sp.dma_start(W[p0:p0 + EMB, 0:count, :], dram(w, odd * DIM, [(taps * DIM, EMB), (2 * DIM, count), (1, DIM)])).then_inc(s_w, 16)
            sp.dma_start(W[EMB:EMB + 1, 4, :], dram(b, 0, [(DIM, 1), (1, DIM)])).then_inc(s_w, 16)

            def load(i):
                for im in range(2):
                    for ky in range(3):
                        sp.dma_start(X[i % DEPTH][EMB * im:EMB * im + EMB, 192 * ky:192 * ky + 192],
                                     dram(src, (2 * i + im) * (17 * 17 * EMB) + ky * 17 * EMB,
                                          [(2 * 17 * EMB, 8), (2 * EMB, 8), (1, 3 * EMB)])).then_inc(s_in[i % DEPTH], 16)

            for i in range(DEPTH - 1):
                load(i)
            for i in range(steps):
                if i + DEPTH - 1 < steps:
                    wait(sp, s_t, 5 * i)
                    load(i + DEPTH - 1)
                sp.wait_ge(s_o, i + 1)
                sp.dma_start(dram(dst, (2 * i * SEQ + 1) * DIM, [(SEQ * DIM, 2), (DIM, EMB), (1, DIM)]), O[i % 2][:]).then_inc(s_out[i % 2], 16)
            sp.wait_ge(s_cls, 16)
            for p in range(2):
                sp.wait_ge(s_out[p], 8 * steps)

        @block.gpsimd
        def _(pool):
            make_identity(nc, pool, ident, s_id)
            for x in X:
                last = nc.gpsimd.memset(x[:, dim:], 1.0)
            last.then_inc(s_ones, 1)

        @block.tensor
        def _(pe):
            pe.wait_ge(s_id, 2)
            pe.wait_ge(s_ones, 1)
            for i in range(steps + 1):
                if i < steps:
                    pe.wait_ge(s_in[i % DEPTH], 96 * (i // DEPTH + 1))
                    wait(pe, s_ts, i)
                    wait(pe, s_t5, i)
                    for k, (c0, rows) in enumerate(ktiles):
                        nc.tensor.transpose(ps[0:rows, PARTS * k:PARTS * k + PARTS], X[i % DEPTH][:, c0:c0 + rows], ident[:]).then_inc(s_t, 1)
                if i == 0:
                    pe.wait_ge(s_w, 48)
                if i < steps:
                    pe.wait_ge(s_ts, i + 1)
                    pe.wait_ge(s_t5, i + 1)
                    wait(pe, s_o, i - 1)
                    out = ps[:, (2 + i % 2) * BANK:(2 + i % 2) * BANK + DIM]
                    for k, (c0, rows) in enumerate(ktiles):
                        last = nc.tensor.matmul(out, XT[0:rows, k, :], W[0:rows, k, :], start=(k == 0), stop=(k == 4))
                    last.then_inc(s_mm, 1)

        @block.scalar
        def _(act):
            for i in range(steps):
                act.wait_ge(s_t, 5 * i + 4)
                nc.scalar.copy(XT[:, 0:4, :].rearrange("p k c -> p (k c)"), ps[:, 0:BANK]).then_inc(s_ts, 1)

        @block.vector
        def _(dve):
            for i in range(steps):
                dve.wait_ge(s_t, 5 * i + 5)
                nc.vector.tensor_copy(XT[0:EMB + 1, 4, :], ps[0:EMB + 1, BANK:BANK + PARTS]).then_inc(s_t5, 1)
                dve.wait_ge(s_mm, i + 1)
                wait(dve, s_out[i % 2], 16 * (i // 2))
                nc.vector.tensor_copy(O[i % 2][:], ps[:, (2 + i % 2) * BANK:(2 + i % 2) * BANK + DIM]).then_inc(s_o, 1)


def moments(nc, dve, stats, tmp, s, base):
    a = [stats[:, :, n] for n in range(6)]
    nc.vector.tensor_tensor(tmp[0], a[1], a[4], ALU.add).then_inc(s, 1)
    nc.vector.tensor_tensor(tmp[1], a[1], a[4], ALU.subtract).then_inc(s, 1)
    nc.vector.tensor_tensor(tmp[2], a[2], a[5], ALU.add).then_inc(s, 1)
    dve.wait_ge(s, base + 3)
    nc.vector.tensor_scalar(tmp[0], tmp[0], 0.5, None, ALU.mult).then_inc(s, 1)
    nc.vector.tensor_tensor(tmp[1], tmp[1], tmp[1], ALU.mult).then_inc(s, 1)
    nc.vector.tensor_scalar(tmp[2], tmp[2], 1.0 / DIM, EPS, ALU.mult, ALU.add).then_inc(s, 1)
    dve.wait_ge(s, base + 6)
    nc.vector.scalar_tensor_tensor(tmp[2], tmp[1], 0.25, tmp[2], ALU.mult, ALU.add).then_inc(s, 1)


HEADS = 12


def attention(nc, name, src, raw, rows, known, stats, w, second):
    HG = 6
    with ExitStack() as ctx:
        st = Stage(nc, ctx, name)
        xT = st.sbuf("xT", [HALF + 1, 2, TOKENS])
        ident = st.sbuf("ident", [PARTS, PARTS])
        WT = st.sbuf("WT", [HALF + 1, 2, 4, DIM])
        mask = st.sbuf("mask", [HALF, HG])
        qT = st.sbuf("qT", [HALF, 2, TOKENS])
        kT = st.sbuf("kT", [HALF, 2, TOKENS])
        oT = st.sbuf("oT", [HALF + 1, 2, TOKENS])
        v = st.sbuf("v", [SEQ, IMAGES, DIM])

        with ExitStack() as ctx2:
            s2 = Stage(nc, ctx2, name + "_prep")
            ps = s2.psum()
            xn = s2.sbuf("xn", [TILE, NTILE, DIM])
            norm = NormedColumns(nc, s2, ps, src, rows, xT, ident, xn, raw=raw, known=known)
            raw = s2.sbuf("raw", [HALF, 4, 2, DIM])
            bpad = s2.sbuf("bpad", [HALF, 2, HALF + 1]) if second else None
            g = s2.sbuf("g", [HALF, 2]) if second else None
            s_w, s_mask, s_t, s_ts, s_b, s_c, s_g, s_qk, s_e, s_v, s_vs = (
                s2.sem(n) for n in ("w", "mask", "t", "ts", "b", "c", "g", "qk", "e", "v", "vs"))
            COLS, NCH, WB = 416, 5, 4
            jobs = [(mat, g_, c) for c in range(NCH) for mat in range(2) for g_ in range(2)]
            block = ctx2.enter_context(nc.Block())

            @block.sync
            def _(sp):
                norm.load(sp)
                for m in range(4):
                    sp.dma_start(raw[:, m, :, :], dram(w["w"]["qkvo"[m]][0], w["w"]["qkvo"[m]][1] * DIM,
                                                       [(DIM, HALF), (HALF * DIM, 2), (1, DIM)])).then_inc(s_w, 16)
                n = 4
                for m in range(4):
                    if not second or m == 3:
                        sp.dma_start(WT[HALF:HALF + 1, 1, m, :], dram(w["b"]["qkvo"[m]], 0, [(DIM, 1), (1, DIM)])).then_inc(s_w, 16)
                        n += 1
                if second:
                    with nc.allow_non_contiguous_dma(reason="columns of the norm's gain and bias"):
                        sp.wait_ge(s_c, 1)
                        for kb in range(2):
                            sp.dma_start(bpad[:, kb, HALF:], dram(w["lnb"], HALF * kb, [(1, HALF), (1, 1)])).then_inc(s_w, 16)
                            sp.dma_start(g[:, kb:kb + 1], dram(w["lng"], HALF * kb, [(1, HALF), (1, 1)])).then_inc(s_w, 16)
                    n += 4
                sp.wait_ge(s_w, 16 * n)
                sp.sem_inc(s_b, 1)

            @block.gpsimd
            def _(pool):
                norm.constants(pool)
                nc.gpsimd.memset(mask[:], 1.0).then_inc(s_mask, 1)
                pool.wait_ge(s_mask, 1)
                nc.gpsimd.affine_select(out=mask[:], in_=mask[:], compare_op=ALU.is_ge, fill=0.0, base=0,
                                        pattern=[[-16, HG]], channel_multiplier=1).then_inc(s_mask, 1)
                pool.wait_ge(s_mask, 2)
                nc.gpsimd.affine_select(out=mask[:], in_=mask[:], compare_op=ALU.is_ge, fill=0.0, base=15,
                                        pattern=[[16, HG]], channel_multiplier=-1)
                norm.roots(pool)

            @block.tensor
            def _(pe):
                pe.wait_ge(norm.ident_done, 2)
                pe.wait_ge(s_b, 1)
                for m in range(4):
                    for kb in range(2):
                        for eb in range(2):
                            c = (WB + m) * BANK + (2 * kb + eb) * HALF
                            last = nc.tensor.transpose(ps[0:HALF, c:c + HALF], raw[:, m, eb, HALF * kb:HALF * kb + HALF], ident[0:HALF, 0:HALF])
                    last.then_inc(s_t, 1)
                pe.wait_ge(s_ts, 4)
                if second:
                    for m in range(3):
                        for kb in range(2):
                            last = nc.tensor.matmul(ps[0:HALF + 1, (WB + m) * BANK:(WB + m) * BANK + DIM], bpad[:, kb, :],
                                                    WT[0:HALF, kb, m, :], start=(kb == 0), stop=(kb == 1))
                    last.then_inc(s_t, 1)
                if second:
                    pe.wait_ge(s_g, 5)

                def queries_and_keys(chunk):
                    pe.wait_ge(norm.turned, 2 * (chunk + 1))
                    for n, (mat, g_, c) in enumerate(jobs):
                        if c != chunk:
                            continue
                        wait(pe, s_e, n - 3)
                        for kb in range(2):
                            last = nc.tensor.matmul(ps[0:HALF, (WB + n % 4) * BANK:(WB + n % 4) * BANK + COLS],
                                                    WT[0:HALF + kb, kb, mat, HALF * g_:HALF * g_ + HALF],
                                                    xT[0:HALF + kb, kb, COLS * c:COLS * c + COLS], start=(kb == 0), stop=(kb == 1))
                        last.then_inc(s_qk, 1)

                norm.turn(pe, queries_and_keys)
                for n in range(IMAGES // 2):
                    wait(pe, s_vs, n - 2)
                    for i in range(2):
                        at = SEQ * (2 * n + i)
                        for kb in range(2):
                            last = nc.tensor.matmul(ps[0:SEQ, (n % 3) * BANK + DIM * i:(n % 3) * BANK + DIM * i + DIM], xT[0:HALF + kb, kb, at:at + SEQ],
                                                    WT[0:HALF + kb, kb, 2, :], start=(kb == 0), stop=(kb == 1))
                    last.then_inc(s_v, 1)

            @block.scalar
            def _(act):
                for m in range(4):
                    act.wait_ge(s_t, m + 1)
                    nc.scalar.copy(WT[0:HALF, :, m, :].rearrange("p k (e c) -> p k e c", e=2),
                                   ps[0:HALF, (WB + m) * BANK:(WB + m) * BANK + 384].rearrange("p (k e c) -> p k e c", k=2, e=2)).then_inc(s_ts, 1)
                if second:
                    act.wait_ge(s_t, 5)
                    for m in range(3):
                        nc.scalar.copy(WT[HALF:HALF + 1, 1, m, :], ps[HALF:HALF + 1, (WB + m) * BANK:(WB + m) * BANK + DIM]).then_inc(s_g, 1)
                    for kb in range(2):
                        nc.scalar.activation(WT[0:HALF, kb, 0:3, :], WT[0:HALF, kb, 0:3, :], ACT.Identity, scale=g[:, kb:kb + 1]).then_inc(s_g, 1)
                norm.copy(act)
                for n in range(IMAGES // 2):
                    act.wait_ge(s_v, n + 1)
                    nc.scalar.copy(v[:, 2 * n:2 * n + 2, :].rearrange("p i c -> p (i c)"),
                                   ps[0:SEQ, (n % 3) * BANK:(n % 3) * BANK + 2 * DIM]).then_inc(s_vs, 1)

            @block.vector
            def _(dve):
                if second:
                    nc.vector.memset(bpad[:], 0.0).then_inc(s_c, 1)
                nc.vector.memset(oT[HALF:HALF + 1, :, :], 1.0)
                norm.normalise(dve)
                for n, (mat, g_, c) in enumerate(jobs):
                    dve.wait_ge(s_qk, n + 1)
                    nc.vector.tensor_copy((qT, kT)[mat][:, g_, COLS * c:COLS * c + COLS], ps[0:HALF, (WB + n % 4) * BANK:(WB + n % 4) * BANK + COLS]).then_inc(s_e, 1)

        with ExitStack() as ctx2:
            s2 = Stage(nc, ctx2, name + "_images")
            ps = s2.psum()
            qi = [s2.sbuf(f"qi{p}", [HALF, 2, SEQ]) for p in range(2)]
            kbd = [s2.sbuf(f"kbd{p}", [HALF, 2, HG, SEQ]) for p in range(2)]
            vi = s2.sbuf("vi", [SEQ, DIM])
            mx = s2.sbuf("mx", [SEQ, 2, HG])
            rs = s2.sbuf("rs", [SEQ, HEADS])
            sums = s2.sbuf("sums", [SEQ, HEADS])
            S = s2.sbuf("S", [SEQ, 2, HG, SEQ])
            E = s2.sbuf("E", [SEQ, HEADS, SEQ])
            P = s2.sbuf("P", [SEQ, HEADS, SEQ])
            pT = s2.sbuf("pT", [SEQ, HEADS, SEQ])
            own = s2.sbuf("own", [HALF, 2])
            odd = s2.sbuf("odd", [HALF, 2, SEQ])
            names = ("q", "kbd", "sc", "mx", "sub", "exp", "sum", "rs", "p", "pt", "pts", "v", "av", "own", "odd", "sel")
            s = {n: s2.sem(n) for n in names}
            bS = ps[0:SEQ, 0:2 * BANK].rearrange("p (g c) -> p g c", g=2)[:, :, 0:HG * SEQ].rearrange("p g (h k) -> p g h k", h=HG)
            bP = ps[0:SEQ, 2 * BANK:4 * BANK].rearrange("p (g c) -> p g c", g=2)
            bA = ps[0:HALF, 4 * BANK:4 * BANK + 4 * SEQ].rearrange("p (g e q) -> p g e q", g=2, e=2)

            def live(i):
                return 0 <= i < IMAGES if isinstance(i, int) else True

            def columns(i):
                return bass.ds(i * SEQ, SEQ)

            def schedule(eng, body):
                for t in range(6):
                    body(t, t % 2)
                with eng.Fori(6, IMAGES - 1, 2) as t:
                    body(t, 0)
                    body(t + 1, 1)
                for t in range(IMAGES, IMAGES + 4):
                    body(t, t % 2)

            block = ctx2.enter_context(nc.Block())

            @block.gpsimd
            def _(pool):
                def body(t, p):
                    k = t - 2
                    if live(t):
                        wait(pool, s["sc"], t - 1)
                        nc.gpsimd.tensor_copy(qi[p][:], qT[:, :, columns(t)]).then_inc(s["q"], 1)
                        for g_ in range(2):
                            last = nc.gpsimd.tensor_tensor(kbd[p][:, g_, :, :], spread(kT[:, g_, columns(t)], 1, HG), spread(mask[:], 2, SEQ), ALU.mult)
                        last.then_inc(s["kbd"], 1)
                    if live(k):
                        pool.wait_ge(s["rs"], k + 1)
                        wait(pool, s["pt"], k)
                        nc.gpsimd.tensor_tensor(P[:], E[:], spread(rs[:], 2, SEQ), ALU.mult).then_inc(s["p"], 1)

                schedule(pool, body)

            @block.vector
            def _(dve):
                for e in range(2):
                    nc.vector.reduce_sum(own[:, e:e + 1], mask[:, e::2], axis=AX_X).then_inc(s["own"], 1)
                dve.wait_ge(s["own"], 2)

                def body(t, p):
                    m, k, n = t - 1, t - 2, t - 4
                    if live(k):
                        dve.wait_ge(s["exp"], k + 1)
                        nc.vector.reduce_sum(sums[:], E[:], axis=AX_X).then_inc(s["sum"], 1)
                        dve.wait_ge(s["sum"], k + 1)
                        wait(dve, s["p"], k)
                        nc.vector.reciprocal(rs[:], sums[:]).then_inc(s["rs"], 1)
                    if live(n):
                        dve.wait_ge(s["av"], n + 1)
                        nc.vector.tensor_scalar(odd[:], bA[:, :, 1, :], own[:, 1:2], None, ALU.mult).then_inc(s["odd"], 1)
                        dve.wait_ge(s["odd"], n + 1)
                        nc.vector.scalar_tensor_tensor(oT[0:HALF, :, columns(n)], bA[:, :, 0, :], own[:, 0:1], odd[:], ALU.mult, ALU.add).then_inc(s["sel"], 1)
                    if live(m):
                        dve.wait_ge(s["sc"], m + 1)
                        nc.vector.reduce_max(mx[:], bS, axis=AX_X).then_inc(s["mx"], 1)
                        dve.wait_ge(s["mx"], m + 1)
                        wait(dve, s["exp"], m)
                        nc.vector.tensor_tensor(S[:], bS, spread(mx[:], 3, SEQ), ALU.subtract).then_inc(s["sub"], 1)

                schedule(dve, body)

            @block.scalar
            def _(act):
                def body(t, p):
                    m, l = t - 1, t - 3
                    if live(l):
                        wait(act, s["av"], l)
                        nc.scalar.copy(vi[:], v[:, bass.ds(l, 1), :].rearrange("p a c -> p (a c)")).then_inc(s["v"], 1)
                        act.wait_ge(s["pt"], l + 1)
                        nc.scalar.copy(pT[:].rearrange("p (g h) k -> p g (h k)", g=2), bP[:, :, 0:HG * SEQ]).then_inc(s["pts"], 1)
                    if live(m):
                        act.wait_ge(s["sub"], m + 1)
                        wait(act, s["p"], m)
                        nc.scalar.activation(E[:].rearrange("p h k -> p (h k)"), S[:].rearrange("p g h k -> p (g h k)"), ACT.Exp,
                                             scale=0.25).then_inc(s["exp"], 1)

                schedule(act, body)

            @block.tensor
            def _(pe):
                def body(t, p):
                    m, l = t - 1, t - 3
                    if live(l):
                        pe.wait_ge(s["p"], l + 1)
                        wait(pe, s["pts"], l)
                        for h in range(HEADS):
                            c = SEQ * (h % HG)
                            last = nc.tensor.transpose(bP[:, h // HG, c:c + SEQ], P[:, h, :], ident[0:SEQ, 0:SEQ])
                        last.then_inc(s["pt"], 1)
                    if live(m):
                        pe.wait_ge(s["kbd"], m + 1)
                        pe.wait_ge(s["q"], m + 1)
                        wait(pe, s["sub"], m)
                        for g_ in range(2):
                            last = nc.tensor.matmul(bS[:, g_, :, :].rearrange("p h k -> p (h k)"), qi[1 - p][:, g_, :],
                                                    kbd[1 - p][:, g_, :, :].rearrange("p h k -> p (h k)"), start=True, stop=True)
                        last.then_inc(s["sc"], 1)
                    if live(l):
                        pe.wait_ge(s["pts"], l + 1)
                        pe.wait_ge(s["v"], l + 1)
                        wait(pe, s["sel"], l)
                        for pair in range(HEADS // 2):
                            g_, j = divmod(pair, HG // 2)
                            last = nc.tensor.matmul(bA[32 * j:32 * j + 32, g_, :, :].rearrange("p e q -> p (e q)"), vi[:, 32 * pair:32 * pair + 32],
                                                    pT[:, 2 * pair:2 * pair + 2, :].rearrange("p h q -> p (h q)"), start=True, stop=True)
                        last.then_inc(s["av"], 1)

                schedule(pe, body)

        with ExitStack() as ctx2:
            s2 = Stage(nc, ctx2, name + "_last")
            ps = s2.psum()
            s_pr, s_res = s2.sem("pr"), s2.sem("res")
            block = ctx2.enter_context(nc.Block())

            @block.tensor
            def _(pe):
                for i in range(NTILE):
                    wait(pe, s_res, i - 7)
                    for kb in range(2):
                        last = nc.tensor.matmul(ps[0:TILE, (i % 8) * BANK:(i % 8) * BANK + DIM], oT[0:HALF + kb, kb, TILE * i:TILE * i + TILE],
                                                WT[0:HALF + kb, kb, 3, :], start=(kb == 0), stop=(kb == 1))
                    last.then_inc(s_pr, 1)

            @block.vector
            def _(dve):
                for i in range(NTILE):
                    dve.wait_ge(s_pr, i + 1)
                    nc.vector.tensor_tensor(rows[:, i, :], ps[0:TILE, (i % 8) * BANK:(i % 8) * BANK + DIM], rows[:, i, :], ALU.add).then_inc(s_res, 1)
                    if i >= 1:
                        dve.wait_ge(s_res, i)
                        nc.vector.bn_stats(stats[:, i - 1, :], rows[:, i - 1, :])
                dve.wait_ge(s_res, NTILE)
                nc.vector.bn_stats(stats[:, NTILE - 1, :], rows[:, NTILE - 1, :])


CHUNK, NCHUNK, LANES = 64, 3, TOKENS // 2
STATE = 16


class NormedColumns:
    BANKS = 2
    PER = 4
    COPIES = 2 * (NTILE // PER)

    def __init__(self, nc, st, ps, src, rows, xT, ident, xn, affine=None, raw=None, known=None):
        self.nc, self.ps, self.src, self.rows, self.xT, self.ident, self.xn = nc, ps, src, rows, xT, ident, xn
        self.affine, self.raw, self.rounds = affine, raw, 2 if raw is not None else 1
        self.known = known
        self.stats = st.sbuf("norm_stats", [TILE, NTILE, 6]) if known is None or raw is not None else None
        self.tmp = st.sbuf("norm_tmp", [TILE, 3, NTILE])
        self.rstd = st.sbuf("norm_rstd", [TILE, NTILE])
        self.mhalf = st.sbuf("norm_mhalf", [TILE, NTILE])
        self.gb = st.sbuf("norm_gb", [HALF, 2, 2])
        self.loaded, self.gains, self.ident_done, self.consts, self.stat, self.moment, self.root, self.normed, self.in_psum, self.turned = (
            st.sem("norm_" + n) for n in ("loaded", "gains", "ident", "consts", "stat", "moment", "root", "normed", "in_psum", "turned"))

    def load(self, sp):
        if self.src is not None:
            sp.dma_start(self.rows[:], dram(self.src, 0, [(DIM, TILE), (TILE * DIM, NTILE), (1, DIM)])).then_inc(self.loaded, 16)
        if self.affine:
            with self.nc.allow_non_contiguous_dma(reason="columns of the norm's gain and bias"):
                for n in range(2):
                    for kb in range(2):
                        sp.dma_start(self.gb[:, n, kb:kb + 1], dram(self.affine[n], HALF * kb, [(1, HALF), (1, 1)])).then_inc(self.gains, 16)

    def constants(self, pool):
        make_identity(self.nc, pool, self.ident, self.ident_done)
        self.nc.gpsimd.memset(self.mhalf[:], -0.5).then_inc(self.consts, 1)

    def roots(self, pool):
        pool.wait_ge(self.consts, 1)
        for r in range(self.rounds):
            pool.wait_ge(self.moment, 7 * (r + 1))
            self.nc.gpsimd.tensor_tensor(self.rstd[:], self.tmp[:, 2, :], self.mhalf[:], ALU.pow).then_inc(self.root, 1)

    def normalise(self, dve):
        nc, rows, tmp = self.nc, self.rows, self.tmp
        nc.vector.memset(self.xT[HALF:HALF + 1, :, :], 1.0)
        if self.src is not None:
            dve.wait_ge(self.loaded, 16)
        for r in range(self.rounds):
            frm = self.raw if r < self.rounds - 1 else rows
            if r == 0 and self.known is not None:
                stats = self.known
            else:
                stats = self.stats
                for i in range(NTILE):
                    wait(dve, self.normed, i + 1 if r else 0)
                    nc.vector.bn_stats(stats[:, i, :], frm[:, i, :]).then_inc(self.stat, 1)
                dve.wait_ge(self.stat, NTILE * (1 if self.known is not None else r + 1))
            moments(nc, dve, stats[:], [tmp[:, n, :] for n in range(3)], self.moment, 7 * r)
            dve.wait_ge(self.root, r + 1)
            to = self.xn if r == self.rounds - 1 else rows
            for i in range(NTILE):
                nc.vector.tensor_scalar(to[:, i, :], frm[:, i, :], tmp[:, 0, i:i + 1], self.rstd[:, i:i + 1], ALU.subtract, ALU.mult).then_inc(self.normed, 1)

    def turn(self, pe, then=None):
        for n in range(self.COPIES):
            g, kb = n // 2, n % 2
            wait(pe, self.turned, n - self.BANKS + 1)
            for j in range(self.PER):
                tile = self.PER * g + j
                pe.wait_ge(self.normed, NTILE * (self.rounds - 1) + tile + 1)
                c = (1 + n % self.BANKS) * BANK + TILE * j
                last = self.nc.tensor.transpose(self.ps[0:HALF, c:c + TILE], self.xn[:, tile, HALF * kb:HALF * kb + HALF], self.ident[0:TILE, 0:TILE])
            last.then_inc(self.in_psum, 1)
            if then and kb == 1 and g >= 1:
                then(g - 1)
        if then:
            then(self.COPIES // 2 - 1)

    def copy(self, act):
        if self.affine:
            act.wait_ge(self.gains, 64)
        for n in range(self.COPIES):
            g, kb = n // 2, n % 2
            act.wait_ge(self.in_psum, n + 1)
            out = self.xT[0:HALF, kb, self.PER * TILE * g:self.PER * TILE * (g + 1)]
            got = self.ps[0:HALF, (1 + n % self.BANKS) * BANK:(1 + n % self.BANKS) * BANK + self.PER * TILE]
            if self.affine:
                self.nc.scalar.activation(out, got, ACT.Identity, scale=self.gb[:, 0, kb:kb + 1], bias=self.gb[:, 1, kb:kb + 1]).then_inc(self.turned, 1)
            else:
                self.nc.scalar.copy(out, got).then_inc(self.turned, 1)


def state_space(nc, name, rows, known, stats, abc, w):
    GROUP = 4 * SEQ
    groups = TOKENS // GROUP
    NL1 = 11
    with ExitStack() as ctx:
        st = Stage(nc, ctx, name)
        delta = st.sbuf("delta", [PARTS, NCHUNK, LANES])
        u = st.sbuf("u", [PARTS, NCHUNK, LANES])
        dt = st.sbuf("dt", [PARTS, NCHUNK])
        mdt = st.sbuf("mdt", [PARTS, NCHUNK])
        ident = st.sbuf("ident", [PARTS, PARTS])
        diag = st.sbuf("diag", [PARTS, NCHUNK, PARTS])
        with ExitStack() as ctx2:
            s2 = Stage(nc, ctx2, name + "_mlp")
            xT = s2.sbuf("xT", [HALF + 1, 2, TOKENS])
            W1 = s2.sbuf("W1", [HALF + 1, 2, 1344])
            W2 = s2.sbuf("W2", [PARTS, 9, HALF])
            W2d = s2.sbuf("W2d", [HALF, 2, DIM])
            b2 = s2.sbuf("b2", [HALF, 1])
            b2d = s2.sbuf("b2d", [PARTS, NCHUNK])
            Dc = s2.sbuf("D", [PARTS, NCHUNK])
            ldt = s2.sbuf("ldt", [PARTS, NCHUNK])
            hid = [s2.sbuf(f"hid{p}", [PARTS, NL1, GROUP]) for p in range(2)]
            ABC = s2.sbuf("ABC", [HALF, TOKENS])
            xn = s2.sbuf("xn", [TILE, NTILE, DIM])
            ps = s2.psum()
            norm = NormedColumns(nc, s2, ps, None, rows, xT, ident, xn, known=known)
            s_w, s_z, s_l1, s_act, s_l2, s_e2, s_u, s_abc, s_dt, s_dg, s_c = (
                s2.sem(n) for n in ("w", "z", "l1", "act", "l2", "e2", "u", "abc", "dt", "dg", "c"))
            block = ctx2.enter_context(nc.Block())
            NB2 = 6
            wload = [0]

            @block.sync
            def _(sp):
                ctx2.enter_context(nc.allow_non_contiguous_dma(reason="columns of biases"))
                norm.load(sp)
                n = 0
                sp.wait_ge(s_z, 1)
                c = 0
                for m in "ABCd":
                    wide = DIM if m == "d" else 2 * DIM
                    sp.dma_start(W1[0:HALF, :, c:c + wide], dram(w[m + "_w1"], 0, [(wide, HALF), (HALF * wide, 2), (1, wide)])).then_inc(s_w, 16)
                    sp.dma_start(W1[HALF:HALF + 1, 1, c:c + wide], dram(w[m + "_b1"], 0, [(wide, 1), (1, wide)])).then_inc(s_w, 16)
                    c += wide
                    n += 2
                for i, m in enumerate("ABC"):
                    sp.dma_start(W2[:, 3 * i:3 * i + 3, 32 * i:32 * i + STATE], dram(w[m + "_w2"], 0, [(STATE, PARTS), (PARTS * STATE, 3), (1, STATE)])).then_inc(s_w, 16)
                    sp.dma_start(b2[32 * i:32 * i + STATE, :], dram(w[m + "_b2"], 0, [(1, STATE), (1, 1)])).then_inc(s_w, 16)
                    n += 2
                sp.dma_start(W2d[:], dram(w["d_w2"], 0, [(DIM, HALF), (HALF * DIM, 2), (1, DIM)])).then_inc(s_w, 16)
                n += 1
                for half in range(2):
                    p = slice(CHUNK * half, CHUNK * half + CHUNK)
                    for to, frm in ((b2d, "d_b2"), (Dc, "D_param"), (ldt, "log_dt")):
                        sp.dma_start(to[p, :].unsqueeze(2), dram(w[frm], 0, [(1, CHUNK), (CHUNK, NCHUNK), (1, 1)])).then_inc(s_w, 16)
                        n += 1
                sp.wait_ge(s_w, 16 * n)
                sp.sem_inc(s_c, 1)
                sp.wait_ge(norm.turned, norm.COPIES)
                for half in range(2):
                    for c in range(NCHUNK):
                        d = c * CHUNK
                        while d < (c + 1) * CHUNK:
                            kb, r = divmod(d, HALF)
                            k = min((c + 1) * CHUNK - d, HALF - r)
                            p0 = CHUNK * half + d - c * CHUNK
                            sp.dma_start(u[p0:p0 + k, c, :], xT[r:r + k, kb, LANES * half:LANES * half + LANES]).then_inc(s_u, 16)
                            d += k
                sp.wait_ge(s_e2, NB2 * groups)
                for i in range(3):
                    sp.dma_start(dram(abc, i * STATE * TOKENS, [(TOKENS, STATE), (1, TOKENS)]), ABC[32 * i:32 * i + STATE, :]).then_inc(s_abc, 16)
                sp.wait_ge(s_abc, 48)
                sp.wait_ge(s_u, 16 * 8)

            @block.gpsimd
            def _(pool):
                nc.gpsimd.memset(W2[:], 0.0).then_inc(s_z, 1)
                norm.constants(pool)
                norm.roots(pool)

            @block.vector
            def _(dve):
                norm.normalise(dve)
                dve.wait_ge(s_dt, 1)
                nc.vector.tensor_scalar(mdt[:], dt[:], -1.0, None, ALU.mult)
                dve.wait_ge(norm.ident_done, 2)
                for c in range(NCHUNK):
                    nc.vector.tensor_scalar(diag[:, c, :], ident[:], Dc[:, c:c + 1], None, ALU.mult).then_inc(s_dg, 1)

            def l1(ft):
                return (PARTS * ft, PARTS) if ft < 9 else (9 * PARTS + HALF * (ft - 9), HALF)

            @block.tensor
            def _(pe):
                pe.wait_ge(norm.ident_done, 2)
                norm.turn(pe)
                pe.wait_ge(norm.turned, norm.COPIES)
                pe.wait_ge(s_c, 1)

                def layer2(g):
                    half = g // (groups // 2)
                    pe.wait_ge(s_act, NL1 * (g + 1))
                    wait(pe, s_e2, NB2 * g)
                    for ft in range(9):
                        last = nc.tensor.matmul(ps[0:HALF, 4 * BANK:4 * BANK + GROUP], W2[:, ft, :], hid[g % 2][:, ft, :],
                                                start=(ft == 0), stop=(ft == 8))
                    last.then_inc(s_l2, 1)
                    p = slice(CHUNK * half, CHUNK * half + CHUNK)
                    for c in range(NCHUNK):
                        for kb in range(2):
                            last = nc.tensor.matmul(ps[p, (5 + c) * BANK:(5 + c) * BANK + GROUP], W2d[:, kb, CHUNK * c:CHUNK * c + CHUNK],
                                                    hid[g % 2][0:HALF, 9 + kb, :], start=(kb == 0), stop=(kb == 1))
                        last.then_inc(s_l2, 1)

                for g in range(groups):
                    for ft in range(NL1):
                        c0, rows_ = l1(ft)
                        n = NL1 * g + ft
                        wait(pe, s_act, n - 3)
                        for kb in range(2):
                            k = HALF + kb
                            last = nc.tensor.matmul(ps[0:rows_, (n % 4) * BANK:(n % 4) * BANK + GROUP], W1[0:k, kb, c0:c0 + rows_],
                                                    xT[0:k, kb, GROUP * g:GROUP * g + GROUP], start=(kb == 0), stop=(kb == 1))
                        last.then_inc(s_l1, 1)
                    if g >= 1:
                        layer2(g - 1)
                layer2(groups - 1)

            @block.scalar
            def _(act):
                norm.copy(act)
                act.wait_ge(s_c, 1)
                nc.scalar.activation(dt[:], ldt[:], ACT.Exp).then_inc(s_dt, 1)

                def evacuate2(g):
                    half = g // (groups // 2)
                    cols = slice(GROUP * g, GROUP * g + GROUP)
                    act.wait_ge(s_l2, 4 * g + 1)
                    for i in range(3):
                        p = slice(32 * i, 32 * i + STATE)
                        nc.scalar.activation(ABC[p, cols], ps[p, 4 * BANK:4 * BANK + GROUP], ACT.Abs if i == 0 else ACT.Identity,
                                             bias=b2[p, 0:1]).then_inc(s_e2, 1)
                    p = slice(CHUNK * half, CHUNK * half + CHUNK)
                    here = slice(GROUP * (g % (groups // 2)), GROUP * (g % (groups // 2) + 1))
                    for c in range(NCHUNK):
                        act.wait_ge(s_l2, 4 * g + 2 + c)
                        nc.scalar.activation(delta[p, c, here], ps[p, (5 + c) * BANK:(5 + c) * BANK + GROUP], ACT.Identity,
                                             bias=b2d[p, c:c + 1]).then_inc(s_e2, 1)

                for g in range(groups):
                    for ft in range(NL1):
                        _, rows_ = l1(ft)
                        n = NL1 * g + ft
                        act.wait_ge(s_l1, n + 1)
                        if g >= 2 and ft == 0:
                            act.wait_ge(s_l2, 4 * (g - 1))
                        nc.scalar.activation(hid[g % 2][0:rows_, ft, :], ps[0:rows_, (n % 4) * BANK:(n % 4) * BANK + GROUP],
                                             ACT.Silu).then_inc(s_act, 1)
                    if g >= 1:
                        evacuate2(g - 1)
                evacuate2(groups - 1)
                act.wait_ge(s_e2, NB2 * groups)
                nc.scalar.activation(delta[:].rearrange("p c t -> p (c t)"), delta[:].rearrange("p c t -> p (c t)"), ACT.Sigmoid)

        with ExitStack() as ctx2:
            s2 = Stage(nc, ctx2, name + "_scan")
            ps = s2.psum()
            bc = [s2.sbuf(f"bc{p}", [PARTS, 3, LANES]) for p in range(2)]
            gain = s2.sbuf("gain", [PARTS, NCHUNK, LANES])
            dA = [s2.sbuf(f"dA{p}", [PARTS, LANES]) for p in range(2)]
            wb = [s2.sbuf(f"wb{p}", [PARTS, LANES]) for p in range(2)]
            coef = [s2.sbuf(f"coef{p}", [PARTS, LANES]) for p in range(2)]
            inp = [s2.sbuf(f"inp{p}", [PARTS, LANES]) for p in range(2)]
            S = [s2.sbuf(f"S{p}", [PARTS, LANES]) for p in range(2)]
            prod = [s2.sbuf(f"prod{p}", [PARTS, LANES]) for p in range(2)]
            s_bc = [s2.sem(f"bc{p}") for p in range(2)]
            s_g, s_d0, s_da, s_w, s_wd, s_coef, s_inp, s_scan, s_prod, s_acc, s_ys, s_t, s_res, s_ld = (
                s2.sem(n) for n in ("g", "d0", "da", "w", "wd", "coef", "inp", "scan", "prod", "acc", "ys", "t", "res", "ld"))
            yS = gain

            def pieces(c):
                at = c * LANES
                while at < (c + 1) * LANES:
                    to = min((c + 1) * LANES, (at // BANK + 1) * BANK)
                    yield at, to
                    at = to

            def schedule(eng, body, tail=0):
                for n in range(4):
                    body(n, n % 2)
                with eng.Fori(4, STATE, 2) as n:
                    body(n, 0)
                    body(n + 1, 1)

            block = ctx2.enter_context(nc.Block())

            @block.sync
            def _(sp):
                def body(n, p):
                    wait(sp, s_prod, 3 * (n - 1))
                    sp.sem_inc(s_ld, 1)
                    for i in range(3):
                        sp.dma_start(bc[p][:, i, :], dram(abc, (i * STATE + n) * TOKENS, [(LANES, 2), (0, CHUNK), (1, LANES)])).then_inc(s_bc[p], 16)

                schedule(sp, body)

            def loaded(eng, n, p):
                eng.wait_ge(s_bc[p], 48 * (n - p + 2) // 2 if isinstance(n, int) else (n - p) * 24 + 48)

            @block.scalar
            def _(act):
                def body(n, p):
                    loaded(act, n, p)
                    for c in range(NCHUNK):
                        j = 3 * n + c
                        q = (3 * p + c) % 2
                        wait(act, s_inp, j - 1)
                        nc.scalar.activation(dA[q][:], bc[p][:, 0, :], ACT.Exp, scale=mdt[:, c:c + 1]).then_inc(s_da, 1)

                schedule(act, body)
                act.wait_ge(s_acc, 3 * STATE)
                for c in range(NCHUNK):
                    nc.scalar.copy(yS[:, c, :], ps[:, LANES * c:LANES * c + LANES]).then_inc(s_ys, 1)

            @block.gpsimd
            def _(pool):
                def prods(j, p, q):
                    pool.wait_ge(s_scan, j + 1)
                    wait(pool, s_acc, j - 1)
                    nc.gpsimd.tensor_tensor(prod[q][:], S[q][:], bc[p][:, 2, :], ALU.mult).then_inc(s_prod, 1)

                pool.wait_ge(s_g, 5)

                def body(n, p):
                    loaded(pool, n, p)
                    for c in range(NCHUNK):
                        j = 3 * n + c
                        q = (3 * p + c) % 2
                        if c < NCHUNK - 1:
                            wait(pool, s_inp, j - 1)
                            nc.gpsimd.tensor_tensor(wb[q][:], gain[:, c, :], bc[p][:, 1, :], ALU.mult).then_inc(s_w, 1)
                        if not isinstance(n, int) or j >= 1:
                            prods(j - 1, p if c else 1 - p, 1 - q)

                schedule(pool, body)
                prods(3 * STATE - 1, 1, (3 * STATE - 1) % 2)

            @block.vector
            def _(dve):
                nc.vector.tensor_scalar(gain[:], delta[:], -1.0, 1.0, ALU.mult, ALU.add).then_inc(s_g, 1)
                dve.wait_ge(s_g, 1)
                nc.vector.tensor_tensor(gain[:], gain[:], u[:], ALU.mult).then_inc(s_g, 1)
                dve.wait_ge(s_g, 2)
                for c in range(NCHUNK):
                    nc.vector.tensor_scalar(gain[:, c, :], gain[:, c, :], dt[:, c:c + 1], None, ALU.mult).then_inc(s_g, 1)
                nc.vector.memset(delta[:].rearrange("p c (b l) -> p (c b) l", l=SEQ)[:, :, 0:1], 0.0).then_inc(s_d0, 1)
                dve.wait_ge(s_d0, 1)

                def body(n, p):
                    for c in range(NCHUNK):
                        j = 3 * n + c
                        q = (3 * p + c) % 2
                        dve.wait_ge(s_da, j + 1)
                        wait(dve, s_scan, j - 1)
                        nc.vector.tensor_tensor(coef[q][:], delta[:, c, :], dA[q][:], ALU.mult).then_inc(s_coef, 1)
                        if c < NCHUNK - 1:
                            dve.wait_ge(s_w, (NCHUNK - 1) * n + c + 1)
                        else:
                            loaded(dve, n, p)
                            nc.vector.tensor_tensor(wb[q][:], gain[:, c, :], bc[p][:, 1, :], ALU.mult).then_inc(s_wd, 1)
                            dve.wait_ge(s_wd, n + 1)
                        nc.vector.tensor_tensor(inp[q][:], wb[q][:], dA[q][:], ALU.mult).then_inc(s_inp, 1)
                        dve.wait_ge(s_coef, j + 1)
                        dve.wait_ge(s_inp, j + 1)
                        wait(dve, s_prod, j - 1)
                        nc.vector.tensor_tensor_scan(S[q][:], coef[q][:], inp[q][:], 0.0, ALU.mult, ALU.add).then_inc(s_scan, 1)

                schedule(dve, body)
                for t in range(10):
                    dve.wait_ge(s_t, t + 1)
                    out = rows[:, t::10, :].rearrange("p h (c d) -> p c h d", c=NCHUNK)
                    nc.vector.tensor_tensor(out, ps[0:TILE, (t % 8) * BANK:(t % 8) * BANK + 384].rearrange("p (c h d) -> p c h d", c=NCHUNK, h=2),
                                            out, ALU.add).then_inc(s_res, 1)
                    dve.wait_ge(s_res, t + 1)
                    for i in (t, t + 10):
                        nc.vector.bn_stats(stats[:, i, :], rows[:, i, :])

            @block.tensor
            def _(pe):
                begun = set()
                for c in range(NCHUNK):
                    for a, b in pieces(c):
                        nc.tensor.matmul(ps[:, a:b], diag[:, c, :], u[:, c, a - LANES * c:b - LANES * c], start=(a // BANK not in begun),
                                         stop=True, skip_group_check=True)
                        begun.add(a // BANK)

                def body(n, p):
                    for c in range(NCHUNK):
                        j = 3 * n + c
                        q = (3 * p + c) % 2
                        pe.wait_ge(s_prod, j + 1)
                        for a, b in pieces(c):
                            last = nc.tensor.matmul(ps[:, a:b], ident[:], prod[q][:, a - LANES * c:b - LANES * c], start=False, stop=True,
                                                    skip_group_check=True)
                        last.then_inc(s_acc, 1)

                schedule(pe, body)
                pe.wait_ge(s_ys, 3)
                for t in range(10):
                    wait(pe, s_res, t - 7)
                    for c in range(NCHUNK):
                        last = nc.tensor.transpose(ps[0:TILE, (t % 8) * BANK + PARTS * c:(t % 8) * BANK + PARTS * c + PARTS],
                                                   yS[:, c, TILE * t:TILE * t + TILE], ident[:])
                    last.then_inc(s_t, 1)


EXPERTS = 8


def experts(nc, name, rows, base, h_out, known, stats, xs, ys, w, gated):
    slots = 1 if gated else 2
    ntiles = (slots * TOKENS + PARTS - 1) // PARTS + EXPERTS - 1
    ntiles += ntiles % 2
    hidden = 469 if gated else 768
    fts = [(c, min(PARTS, hidden - c)) for c in range(0, hidden, PARTS)]
    nft = len(fts)
    wide = 2 * hidden if gated else hidden
    cut = hidden if gated else hidden // 2
    with ExitStack() as ctx:
        st = Stage(nc, ctx, name)
        pos = [st.sbuf(f"pos{k}", [TILE, NTILE], U32) for k in range(slots)]
        score = [st.sbuf(f"score{k}", [TILE, NTILE]) for k in range(slots)]
        texp = st.sbuf("texp", [1, ntiles], I32)
        ident = st.sbuf("ident", [PARTS, PARTS])
        W1 = st.sbuf("W1", [HALF + 1, 2, EXPERTS, wide])
        W2 = st.sbuf("W2", [PARTS, nft, EXPERTS, DIM])
        B2 = None if gated else st.sbuf("B2", [PARTS, EXPERTS, DIM])

        with ExitStack() as ctx2:
            s2 = Stage(nc, ctx2, name + "_route")
            xT = s2.sbuf("xT", [HALF + 1, 2, TOKENS])
            xn = s2.sbuf("xn", [TILE, NTILE, DIM])
            ps = s2.psum()
            norm = NormedColumns(nc, s2, ps, None, rows, xT, ident, xn, None if gated else (w["lng"], w["lnb"]), known=known)
            zeros = s2.sbuf("zeros", [PARTS, 4 * DIM])
            graw = s2.sbuf("graw", [EXPERTS, DIM + 1])
            GT = s2.sbuf("GT", [HALF + 1, 2, EXPERTS])
            L = s2.sbuf("L", [TILE, NTILE, EXPERTS])
            best = [s2.sbuf(f"best{k}", [TILE, NTILE]) for k in range(slots)]
            OH = [s2.sbuf(f"OH{k}", [TILE, NTILE, EXPERTS]) for k in range(slots)]
            both = s2.sbuf("both", [TILE, NTILE, EXPERTS])
            key = s2.sbuf("key", [TILE, NTILE, EXPERTS])
            top = s2.sbuf("top", [TILE, NTILE])
            order_i, order = s2.sbuf("order_i", [TILE, EXPERTS], I32), s2.sbuf("order", [TILE, EXPERTS])
            NTH = TOKENS // PARTS + 1
            thr_i, thr = s2.sbuf("thr_i", [TILE, NTH], I32), s2.sbuf("thr", [TILE, NTH])
            tn_i, tn = s2.sbuf("tn_i", [1, ntiles], I32), s2.sbuf("tn", [1, ntiles])
            upper = s2.sbuf("upper", [TILE, TILE])
            ones = s2.sbuf("ones", [TILE, TILE])
            chain0 = s2.sbuf("chain0", [TILE, EXPERTS, NTILE])
            tot = s2.sbuf("tot", [TILE, EXPERTS, NTILE])
            incl = s2.sbuf("incl", [TILE, EXPERTS, NTILE])
            over = s2.sbuf("over", [TILE, EXPERTS, NTH])
            nt, ntin = s2.sbuf("nt", [TILE, EXPERTS]), s2.sbuf("ntin", [TILE, EXPERTS])
            start = s2.sbuf("start", [TILE, EXPERTS])
            place = s2.sbuf("place", [TILE, NTILE, EXPERTS])
            pf = s2.sbuf("pf", [TILE, NTILE])
            tge = s2.sbuf("tge", [1, ntiles, EXPERTS])
            te = s2.sbuf("te", [1, ntiles])
            s_g, s_fill, s_zero, s_gt, s_gts, s_lg, s_cst, s_v, s_oh, s_rank, s_pos, s_exp, s_sc, s_up = (
                s2.sem(n) for n in ("g", "fill", "zero", "gt", "gts", "lg", "cst", "v", "oh", "rank", "pos", "exp", "sc", "up"))
            parts1 = 2 if gated else 1
            raw1 = [s2.sbuf(f"raw1{p}", [PARTS, parts1, nft, DIM]) for p in range(2)]
            raw2 = [s2.sbuf(f"raw2{p}", [HALF, 2, hidden]) for p in range(2)]
            s_in = [s2.sem(f"in{p}") for p in range(2)]
            s_b, s_t, s_e, s_gate = s2.sem("b"), s2.sem("t"), s2.sem("e"), s2.sem("gate")
            whole = hidden // PARTS
            left = hidden - whole * PARTS
            jobs = []
            for part in range(parts1):
                for kb in range(2):
                    for f0 in range(0, nft, 4):
                        jobs.append((1, part, kb, fts[f0:f0 + 4]))
            for f0, (c0, k) in enumerate(fts):
                jobs.append((2, f0, 0, [(c0, k)]))
            njobs = len(jobs)
            nbanks = njobs // 2
            ndma = (parts1 * (2 if left else 1)) + 1

            def first_experts(body):
                body(0, 0)
                body(1, 1)

            def other_experts(eng, body, between=None):
                body(2, 0)
                if between:
                    between()
                body(3, 1)
                with eng.Fori(4, EXPERTS - 1, 2) as e:
                    body(e, 0)
                    body(e + 1, 1)

            block = ctx2.enter_context(nc.Block())

            @block.sync
            def _(sp):
                norm.load(sp)
                with nc.allow_non_contiguous_dma(reason="eight biases"):
                    sp.dma_start(graw[:, 0:DIM], w["gate_w"]).then_inc(s_g, 16)
                    sp.dma_start(graw[:, DIM:], dram(w["gate_b"], 0, [(1, EXPERTS), (1, 1)])).then_inc(s_g, 16)
                def body(e, p):
                    wait(sp, s_t, njobs * (e - 1))
                    sp.sem_inc(s_gate, 1)
                    for part in range(parts1):
                        frm = w["w1"][part]
                        sp.dma_start(raw1[p][:, part, 0:whole, :], dram(frm, e * (hidden * DIM), [(DIM, PARTS), (PARTS * DIM, whole), (1, DIM)])).then_inc(s_in[p], 16)
                        if left:
                            sp.dma_start(raw1[p][0:left, part, whole, :], dram(frm, e * (hidden * DIM) + whole * PARTS * DIM, [(DIM, left), (1, DIM)])).then_inc(s_in[p], 16)
                    sp.dma_start(raw2[p][:], dram(w["w2"], e * (hidden * DIM), [(hidden, HALF), (HALF * hidden, 2), (1, hidden)])).then_inc(s_in[p], 16)

                first_experts(body)
                if not gated:
                    sp.dma_start(W1[HALF:HALF + 1, 1, :, :].rearrange("p e c -> p (e c)"), dram(w["b1"], 0, [(EXPERTS * hidden, 1), (1, EXPERTS * hidden)])).then_inc(s_b, 16)
                    sp.dma_start(B2[:].rearrange("p e c -> p (e c)"), dram(w["b2"], 0, [(0, PARTS), (1, EXPERTS * DIM)])).then_inc(s_b, 16)
                sp.wait_ge(s_zero, 1)
                for n in range(0, ntiles, 4):
                    sp.dma_start(dram(xs, n * PARTS * DIM, [(4 * DIM, PARTS), (1, 4 * DIM)]), zeros[:]).then_inc(s_fill, 16)
                other_experts(sp, body)
                if not gated:
                    sp.wait_ge(s_b, 32)
                sp.wait_ge(s_fill, 16 * (ntiles // 4))

            @block.gpsimd
            def _(pool):
                norm.constants(pool)
                nc.gpsimd.iota(order_i[:], pattern=[[-1, EXPERTS]], base=EXPERTS, channel_multiplier=0)
                nc.gpsimd.iota(thr_i[:], pattern=[[PARTS, NTH]], base=0, channel_multiplier=0)
                nc.gpsimd.iota(tn_i[:], pattern=[[1, ntiles]], base=0, channel_multiplier=0).then_inc(s_cst, 1)
                pool.wait_ge(s_cst, 1)
                nc.gpsimd.memset(upper[:], 1.0).then_inc(s_up, 1)
                nc.gpsimd.memset(ones[:], 1.0)
                pool.wait_ge(s_up, 1)
                nc.gpsimd.affine_select(out=upper[:], in_=upper[:], compare_op=ALU.is_gt, fill=0.0, base=0,
                                        pattern=[[1, TILE]], channel_multiplier=-1).then_inc(s_up, 1)
                nc.gpsimd.memset(zeros[:], 0.0).then_inc(s_zero, 1)
                norm.roots(pool)
                pool.wait_ge(s_fill, 16 * (ntiles // 4))
                for k in range(slots):
                    pool.wait_ge(s_pos, k + 1)
                    for i in range(NTILE):
                        nc.gpsimd.indirect_dma_start(out=xs, out_offset=bass.IndirectOffsetOnAxis(ap=pos[k][:, i:i + 1], axis=0),
                                                     in_=xn[:, i, :], in_offset=None).then_inc(s_sc, 16)
                pool.wait_ge(s_sc, 16 * NTILE * slots)

            @block.tensor
            def _(pe):
                def body(e, p):
                    pe.wait_ge(s_in[p], 16 * ndma * (e - p + 2) // 2 if isinstance(e, int) else (e - p) * (8 * ndma) + 16 * ndma)
                    for n, (kind, a, kb, ts) in enumerate(jobs):
                        wait(pe, s_e, njobs * e + n - (nbanks - 1))
                        b = (3 + n % nbanks) * BANK
                        if kind == 1:
                            for f, (c0, k) in enumerate(ts):
                                last = nc.tensor.transpose(ps[0:HALF, b + PARTS * f:b + PARTS * f + k],
                                                           raw1[p][0:k, a, c0 // PARTS, HALF * kb:HALF * kb + HALF], ident[0:k, 0:k])
                        else:
                            c0, k = ts[0]
                            for h in range(2):
                                last = nc.tensor.transpose(ps[0:k, b + HALF * h:b + HALF * h + HALF], raw2[p][:, h, c0:c0 + k], ident[0:HALF, 0:HALF])
                        last.then_inc(s_t, 1)

                pe.wait_ge(norm.ident_done, 2)
                pe.wait_ge(s_g, 32)
                for kb in range(2):
                    last = nc.tensor.transpose(ps[0:HALF + kb, kb * EXPERTS:(kb + 1) * EXPERTS], graw[:, HALF * kb:HALF * kb + HALF + kb],
                                               ident[0:EXPERTS, 0:EXPERTS])
                last.then_inc(s_gt, 1)
                first_experts(body)
                pe.wait_ge(s_gts, 1)

                def logits(g):
                    pe.wait_ge(norm.turned, 2 * (g + 1))
                    for i in range(norm.PER * g, norm.PER * (g + 1)):
                        for kb in range(2):
                            last = nc.tensor.matmul(ps[0:TILE, 2 * EXPERTS + EXPERTS * i:2 * EXPERTS + EXPERTS * i + EXPERTS],
                                                    xT[0:HALF + kb, kb, TILE * i:TILE * i + TILE], GT[0:HALF + kb, kb, :], start=(kb == 0), stop=(kb == 1))
                    last.then_inc(s_lg, 1)

                norm.turn(pe, logits)

                def rank():
                    pe.wait_ge(s_oh, 1)
                    pe.wait_ge(s_up, 2)
                    pe.wait_ge(norm.turned, norm.COPIES)
                    flat = both[:].rearrange("p t e -> p (t e)")
                    nc.tensor.matmul(ps[0:TILE, BANK:BANK + NTILE * EXPERTS], upper[:], flat, start=True, stop=True)
                    nc.tensor.matmul(ps[0:TILE, BANK + 256:BANK + 256 + NTILE * EXPERTS], ones[:], flat, start=True, stop=True).then_inc(s_rank, 1)

                other_experts(pe, body, rank)

            @block.vector
            def _(dve):
                count = [0]

                def link(ins):
                    count[0] += 1
                    ins.then_inc(s_v, 1)
                    dve.wait_ge(s_v, count[0])

                dve.wait_ge(s_gt, 1)
                nc.vector.tensor_copy(GT[0:HALF, 0, :], ps[0:HALF, 0:EXPERTS])
                nc.vector.tensor_copy(GT[:, 1, :], ps[0:HALF + 1, EXPERTS:2 * EXPERTS]).then_inc(s_gts, 1)
                norm.normalise(dve)
                nc.vector.memset(chain0[:], 1.0)
                link(nc.vector.memset(start[:], 1.0))
                link(nc.vector.memset(chain0[:, :, 0:1], 0.0))
                dve.wait_ge(s_cst, 1)
                nc.vector.tensor_copy(order[:], order_i[:])
                nc.vector.tensor_copy(thr[:], thr_i[:])
                link(nc.vector.tensor_copy(tn[:], tn_i[:]))
                dve.wait_ge(s_lg, NTILE // norm.PER)
                link(nc.vector.tensor_copy(L[:].rearrange("p t e -> p (t e)"), ps[0:TILE, 2 * EXPERTS:2 * EXPERTS + NTILE * EXPERTS]))
                for k in range(slots):
                    link(nc.vector.reduce_max(best[k][:], L[:], axis=AX_X))
                    link(nc.vector.tensor_tensor(key[:], L[:], spread(best[k][:], 2, EXPERTS), ALU.is_equal))
                    link(nc.vector.tensor_tensor(key[:], key[:], spread(order[:], 1, NTILE), ALU.mult))
                    link(nc.vector.reduce_max(top[:], key[:], axis=AX_X))
                    link(nc.vector.tensor_tensor(OH[k][:], key[:], spread(top[:], 2, EXPERTS), ALU.is_equal))
                    if k + 1 < slots:
                        link(nc.vector.scalar_tensor_tensor(L[:].rearrange("p t e -> p (t e)"), OH[k][:].rearrange("p t e -> p (t e)"), -3.0e38,
                                                            L[:].rearrange("p t e -> p (t e)"), ALU.mult, ALU.add))
                if slots == 2:
                    nc.vector.tensor_tensor(both[:], OH[0][:], OH[1][:], ALU.add).then_inc(s_oh, 1)
                    link(nc.vector.tensor_tensor(score[1][:], best[1][:], best[0][:], ALU.subtract))
                else:
                    nc.vector.tensor_copy(both[:], OH[0][:]).then_inc(s_oh, 1)
                dve.wait_ge(s_rank, 1)
                link(nc.vector.tensor_copy(tot[:].rearrange("p e t -> p t e"), ps[0:TILE, BANK + 256:BANK + 256 + NTILE * EXPERTS].rearrange("p (t e) -> p t e", e=EXPERTS)))
                link(nc.vector.tensor_tensor_scan(incl[:].rearrange("p e t -> p (e t)"), chain0[:].rearrange("p e t -> p (e t)"),
                                                  tot[:].rearrange("p e t -> p (e t)"), 0.0, ALU.mult, ALU.add))
                link(nc.vector.tensor_tensor(over[:], spread(incl[:, :, NTILE - 1], 2, NTH), spread(thr[:], 1, EXPERTS), ALU.is_gt))
                link(nc.vector.reduce_sum(nt[:], over[:], axis=AX_X))
                link(nc.vector.tensor_tensor_scan(ntin[:], start[:], nt[:], 0.0, ALU.mult, ALU.add))
                link(nc.vector.tensor_tensor(start[:], ntin[:], nt[:], ALU.subtract))
                link(nc.vector.tensor_scalar(start[:], start[:], float(PARTS), None, ALU.mult))
                link(nc.vector.tensor_tensor(incl[:], incl[:], tot[:], ALU.subtract))
                link(nc.vector.tensor_tensor(place[:], spread(start[:], 1, NTILE), incl[:].rearrange("p e t -> p t e"), ALU.add))
                link(nc.vector.tensor_tensor(place[:], place[:], ps[0:TILE, BANK:BANK + NTILE * EXPERTS].rearrange("p (t e) -> p t e", e=EXPERTS), ALU.add))
                for k in range(slots):
                    link(nc.vector.tensor_tensor(key[:], place[:], OH[k][:], ALU.mult))
                    link(nc.vector.reduce_sum(pf[:], key[:], axis=AX_X))
                    nc.vector.tensor_copy(pos[k][:], pf[:]).then_inc(s_pos, 1)
                    dve.wait_ge(s_pos, k + 1)
                link(nc.vector.tensor_tensor(tge[:], spread(tn[:], 2, EXPERTS), spread(ntin[0:1, :], 1, ntiles), ALU.is_ge))
                link(nc.vector.reduce_sum(te[:], tge[:], axis=AX_X))
                link(nc.vector.tensor_scalar(te[:], te[:], float(EXPERTS - 1), None, ALU.min))
                nc.vector.tensor_copy(texp[:], te[:])
                if slots == 2:
                    dve.wait_ge(s_exp, 1)
                    link(nc.vector.tensor_scalar(score[0][:], score[1][:], 1.0, None, ALU.add))
                    link(nc.vector.reciprocal(score[0][:], score[0][:]))
                    link(nc.vector.tensor_tensor(score[1][:], score[1][:], score[0][:], ALU.mult))

            @block.scalar
            def _(act):
                def body(e, p):
                    for n, (kind, a, kb, ts) in enumerate(jobs):
                        act.wait_ge(s_t, njobs * e + n + 1)
                        b = (3 + n % nbanks) * BANK
                        if kind == 1:
                            c0 = a * hidden + ts[0][0]
                            k = sum(x[1] for x in ts)
                            to = W1[0:HALF, kb, bass.ds(e, 1), c0:c0 + k].rearrange("p a c -> p (a c)")
                            nc.scalar.copy(to, ps[0:HALF, b:b + k]).then_inc(s_e, 1)
                        else:
                            k = ts[0][1]
                            to = W2[0:k, a, bass.ds(e, 1), :].rearrange("p a c -> p (a c)")
                            nc.scalar.copy(to, ps[0:k, b:b + DIM]).then_inc(s_e, 1)

                first_experts(body)
                norm.copy(act)
                other_experts(act, body)
                if slots == 2:
                    act.wait_ge(s_rank, 1)
                    act.wait_ge(s_oh, 1)
                    act.wait_ge(s_pos, 1)
                    nc.scalar.activation(score[1][:], score[1][:], ACT.Exp).then_inc(s_exp, 1)

        with ExitStack() as ctx2:
            s2 = Stage(nc, ctx2, name + "_tiles")
            ps = s2.psum()
            X = [s2.sbuf(f"X{p}", [PARTS, DIM]) for p in range(2)]
            XT = s2.sbuf("XT", [HALF + 1, 2, PARTS])
            G = s2.sbuf("G", [PARTS, hidden])
            act_out = s2.sbuf("act_out", [PARTS, hidden]) if gated else G
            GT = s2.sbuf("GT", [PARTS, nft, PARTS])
            Y = [s2.sbuf(f"Y{p}", [PARTS, DIM]) for p in range(2)]
            gb = s2.sbuf("gb", [HALF, 2, 2])
            s_in = [s2.sem(f"in{p}") for p in range(2)]
            s_out = [s2.sem(f"out{p}") for p in range(2)]
            s_gb, s_xt, s_xts, s_l1, s_g1, s_g2, s_gt, s_gts, s_l2, s_y, s_gate = (
                s2.sem(n) for n in ("gb", "xt", "xts", "l1", "g1", "g2", "gt", "gts", "l2", "y", "gate"))
            s_g = s_g2 if gated else s_g1
            gper = 1 if gated else 2

            def live(i):
                return 0 <= i < ntiles if isinstance(i, int) else True

            def schedule(eng, body):
                for t in range(4):
                    body(t, t % 2)
                with eng.Fori(4, ntiles - 1, 2) as t:
                    body(t, 0)
                    body(t + 1, 1)
                body(ntiles, 0)
                body(ntiles + 1, 1)

            def paired(each, i, p):
                return each * (i - p + 2) // 2 if isinstance(i, int) else (i - p) * (each // 2) + each

            block = ctx2.enter_context(nc.Block())

            @block.sync
            def _(sp):
                if not gated:
                    with nc.allow_non_contiguous_dma(reason="columns of the norm's gain and bias"):
                        for n, m in enumerate(("lng", "lnb")):
                            for kb in range(2):
                                sp.dma_start(gb[:, n, kb:kb + 1], dram(w[m], HALF * kb, [(1, HALF), (1, 1)])).then_inc(s_gb, 16)

                def body(t, p):
                    if live(t):
                        wait(sp, s_xt, t - 1)
                        sp.sem_inc(s_gate, 1)
                        sp.dma_start(X[p][:], dram(xs, t * (PARTS * DIM), [(DIM, PARTS), (1, DIM)])).then_inc(s_in[p], 16)
                    if live(t - 2):
                        sp.wait_ge(s_y, t - 1)
                        sp.sem_inc(s_gate, 1)
                        sp.dma_start(dram(ys, (t - 2) * (PARTS * DIM), [(DIM, PARTS), (1, DIM)]), Y[p][:]).then_inc(s_out[p], 16)

                schedule(sp, body)
                for p in range(2):
                    sp.wait_ge(s_out[p], 16 * ntiles // 2)

            @block.tensor
            def _(pe):
                def body(t, p):
                    m = t - 1
                    if live(t):
                        pe.wait_ge(s_in[p], paired(16, t, p))
                        wait(pe, s_xts, t)
                        for kb in range(2):
                            last = nc.tensor.transpose(ps[0:HALF, PARTS * kb:PARTS * kb + PARTS], X[p][:, HALF * kb:HALF * kb + HALF], ident[:])
                        last.then_inc(s_xt, 1)
                    if live(m):
                        pe.wait_ge(s_g, gper * t)
                        wait(pe, s_gts, 2 * m)
                        for f, (c0, k) in enumerate(fts):
                            last = nc.tensor.transpose(ps[0:k, BANK + PARTS * f:BANK + PARTS * f + PARTS], G[:, c0:c0 + k], ident[:])
                        last.then_inc(s_gt, 1)
                    if live(t):
                        e = pe.value_load(texp[0:1, t:t + 1] if isinstance(t, int) else texp[0:1, bass.ds(t, 1)], min_val=0, max_val=EXPERTS - 1)
                        pe.wait_ge(s_xts, t + 1)
                        wait(pe, s_g1, 2 // (1 if not gated else 2) * t)
                        if gated:
                            wait(pe, s_g2, t)
                        for c in range(2):
                            for kb in range(2):
                                k = HALF if kb == 0 or gated else HALF + 1
                                last = nc.tensor.matmul(ps[:, (3 + c) * BANK:(3 + c) * BANK + cut], XT[0:k, kb, :],
                                                        W1[0:k, kb, bass.ds(e, 1), cut * c:cut * c + cut].rearrange("p a c -> p (a c)"),
                                                        start=(kb == 0), stop=(kb == 1))
                            last.then_inc(s_l1, 1)
                    if live(m):
                        e = pe.value_load(texp[0:1, m:m + 1] if isinstance(m, int) else texp[0:1, bass.ds(m, 1)], min_val=0, max_val=EXPERTS - 1)
                        pe.wait_ge(s_gts, 2 * t)
                        wait(pe, s_y, m)
                        out = ps[:, 5 * BANK:5 * BANK + DIM]
                        for f, (c0, k) in enumerate(fts):
                            last = nc.tensor.matmul(out, GT[0:k, f, :], W2[0:k, f, bass.ds(e, 1), :].rearrange("p a c -> p (a c)"),
                                                    start=(f == 0), stop=(f == nft - 1))
                        last.then_inc(s_l2, 1)

                schedule(pe, body)

            @block.scalar
            def _(act):
                if not gated:
                    act.wait_ge(s_gb, 64)

                def body(t, p):
                    m = t - 1
                    if live(m):
                        act.wait_ge(s_gt, t)
                        wait(act, s_l2, m)
                        if nft > 4:
                            nc.scalar.copy(GT[:, 4:, :].rearrange("p f c -> p (f c)"), ps[:, 2 * BANK:2 * BANK + PARTS * (nft - 4)]).then_inc(s_gts, 1)
                    if live(t):
                        for c in range(2 if not gated else 1):
                            act.wait_ge(s_l1, 2 * t + c + 1)
                            if c == 0:
                                wait(act, s_gt if not gated else s_g2, t)
                            nc.scalar.activation(act_out[:, cut * c:cut * c + cut], ps[:, (3 + c) * BANK:(3 + c) * BANK + cut],
                                                 ACT.Silu if gated else ACT.Gelu).then_inc(s_g1, 1)

                schedule(act, body)

            @block.vector
            def _(dve):
                if not gated:
                    nc.vector.memset(XT[HALF:HALF + 1, :, :], 1.0)
                    dve.wait_ge(s_gb, 64)

                def body(t, p):
                    m, n = t - 1, t - 2
                    if live(n) and not gated:
                        e = dve.value_load(texp[0:1, n:n + 1] if isinstance(n, int) else texp[0:1, bass.ds(n, 1)], min_val=0, max_val=EXPERTS - 1)
                    if live(t):
                        dve.wait_ge(s_xt, t + 1)
                        wait(dve, s_l1, 2 * t)
                        for kb in range(2):
                            got = ps[0:HALF, PARTS * kb:PARTS * kb + PARTS]
                            if gated:
                                last = nc.vector.tensor_copy(XT[0:HALF, kb, :], got)
                            else:
                                last = nc.vector.tensor_scalar(XT[0:HALF, kb, :], got, gb[:, 0, kb:kb + 1], gb[:, 1, kb:kb + 1], ALU.mult, ALU.add)
                        last.then_inc(s_xts, 1)
                    if live(m):
                        dve.wait_ge(s_gt, t)
                        wait(dve, s_l2, m)
                        if gated:
                            nc.vector.tensor_copy(GT[:, 0:3, :].rearrange("p f c -> p (f c)"), ps[:, BANK:BANK + 3 * PARTS]).then_inc(s_gts, 1)
                            k = fts[3][1]
                            nc.vector.tensor_copy(GT[0:k, 3, :], ps[0:k, BANK + 3 * PARTS:BANK + 4 * PARTS]).then_inc(s_gts, 1)
                        else:
                            nc.vector.tensor_copy(GT[:, 0:4, :].rearrange("p f c -> p (f c)"), ps[:, BANK:BANK + 4 * PARTS]).then_inc(s_gts, 1)
                    if live(n):
                        dve.wait_ge(s_l2, n + 1)
                        if not isinstance(n, int) or n >= 2:
                            dve.wait_ge(s_out[p], paired(16, n - 2, p))
                        y = ps[:, 5 * BANK:5 * BANK + DIM]
                        if gated:
                            nc.vector.tensor_copy(Y[p][:], y).then_inc(s_y, 1)
                        else:
                            nc.vector.tensor_tensor(Y[p][:], y, B2[:, bass.ds(e, 1), :].rearrange("p a c -> p (a c)"), ALU.add).then_inc(s_y, 1)
                    if live(t) and gated:
                        dve.wait_ge(s_l1, 2 * t + 2)
                        dve.wait_ge(s_g1, t + 1)
                        wait(dve, s_gt, t)
                        nc.vector.tensor_tensor(G[:], act_out[:], ps[:, 4 * BANK:4 * BANK + cut], ALU.mult).then_inc(s_g2, 1)

                schedule(dve, body)

        with ExitStack() as ctx2:
            s2 = Stage(nc, ctx2, name + "_sum")
            Yg = [s2.sbuf(f"Y{k}", [TILE, NTILE, DIM]) for k in range(slots)]
            s_ga = [[s2.sem(f"ga{k}{i}") for i in range(5)] for k in range(slots)]
            s_v, s_base, s_out = s2.sem("v"), s2.sem("base"), s2.sem("out")
            per = NTILE // 5
            block = ctx2.enter_context(nc.Block())

            @block.sync
            def _(sp):
                if h_out is not None:
                    for q in range(5):
                        sp.wait_ge(s_v, slots * per * (q + 1))
                        sp.dma_start(dram(h_out, q * per * TILE * DIM, [(DIM, TILE), (TILE * DIM, per), (1, DIM)]), rows[:, per * q:per * q + per, :]).then_inc(s_out, 16)
                    sp.wait_ge(s_out, 80)

            @block.gpsimd
            def _(pool):
                for i in range(NTILE):
                    for k in range(slots):
                        nc.gpsimd.indirect_dma_start(out=Yg[k][:, i, :], out_offset=None, in_=dram(ys, 0, [(DIM, ntiles * PARTS), (1, DIM)]),
                                                     in_offset=bass.IndirectOffsetOnAxis(ap=pos[k][:, i:i + 1], axis=0)).then_inc(s_ga[k][i // per], 16)

            @block.vector
            def _(dve):
                if base is not None:
                    for i in range(NTILE):
                        nc.vector.tensor_tensor(rows[:, i, :], rows[:, i, :], base[:, i, :], ALU.add).then_inc(s_base, 1)
                    dve.wait_ge(s_base, NTILE)
                n = 0
                for q in range(5):
                    for k in range(slots):
                        dve.wait_ge(s_ga[k][q], 16 * per)
                        wait(dve, s_v, n)
                        for i in range(per * q, per * q + per):
                            if slots == 1:
                                ins = nc.vector.tensor_tensor(rows[:, i, :], rows[:, i, :], Yg[k][:, i, :], ALU.add)
                            else:
                                ins = nc.vector.scalar_tensor_tensor(rows[:, i, :], Yg[k][:, i, :], score[k][:, i:i + 1], rows[:, i, :], ALU.mult, ALU.add)
                            ins.then_inc(s_v, 1)
                            n += 1
                    if stats is not None:
                        dve.wait_ge(s_v, n)
                        for i in range(per * q, per * q + per):
                            nc.vector.bn_stats(stats[:, i, :], rows[:, i, :])



def tower(nc, a, out):
    def scratch(name, shape):
        return nc.dram_tensor(name, shape, F32, kind="Internal").ap()

    def under(prefix, names):
        return {n: a[prefix + n] for n in names}

    xpad = scratch("xpad", [IMAGES, CHANNELS, PAD_ROWS, PAD_COLS])
    t1 = scratch("t1", [IMAGES, 33, 33, EMB])
    t2 = scratch("t2", [IMAGES, 17, 17, EMB])
    h0 = scratch("h0", [TOKENS, DIM])
    abc = scratch("abc", [48, TOKENS])
    xs = scratch("xs", [5120, DIM])
    ys = scratch("ys", [5120, DIM])

    performer_names = ("n1g", "n1b", "kqvw", "kqvb", "projw", "projb", "n2g", "n2b", "w1", "b1", "w2", "b2", "w")
    ssm_names = [m + s for m in "ABCd" for s in ("_w1", "_b1", "_w2", "_b2")] + ["D_param", "log_dt"]
    first = {"w": {c: (a["L0_attn_" + c.upper() + "W_w"], 0) for c in "qkvo"}, "b": {c: a["L0_attn_" + c.upper() + "W_b"] for c in "qkvo"}}
    second = {"w": {c: (a["L0_ffn_qkv_w"], DIM * i) for i, c in enumerate("qkv")}, "b": {"o": a["L0_ffn_proj_b"]},
              "lng": a["L0_ffn_ln1_g"], "lnb": a["L0_ffn_ln1_b"]}
    second["w"]["o"] = (a["L0_ffn_proj_w"], 0)
    moe = {"gate_w": a["L0_ffn_gate_w"], "gate_b": a["L0_ffn_gate_b"], "w1": [a["L0_ffn_w1"]], "b1": a["L0_ffn_b1"],
           "w2": a["L0_ffn_w2"], "b2": a["L0_ffn_b2"], "lng": a["L0_ffn_ln2_g"], "lnb": a["L0_ffn_ln2_b"]}
    glu = {"gate_w": a["L1_ffn_Wg"], "gate_b": a["L1_ffn_bg"], "w1": [a["L1_ffn_W1"], a["L1_ffn_W2"]], "w2": a["L1_ffn_W3"]}

    with nc.cleanup_on_exit():
        performer(nc, "a1", xpad, t1, under("L0_tok_a1_", performer_names), True, a["x"])
    with nc.cleanup_on_exit():
        performer(nc, "a2", t1, t2, under("L0_tok_a2_", performer_names), False)
    with nc.cleanup_on_exit():
        project(nc, t2, h0, a["L0_tok_proj_w"], a["L0_tok_proj_b"], a["cls_tok"])
    with nc.sbuf_tensor("stats_a", [TILE, NTILE, 6], F32) as stats_a, nc.sbuf_tensor("stats_b", [TILE, NTILE, 6], F32) as stats_b, \
            nc.sbuf_tensor("h_b", [TILE, NTILE, DIM], F32) as h_b:
        with nc.sbuf_tensor("h_a", [TILE, NTILE, DIM], F32) as h_a:
            with nc.cleanup_on_exit():
                attention(nc, "at", h0, None, h_a, None, stats_a, first, False)
            with nc.cleanup_on_exit():
                attention(nc, "fa", None, h_a, h_b, stats_a, stats_b, second, True)
            with nc.cleanup_on_exit():
                experts(nc, "moe", h_b, h_a, None, stats_b, stats_a, xs, ys, moe, False)
        with nc.cleanup_on_exit():
            state_space(nc, "ssm", h_b, stats_a, stats_b, abc, under("L1_attn_", ssm_names))
        with nc.cleanup_on_exit():
            experts(nc, "glu", h_b, None, out, stats_b, None, xs, ys, glu, True)



def kernel(**inputs):
    import numpy as np
    from concourse import bacc
    from concourse.bass_utils import run_bass_kernel_spmd

    nc = bacc.Bacc("TRN2", target_bir_lowering=False, num_devices=1)
    arrays = {"in_" + n: np.ascontiguousarray(v) for n, v in inputs.items()}
    a = {n: nc.dram_tensor("in_" + n, v.shape, F32, kind="ExternalInput").ap() for n, v in inputs.items()}
    out = nc.dram_tensor("out", (IMAGES, TOKENS // IMAGES, DIM), F32, kind="ExternalOutput").ap()
    tower(nc, a, dram(out, 0, [(DIM, TOKENS), (1, DIM)]))
    return run_bass_kernel_spmd(nc, [arrays], core_ids=[0]).results[0]["out"]
```
